# Optimizing a Trainium2 kernel written in Bass

```python
import numpy as np
import jax
import jax.numpy as jnp

def _softmax(x, axis=-1):
    return jax.nn.softmax(x, axis=axis)

def _gelu(x):
    return jax.nn.gelu(x, approximate=True)

def _silu(x):
    return jax.nn.silu(x)

def _sigmoid(x):
    return jax.nn.sigmoid(x)

def _layernorm(x, axis=-1, eps=1e-05):
    m = jnp.mean(x, axis=axis, keepdims=True)
    v = jnp.var(x, axis=axis, keepdims=True)
    return (x - m) / jnp.sqrt(v + eps)

def _scatter_add(tgt, idx, src, axis=0):
    return tgt.at[idx].add(src)

def _segment_sum(src, seg, n):
    return jax.ops.segment_sum(src, seg, n)
kernel_name = 'mk_adj_ffn_d1_adj_r2_9f2adb'

def setup_inputs(seed: int=0):
    np.random.seed(seed)
    _w = jnp.asarray

    def _rec_inputs():
        import jax
        import jax.numpy as jnp
        _gk = jax.random.key(seed)
        x = -0.0002928 + 1 * jax.random.normal(jax.random.fold_in(_gk, 1), (2048, 512), jnp.float32)
        _a = jax.random.bernoulli(jax.random.fold_in(_gk, 2), 0.00390625, (2048, 2048))
        _a = jnp.logical_or(_a, jnp.swapaxes(_a, -1, -2))
        _a = jnp.logical_or(_a, jnp.eye(2048, dtype=bool))
        _af = _a.astype(jnp.float32)
        adj = _af
        return (x, adj)
    x, adj = _rec_inputs()

    def _L0_gnn_setup():
        import jax, jax.numpy as jnp
        import numpy as np
        N = 2048
        D_IN = 512
        H = 16
        DH = D_IN // H
        ALPHA = 0.2
        MASK_VAL = -65500.0
        key = jax.random.key(seed)
        ks = jax.random.split(key, 7)
        x = jax.random.normal(ks[0], (N, D_IN), dtype=jnp.float32)
        adj = jax.random.randint(ks[1], (N, N), 0, 2).astype(jnp.float32)
        s = 1.0 / np.sqrt(D_IN)
        W_seq = jax.random.normal(ks[2], (D_IN, D_IN), dtype=jnp.float32) * s
        a1 = jax.random.normal(ks[3], (DH,), dtype=jnp.float32) / np.sqrt(DH)
        a2 = jax.random.normal(ks[4], (DH,), dtype=jnp.float32) / np.sqrt(DH)
        W_out = jax.random.normal(ks[5], (D_IN, D_IN), dtype=jnp.float32) * s
        b_out = jax.random.normal(ks[6], (D_IN,), dtype=jnp.float32) * 0.01
        return {'x': x, 'adj': adj, 'W_seq': W_seq, 'a1': a1, 'a2': a2, 'W_out': W_out, 'b_out': b_out}
    _L0_gnn_all = _L0_gnn_setup()
    _L0_gnn_in = {k: v for k, v in _L0_gnn_all.items() if k in ('W_seq', 'a1', 'a2', 'W_out', 'b_out')}
    del _L0_gnn_all

    def _L0_ffn_setup():
        import jax, jax.numpy as jnp
        import numpy as np
        LN_EPS = 1e-05

        def entmax15(z):
            z = z / 2.0
            z = z - jnp.max(z, axis=-1, keepdims=True)
            zs = -jnp.sort(-z, axis=-1)
            k = jnp.arange(1, z.shape[-1] + 1, dtype=z.dtype)
            mean = jnp.cumsum(zs, axis=-1) / k
            meansq = jnp.cumsum(zs * zs, axis=-1) / k
            ss = k * (meansq - jnp.square(mean))
            delta = (1.0 - ss) / k
            tau = mean - jnp.sqrt(jnp.clip(delta, 0.0))
            support = jnp.sum((tau <= zs).astype(jnp.int32), axis=-1, keepdims=True)
            tau_star = jnp.take_along_axis(tau, support - 1, axis=-1)
            return jnp.square(jnp.clip(z - tau_star, 0.0))

        def layernorm_noaffine(v):
            m = jnp.mean(v, axis=-1, keepdims=True)
            var = jnp.mean(jnp.square(v - m), axis=-1, keepdims=True)
            return (v - m) / jnp.sqrt(var + LN_EPS)

        def cp_mumoe(x, gate, Win, Wout):
            ones = jnp.ones(x.shape[:-1] + (1,), x.dtype)
            xb = jnp.concatenate([x, ones], axis=-1)
            z = jnp.einsum('btd,dr->btr', xb, Win) * gate
            return jnp.einsum('btr,or->bto', z, Wout)
        key = jax.random.key(seed)
        ks = jax.random.split(key, 8)
        B, T, D, O, D2, E, R = (8, 1024, 512, 2048, 512, 16, 256)
        s = lambda k, shape, scale: jax.random.normal(k, shape, jnp.float32) * scale
        return {'x': s(ks[0], (B, T, D), 1.0), 'proj': s(ks[1], (D, E), D ** (-0.5)), 'C1': s(ks[2], (E, R), E ** (-0.5)), 'Win1': s(ks[3], (D + 1, R), D ** (-0.5)), 'Wout1': s(ks[4], (O, R), R ** (-0.5)), 'C2': s(ks[5], (E, R), E ** (-0.5)), 'Win2': s(ks[6], (O + 1, R), O ** (-0.5)), 'Wout2': s(ks[7], (D2, R), R ** (-0.5))}
    _L0_ffn_all = _L0_ffn_setup()
    _L0_ffn_in = {k: v for k, v in _L0_ffn_all.items() if k in ('proj', 'C1', 'Win1', 'Wout1', 'C2', 'Win2', 'Wout2')}
    del _L0_ffn_all
    return {'x': x, 'adj': adj, 'L0_gnn_W_seq': _L0_gnn_in['W_seq'], 'L0_gnn_a1': _L0_gnn_in['a1'], 'L0_gnn_a2': _L0_gnn_in['a2'], 'L0_gnn_W_out': _L0_gnn_in['W_out'], 'L0_gnn_b_out': _L0_gnn_in['b_out'], 'L0_ffn_proj': _L0_ffn_in['proj'], 'L0_ffn_C1': _L0_ffn_in['C1'], 'L0_ffn_Win1': _L0_ffn_in['Win1'], 'L0_ffn_Wout1': _L0_ffn_in['Wout1'], 'L0_ffn_C2': _L0_ffn_in['C2'], 'L0_ffn_Win2': _L0_ffn_in['Win2'], 'L0_ffn_Wout2': _L0_ffn_in['Wout2']}

def reference(x, adj, L0_gnn_W_seq, L0_gnn_a1, L0_gnn_a2, L0_gnn_W_out, L0_gnn_b_out, L0_ffn_proj, L0_ffn_C1, L0_ffn_Win1, L0_ffn_Wout1, L0_ffn_C2, L0_ffn_Win2, L0_ffn_Wout2):
    import jax
    import jax.numpy as jnp

    def _L0_gnn_ref(x, adj, W_seq, a1, a2, W_out, b_out):
        import jax, jax.numpy as jnp
        import numpy as np
        N = 2048
        D_IN = 512
        H = 16
        DH = D_IN // H
        ALPHA = 0.2
        MASK_VAL = -65500.0
        seq = (x @ W_seq).reshape(N, H, DH)
        score1 = jnp.einsum('nhd,d->hn', seq, a1)
        score2 = jnp.einsum('nhd,d->hn', seq, a2)
        scores = score1[:, :, None] + score2[:, None, :]
        scores = jax.nn.leaky_relu(scores, negative_slope=ALPHA)
        scores = scores + (1.0 - adj)[None, :, :] * MASK_VAL
        attn = jax.nn.softmax(scores, axis=-1)
        hidden = jnp.einsum('hij,jhd->ihd', attn, seq).reshape(N, D_IN)
        hidden = hidden @ W_out + b_out
        return jax.nn.elu(hidden)

    def _L0_ffn_ref(x, proj, C1, Win1, Wout1, C2, Win2, Wout2):
        import jax, jax.numpy as jnp
        import numpy as np
        LN_EPS = 1e-05

        def entmax15(z):
            z = z / 2.0
            z = z - jnp.max(z, axis=-1, keepdims=True)
            zs = -jnp.sort(-z, axis=-1)
            k = jnp.arange(1, z.shape[-1] + 1, dtype=z.dtype)
            mean = jnp.cumsum(zs, axis=-1) / k
            meansq = jnp.cumsum(zs * zs, axis=-1) / k
            ss = k * (meansq - jnp.square(mean))
            delta = (1.0 - ss) / k
            tau = mean - jnp.sqrt(jnp.clip(delta, 0.0))
            support = jnp.sum((tau <= zs).astype(jnp.int32), axis=-1, keepdims=True)
            tau_star = jnp.take_along_axis(tau, support - 1, axis=-1)
            return jnp.square(jnp.clip(z - tau_star, 0.0))

        def layernorm_noaffine(v):
            m = jnp.mean(v, axis=-1, keepdims=True)
            var = jnp.mean(jnp.square(v - m), axis=-1, keepdims=True)
            return (v - m) / jnp.sqrt(var + LN_EPS)

        def cp_mumoe(x, gate, Win, Wout):
            ones = jnp.ones(x.shape[:-1] + (1,), x.dtype)
            xb = jnp.concatenate([x, ones], axis=-1)
            z = jnp.einsum('btd,dr->btr', xb, Win) * gate
            return jnp.einsum('btr,or->bto', z, Wout)
        a = entmax15(layernorm_noaffine(jnp.einsum('btd,de->bte', x, proj)))
        g1 = jnp.einsum('bte,er->btr', a, C1)
        h = cp_mumoe(x, g1, Win1, Wout1)
        h = jax.nn.gelu(h, approximate=False)
        g2 = jnp.einsum('bte,er->btr', a, C2)
        return cp_mumoe(h, g2, Win2, Wout2)
    x = x + _L0_gnn_ref(_layernorm(x, axis=-1), adj, L0_gnn_W_seq, L0_gnn_a1, L0_gnn_a2, L0_gnn_W_out, L0_gnn_b_out)
    x = x + _L0_ffn_ref(_layernorm(x, axis=-1)[None], L0_ffn_proj, L0_ffn_C1, L0_ffn_Win1, L0_ffn_Wout1, L0_ffn_C2, L0_ffn_Win2, L0_ffn_Wout2)[0]
    return x

_drawn_inputs = setup_inputs


def setup_inputs(seed=0):
    import zlib

    import numpy as np

    out = dict(_drawn_inputs(seed))
    spreads = {}
    factors = {'L0_gnn_b_out': 6.343,
     'L0_ffn_proj': 3.964,
     'L0_ffn_C1': 4.013,
     'L0_ffn_Win1': 3.987,
     'L0_ffn_Wout1': 3.998,
     'L0_ffn_C2': 3.819,
     'L0_ffn_Win2': 3.845,
     'L0_ffn_Wout2': 3.852}
    for name, (base, spread) in spreads.items():
        noise = np.random.default_rng([zlib.crc32(name.encode()), seed]).standard_normal(out[name].shape)
        drawn = base * np.exp(spread * noise) if base else spread * noise
        out[name] = jnp.asarray(drawn.astype(out[name].dtype))
    for name, factor in factors.items():
        out[name] = (out[name] * factor).astype(out[name].dtype)
    return out
```

```python
from contextlib import ExitStack

import concourse.bass as bass
from concourse import mybir

F32 = mybir.dt.float32
BF16 = mybir.dt.bfloat16
F8 = mybir.dt.float8e4
I8 = mybir.dt.int8
I32 = mybir.dt.int32
ALU = mybir.AluOpType
ACT = mybir.ActivationFunctionType
AX = mybir.AxisListType
P = 128


def gat_ffn(nc, x, adj_t, w_seq, a1, a2, w_out, b_out, proj, c1, win1, wout1_t, c2, win2, wout2_t, out):
    N, D = x.shape
    DH = a1.shape[0]
    H = D // DH
    T = N // P
    KD = D // P
    E, R = c1.shape
    KR = R // P
    O = win2.shape[0] - 1
    KO = O // P
    C = 4
    CT = N // C
    EPS = 1e-5
    EDGE = 8.0

    DV = DH + 1
    PART = 3
    SIDE = PART * DV
    GROUP = 4
    NG = T // GROUP
    RING = 2 * GROUP
    SIGNS = 4
    BANKS = 8
    Q_PER_BANK = T // BANKS

    SIGN_ON_DVE = (5, 13)
    POS_ON_POOL = (1, 3, 5, 7, 9, 11, 13, 15)
    act_tiles = [j for j in range(T) if j not in SIGN_ON_DVE]
    pos_dve_tiles = [j for j in range(T) if j not in POS_ON_POOL]
    N_ACT, N_DVE = len(act_tiles), len(SIGN_ON_DVE)
    N_POOL, N_PDVE = len(POS_ON_POOL), len(pos_dve_tiles)

    def up_to(tiles, j):
        return sum(k <= j for k in tiles)

    s1_dram = nc.dram_tensor("s1_rows", [H, N], F32, kind="Internal").ap()

    with ExitStack() as ctx:
        def sb(name, shape, dt=F32, stack=ctx):
            return stack.enter_context(nc.sbuf_tensor(name, shape, dt))

        def sem(name):
            return ctx.enter_context(nc.semaphore(name))

        ident = sb("ident", [P, P])
        w_out_sb = sb("w_out_sb", [P, KD, D])
        b_out_sb = sb("b_out_sb", [P, D])
        rows = sb("rows", [P, T, D])
        x_rows = rows
        hidden = rows
        xn2_t = rows[:, :, :].rearrange("p t d -> p (t d)").rearrange("p (k n) -> p k n", k=KD)
        psum = [ctx.enter_context(nc.psum_tensor(f"bank{b}", [P, 512], F32)) for b in range(BANKS)]

        att = ExitStack()
        seq = sb("seq", [P, T, D], F32, att)
        edges = sb("edges", [P, T, N], I8, att)
        weight = sb("weight", [P, T, H, 2], F32, att)
        row_scale = sb("row_scale", [P, T, H, 2], F32, att)
        s12 = sb("s12", [P, T, 2 * H], F32, att)
        neg_s2 = sb("neg_s2", [P, T, H], F32, att)
        guard = sb("guard", [P, H], F32, att)
        setup = ExitStack()
        w_seq_sb = sb("w_seq_sb", [P, KD, D], F32, setup)
        a12 = sb("a12", [P, 2, DH], F32, setup)
        wa = sb("wa", [P, KD, 2 * H], F32, setup)
        wa_prod = sb("wa_prod", [P, 2, KD, D], F32, setup)
        adj_stage = sb("adj_stage", [P, 2, N], F32, setup)
        xn = [sb(f"xn{i}", [P, D], F32, setup) for i in range(2)]
        xn_t = [sb(f"xn_t{i}", [P, KD, P], F32, setup) for i in range(2)]
        s1_t = sb("s1_t", [H, N], F32, setup)
        stats = sb("stats", [P, T, 6], F32, setup)
        mean_var = sb("mean_var", [P, T, 2], F32, setup)
        std = sb("std", [P, T], F32, setup)
        rstd = sb("rstd", [P, T], F32, setup)
        smax = sb("smax", [P, H], F32, setup)
        shifted = sb("shifted", [P, 3, T, H], F32, setup)
        setup.close()
        signs = sb("signs", [P, SIGNS, N], I8, att)
        masks = [sb(f"masks{i}", [P, 2, N], I8, att) for i in range(RING)]
        s1_bc = [sb(f"s1_bc{i}", [P, N], F32, att) for i in range(2)]
        vals = [sb(f"vals{i}", [P, T, 2, PART, DV], BF16, att) for i in range(2)]
        weighted = sb("weighted", [P, T, 2, DV], F32, att)
        residue = sb("residue", [P, T, 2, DV], F32, att)
        sums = sb("sums", [P, T, 2, DV], F32, att)
        scaled = sb("scaled", [P, T, 2, DH], F32, att)
        den2 = sb("den2", [P, T, 2], F32, att)
        den = sb("den", [P, T], F32, att)
        rden = sb("rden", [P, T], F32, att)
        scale_n = sb("scale_n", [P, T, 2], F32, att)
        att.close()

        ffn = ExitStack()
        x2 = sb("x2", [P, T, D], F32, ffn)
        win1_sb = sb("win1_sb", [P, KD, R], F32, ffn)
        wout1_sb = sb("wout1_sb", [P, KR, O], F32, ffn)
        win2_sb = sb("win2_sb", [P, KO, R], F32, ffn)
        wout2_sb = sb("wout2_sb", [P, KR, D], F32, ffn)
        bias1 = sb("bias1", [P, KR], F32, ffn)
        bias2 = sb("bias2", [P, KR], F32, ffn)
        c1_sb = sb("c1_sb", [E, R], F32, ffn)
        c2_sb = sb("c2_sb", [E, R], F32, ffn)
        proj_sb = sb("proj_sb", [P, KD, E], F32, ffn)
        a_t = sb("a_t", [E, N], F32, ffn)
        z1_pre = sb("z1_pre", [P, KR, N], F32, ffn)
        mid = ExitStack()
        h_copy = [sb(f"h_copy{i}", [P, D], F32, mid) for i in range(2)]
        h_t = [sb(f"h_t{i}", [P, KD, P], F32, mid) for i in range(2)]
        y = sb("y", [P, 2, D], F32, mid)
        y_low = sb("y_low", [P, 2, D], F32, mid)
        y_exp = sb("y_exp", [P, 2, D], F32, mid)
        x_plus = sb("x_plus", [P, 2, D], F32, mid)
        xn2 = [sb(f"xn2_{i}", [P, D], F32, mid) for i in range(2)]
        stats2 = sb("stats2", [P, T, 6], F32, mid)
        mean_var2 = sb("mean_var2", [P, T, 2], F32, mid)
        std2 = sb("std2", [P, T], F32, mid)
        rstd2 = sb("rstd2", [P, T], F32, mid)
        ent = {n: sb(f"ent_{n}", [P, T, E], F32, mid) for n in
               ("u", "c", "sq", "v", "z", "rest", "sorted", "sorted2", "cum", "cum2", "mean", "msq",
                "delta", "root", "tau", "in_support", "pick", "a")}
        k_int = sb("k_int", [P, E], I32, mid)
        k_row = sb("k_row", [P, E], F32, mid)
        inv_k = sb("inv_k", [P, E], F32, mid)
        keep = sb("keep", [P, T, E], F32, mid)
        col = {n: sb(f"col_{n}", [P, T], F32, mid) for n in
               ("sum", "mean", "var", "std", "rstd", "max", "support", "tau")}
        a_col = [sb(f"a_col{i}", [P, E], F32, mid) for i in range(2)]
        mid.close()
        last = ExitStack()
        z1 = [sb(f"z1_{i}", [P, KR, CT], F32, last) for i in range(2)]
        gate2 = [sb(f"gate2_{i}", [P, KR, CT], F32, last) for i in range(2)]
        z2 = [sb(f"z2_{i}", [P, KR, CT], F32, last) for i in range(2)]
        HR = 4
        h_ring = [sb(f"h_ring{i}", [P, CT], F32, last) for i in range(HR)]
        out_rows = sb("out_rows", [P, 2, D], F32, last)
        last.close()
        ffn.close()

        ONE = 1
        x_in = [sem(f"x_in{q}") for q in range(4)]
        w_seq_in = sem("w_seq_in")
        a_in = sem("a_in")
        adj_in = [sem(f"adj_in{i}") for i in range(2)]
        w_out_in = sem("w_out_in")
        s1_saved = sem("s1_saved")
        s1_in = [sem(f"s1_in{i}") for i in range(2)]
        x2_in = sem("x2_in")
        ffn_in = sem("ffn_in")
        out_saved = [sem(f"out_saved{i}") for i in range(2)]
        ident_ready = sem("ident_ready")
        dve_step = sem("dve_step")
        std_ready = sem("std_ready")
        wa_ready = sem("wa_ready")
        xn_ready = sem("xn_ready")
        xn_turned = sem("xn_turned")
        xn_t_ready = sem("xn_t_ready")
        proj_done = sem("proj_done")
        seq_ready = sem("seq_ready")
        s12_ready = sem("s12_ready")
        edges_ready = sem("edges_ready")
        smax_ready = sem("smax_ready")
        guard_ready = sem("guard_ready")
        shifted_ready = sem("shifted_ready")
        weights_ready = sem("weights_ready")
        signs_act = sem("signs_act")
        signs_dve = sem("signs_dve")
        neg_cut = sem("neg_cut")
        pos_dve = sem("pos_dve")
        pos_pool = sem("pos_pool")
        bank_passed = sem("bank_passed")
        vals_ready = sem("vals_ready")
        pe_passed_waits = sem("pe_passed_waits")
        sp_passed_waits = sem("sp_passed_waits")
        bank_free = sem("bank_free")
        scale_ready = sem("scale_ready")
        scaled_ready = sem("scaled_ready")
        head_done = sem("head_done")
        h_copied = sem("h_copied")
        h_turned = sem("h_turned")
        h_t_ready = sem("h_t_ready")
        y_done = sem("y_done")
        y_low_ready = sem("y_low_ready")
        y_exp_ready = sem("y_exp_ready")
        y_bank_free = sem("y_bank_free")
        x2_ready = sem("x2_ready")
        x_plus_ready = sem("x_plus_ready")
        stats2_ready = sem("stats2_ready")
        std2_ready = sem("std2_ready")
        xn2_ready = sem("xn2_ready")
        xn2_turned = sem("xn2_turned")
        xn2_t_ready = sem("xn2_t_ready")
        u_done = sem("u_done")
        u_ready = sem("u_ready")
        z1_pre_done = sem("z1_pre_done")
        z1_pre_ready = sem("z1_pre_ready")
        k_ready = sem("k_ready")
        var_ready = sem("var_ready")
        var_std_ready = sem("var_std_ready")
        delta_ready = sem("delta_ready")
        root_ready = sem("root_ready")
        a_col_ready = sem("a_col_ready")
        a_turned = sem("a_turned")
        a_t_ready = sem("a_t_ready")
        gate1_done = sem("gate1_done")
        gate2_done = sem("gate2_done")
        gate2_ready = sem("gate2_ready")
        z1_ready = sem("z1_ready")
        h_done = sem("h_done")
        h_ready = sem("h_ready")
        h_used = sem("h_used")
        z2_ready = sem("z2_ready")
        o_done = sem("o_done")
        o_ready = sem("o_ready")

        x_view = x.rearrange("(t p) d -> p t d", p=P)
        adj_view = adj_t.rearrange("(t p) n -> t p n", p=P)
        out_view = out.rearrange("(t p) d -> t p d", p=P)
        TQ = T // 4

        block = ctx.enter_context(nc.Block())

        @block.sync
        def _(sp):
            for i in range(2):
                sp.sem_inc(out_saved[i], 16)
            for q in range(4):
                sp.dma_start(x_rows[:, q * TQ:(q + 1) * TQ, :], x_view[:, q * TQ:(q + 1) * TQ, :]).then_inc(x_in[q], 16)
            sp.dma_start(w_seq_sb[:], w_seq.rearrange("(k p) n -> p k n", p=P)).then_inc(w_seq_in, 16)
            sp.dma_start(a12[:, 0, :], a1.partition_broadcast(P)).then_inc(a_in, 16)
            sp.dma_start(a12[:, 1, :], a2.partition_broadcast(P)).then_inc(a_in, 16)
            for i in range(2):
                sp.dma_start(adj_stage[:, i, :], adj_view[i]).then_inc(adj_in[i], 16)
            with sp.Fori(1, T // 2) as tp:
                for i in range(2):
                    sp.wait_ge(edges_ready, 2 * tp + i - 1)
                    sp.sem_inc(sp_passed_waits)
                    sp.dma_start(adj_stage[:, i, :], adj_view[bass.ds(2 * tp + i, 1)].rearrange("a p n -> (a p) n"))\
                        .then_inc(adj_in[i], 16)
            sp.dma_start(w_out_sb[:], w_out.rearrange("(k p) n -> p k n", p=P)).then_inc(w_out_in, 16)
            sp.dma_start(b_out_sb[:], b_out.partition_broadcast(P)).then_inc(w_out_in, 16)
            sp.wait_ge(s12_ready, ONE + 2 * T)
            sp.dma_start(s1_dram, s1_t[:]).then_inc(s1_saved, 16)
            sp.wait_ge(s1_saved, 16)
            sp.wait_ge(edges_ready, T)
            sp.wait_ge(weights_ready, 4)

            def load_s1(h, i):
                sp.dma_start(s1_bc[i][:], s1_dram[bass.ds(h, 1), :].rearrange("a n -> (a n)").partition_broadcast(P))\
                    .then_inc(s1_in[i], 16)
            load_s1(0, 0)
            load_s1(1, 1)
            with sp.Fori(1, H // 2) as hp:
                for i in range(2):
                    sp.wait_ge(neg_cut, SIGNS + T * (2 * hp + i - 1))
                    sp.sem_inc(sp_passed_waits)
                    load_s1(2 * hp + i, i)

            sp.wait_ge(head_done, ONE + H)
            for q in range(4):
                sp.dma_start(x2[:, q * TQ:(q + 1) * TQ, :], x_view[:, q * TQ:(q + 1) * TQ, :]).then_inc(x2_in, 16)
            sp.dma_start(proj_sb[:], proj.rearrange("(k p) n -> p k n", p=P)).then_inc(ffn_in, 16)
            sp.dma_start(win1_sb[:], win1[0:D, :].rearrange("(k p) n -> p k n", p=P)).then_inc(ffn_in, 16)
            sp.dma_start(wout1_sb[:], wout1_t.rearrange("(k p) n -> p k n", p=P)).then_inc(ffn_in, 16)
            sp.dma_start(win2_sb[:], win2[0:O, :].rearrange("(k p) n -> p k n", p=P)).then_inc(ffn_in, 16)
            sp.dma_start(wout2_sb[:], wout2_t.rearrange("(k p) n -> p k n", p=P)).then_inc(ffn_in, 16)
            sp.dma_start(c1_sb[:], c1).then_inc(ffn_in, 16)
            sp.dma_start(c2_sb[:], c2).then_inc(ffn_in, 16)
            for k in range(KR):
                sp.dma_start(bias1[:, k:k + 1], win1[D:D + 1, k * P:(k + 1) * P].rearrange("a p -> p a")).then_inc(ffn_in, 16)
                sp.dma_start(bias2[:, k:k + 1], win2[O:O + 1, k * P:(k + 1) * P].rearrange("a p -> p a")).then_inc(ffn_in, 16)

            with sp.Fori(0, T // 2) as tp:
                for i in range(2):
                    sp.wait_ge(o_ready, ONE + 2 * tp + i + 1)
                    sp.sem_inc(sp_passed_waits)
                    sp.dma_start(out_view[bass.ds(2 * tp + i, 1)].rearrange("a p n -> (a p) n"), out_rows[:, i, :])\
                        .then_inc(out_saved[i], 16)
            for i in range(2):
                sp.wait_ge(out_saved[i], 16 + 16 * T // 2)

        FFN_LOADS = 16 * (7 + 2 * KR)

        @block.gpsimd
        def _(pool):
            pool.sem_inc(head_done, ONE)
            nc.gpsimd.memset(ident[:], 1.0).then_inc(ident_ready, 1)
            pool.wait_ge(ident_ready, 1)
            nc.gpsimd.affine_select(out=ident[:], in_=ident[:], compare_op=ALU.is_equal, fill=0.0, base=0,
                                    pattern=[[-1, P]], channel_multiplier=1).then_inc(ident_ready, 1)
            pool.wait_ge(smax_ready, 1)
            nc.gpsimd.partition_all_reduce(guard[:], smax[:], P, bass.bass_isa.ReduceOp.max).then_inc(guard_ready, 1)

            def cut_pos(h, j):
                if j not in POS_ON_POOL:
                    return
                if j % GROUP == min(k for k in POS_ON_POOL if k // GROUP == j // GROUP) % GROUP:
                    pool.wait_ge(bank_passed, BANKS * (NG * h + j // GROUP + 1))
                pool.wait_ge(neg_cut, SIGNS + T * h + j + 1)
                m = masks[j % RING]
                nc.gpsimd.tensor_tensor(m[:, 1, :].bitcast(I32), edges[:, j, :].bitcast(I32), m[:, 0, :].bitcast(I32),
                                        ALU.subtract).then_inc(pos_pool, 1)

            def combine(h):
                pool.wait_ge(scale_ready, h + 1)
                nc.gpsimd.tensor_tensor(scaled[:], sums[:, :, :, 0:DH], scale_n[:].unsqueeze(3).to_broadcast([P, T, 2, DH]),
                                        ALU.mult).then_inc(scaled_ready, 1)
                pool.wait_ge(scaled_ready, h + 1)
                nc.gpsimd.tensor_tensor(hidden[:, :, bass.ds(DH * h, DH)], scaled[:, :, 0, :], scaled[:, :, 1, :],
                                        ALU.add).then_inc(head_done, 1)

            def head(h, is_last):
                for j in range(GROUP, T):
                    cut_pos(h, j)
                if not is_last:
                    for j in range(GROUP):
                        cut_pos(h + 1, j)
                combine(h)

            pool.wait_ge(edges_ready, T)
            for j in range(GROUP):
                cut_pos(0, j)
            with pool.Fori(0, H - 1) as h:
                head(h, False)
            head(H - 1, True)

            nc.gpsimd.iota(k_int[:], pattern=[[1, E]], base=1, channel_multiplier=0).then_inc(k_ready, 1)

        @block.scalar
        def _(act):
            act.sem_inc(seq_ready, ONE)
            act.sem_inc(z1_pre_ready, ONE)
            act.sem_inc(gate2_ready, ONE)
            act.sem_inc(h_ready, ONE)
            act.wait_ge(dve_step, T + 1 + T)
            nc.scalar.activation(std[:], mean_var[:, :, 1], ACT.Sqrt).then_inc(std_ready, 1)

            def copy_xn_t(t, i):
                act.wait_ge(xn_turned, t + 1)
                act.wait_ge(proj_done, t + 1)
                nc.scalar.activation(xn_t[i][:].rearrange("p k n -> p (k n)"), psum[i][:, :], ACT.Copy).then_inc(xn_t_ready, 1)

            def adj_tile(tp, i):
                act.wait_ge(adj_in[i], 16 * tp + 16)
                nc.scalar.activation(edges[:, bass.ds(2 * tp + i, 1), :].rearrange("p a n -> p (a n)"), adj_stage[:, i, :],
                                     ACT.Copy, scale=EDGE).then_inc(edges_ready, 1)

            def evict_seq(t, i):
                act.wait_ge(proj_done, 2 + t + 1)
                nc.scalar.activation(seq[:, bass.ds(t, 1), :].rearrange("p a d -> p (a d)"), psum[2 + i][:, :], ACT.Copy)\
                    .then_inc(seq_ready, 1)

            copy_xn_t(0, 0)
            with act.Fori(0, T // 2 - 1) as tp:
                for i in range(2):
                    copy_xn_t(2 * tp + i + 1, 1 - i)
                    evict_seq(2 * tp + i, i)
                    adj_tile(tp, i)
            copy_xn_t(T - 1, 1)
            evict_seq(T - 2, 0)
            adj_tile(T // 2 - 1, 0)
            evict_seq(T - 1, 1)
            adj_tile(T // 2 - 1, 1)

            act.wait_ge(shifted_ready, 3)
            nc.scalar.activation(weight[:, :, :, 0], shifted[:, 0], ACT.Exp, scale=0.2).then_inc(weights_ready, 1)
            nc.scalar.activation(weight[:, :, :, 1], shifted[:, 0], ACT.Exp).then_inc(weights_ready, 1)
            nc.scalar.activation(row_scale[:, :, :, 0], shifted[:, 1], ACT.Exp, scale=-0.8).then_inc(weights_ready, 1)
            nc.scalar.activation(row_scale[:, :, :, 1], shifted[:, 2], ACT.Exp, scale=0.8).then_inc(weights_ready, 1)

            def sign(h, i, j):
                if j in SIGN_ON_DVE:
                    return
                act.wait_ge(neg_cut, T * h + j + 1)
                nc.scalar.activation(signs[:, j % SIGNS, :], s1_bc[i][:], ACT.Sign,
                                     bias=s12[:, j, bass.ds(H + h, 1)]).then_inc(signs_act, 1)

            def wait_s1(hp, i):
                act.wait_ge(s1_in[i], 16 * hp + 16)

            act.wait_ge(s12_ready, ONE + 2 * T)
            wait_s1(0, 0)
            for j in range(GROUP):
                sign(0, 0, j)
            with act.Fori(0, H // 2 - 1) as hp:
                for i in range(2):
                    for j in range(GROUP, T):
                        sign(2 * hp + i, i, j)
                    wait_s1(hp + i, 1 - i)
                    for j in range(GROUP):
                        sign(2 * hp + i + 1, 1 - i, j)
            for j in range(GROUP, T):
                sign(H - 2, 0, j)
            wait_s1(H // 2 - 1, 1)
            for j in range(T):
                sign(H - 1, 1, j)

            def copy_hidden(t, i):
                act.wait_ge(h_turned, t + 1)
                nc.scalar.activation(h_copy[i][:], hidden[:, bass.ds(t, 1), :].rearrange("p a d -> p (a d)"), ACT.Copy)\
                    .then_inc(h_copied, 1)

            def copy_h_t(t, i):
                act.wait_ge(h_turned, 2 + t + 1)
                act.wait_ge(y_done, t + 1)
                nc.scalar.activation(h_t[i][:].rearrange("p k n -> p (k n)"), psum[i][:, :], ACT.Copy).then_inc(h_t_ready, 1)

            def exp_y(t, i):
                act.wait_ge(y_low_ready, t + 1)
                act.wait_ge(x2_ready, t + 1)
                nc.scalar.activation(y_exp[:, i, :], y_low[:, i, :], ACT.Exp).then_inc(y_exp_ready, 1)

            act.wait_ge(head_done, ONE + H)
            copy_hidden(0, 0)
            copy_hidden(1, 1)
            copy_h_t(0, 0)
            with act.Fori(0, T // 2 - 1) as tp:
                for i in range(2):
                    copy_hidden(2 * tp + i + 2, i)
                    copy_h_t(2 * tp + i + 1, 1 - i)
                    exp_y(2 * tp + i, i)
            copy_h_t(T - 1, 1)
            exp_y(T - 2, 0)
            exp_y(T - 1, 1)

            act.wait_ge(std2_ready, 1)
            nc.scalar.activation(std2[:], mean_var2[:, :, 1], ACT.Sqrt).then_inc(std2_ready, 1)

            def copy_xn2_t(t, i):
                act.wait_ge(xn2_turned, 2 + t + 1)
                nc.scalar.activation(xn2_t[:, :, bass.ds(P * t, P)], psum[i][:, :].rearrange("p (k n) -> p k n", k=KD),
                                     ACT.Copy).then_inc(xn2_t_ready, 1)
            with act.Fori(0, T // 2) as tp:
                for i in range(2):
                    copy_xn2_t(2 * tp + i, i)
            act.wait_ge(var_ready, 1)
            nc.scalar.activation(col["std"][:], col["var"][:], ACT.Sqrt).then_inc(var_std_ready, 1)
            with act.Fori(0, C) as c:
                for k in range(KR):
                    act.wait_ge(z1_pre_done, KR * c + k + 1)
                    nc.scalar.activation(z1_pre[:, k, bass.ds(CT * c, CT)], psum[4 + k][:, :], ACT.Copy)\
                        .then_inc(z1_pre_ready, 1)
            act.wait_ge(delta_ready, 1)
            nc.scalar.activation(ent["root"][:], ent["delta"][:], ACT.Sqrt).then_inc(root_ready, 1)
            with act.Fori(0, T // 2) as tp:
                for i in range(2):
                    act.wait_ge(a_turned, 2 + 2 * tp + i + 1)
                    nc.scalar.activation(a_t[:, bass.ds(P * (2 * tp + i), P)], psum[i][0:E, 0:P], ACT.Copy)\
                        .then_inc(a_t_ready, 1)

            with act.Fori(0, C // 2) as cp:
                for i in range(2):
                    c = 2 * cp + i
                    for k in range(KR):
                        act.wait_ge(gate2_done, KR * c + k + 1)
                        nc.scalar.activation(gate2[i][:, k, :], psum[0][:, :], ACT.Copy).then_inc(gate2_ready, 1)
                    for o in range(KO):
                        act.wait_ge(h_done, KO * c + o + 1)
                        act.wait_ge(h_used, KO * c + o + 1)
                        nc.scalar.activation(h_ring[o % HR][:], psum[1 + o % 3][:, :], ACT.Gelu).then_inc(h_ready, 1)

        @block.vector
        def _(dve):
            dve.sem_inc(s12_ready, ONE)
            dve.sem_inc(z2_ready, ONE)
            dve.sem_inc(o_ready, ONE)
            steps = [0]

            def step(instruction):
                steps[0] += 1
                instruction.then_inc(dve_step, 1)
                dve.wait_ge(dve_step, steps[0])

            for q in range(4):
                dve.wait_ge(x_in[q], 16)
                with dve.Fori(q * TQ, (q + 1) * TQ) as t:
                    nc.vector.bn_stats(stats[:, bass.ds(t, 1), :].rearrange("p a s -> p (a s)"),
                                       x_rows[:, bass.ds(t, 1), :].rearrange("p a s -> p (a s)")).then_inc(dve_step, 1)
            dve.wait_ge(dve_step, T)
            for t in range(T):
                nc.vector.bn_aggr(mean_var[:, t, :], stats[:, t, :]).then_inc(dve_step, 1)
            dve.wait_ge(dve_step, 2 * T)
            steps[0] = 2 * T
            step(nc.vector.tensor_scalar(mean_var[:, :, 1], mean_var[:, :, 1], EPS, None, ALU.add))
            dve.wait_ge(std_ready, 1)
            step(nc.vector.reciprocal(rstd[:], std[:]))

            dve.wait_ge(w_seq_in, 16)
            dve.wait_ge(a_in, 32)
            for s in range(2):
                step(nc.vector.tensor_tensor(
                    wa_prod[:, s].rearrange("p k (h d) -> p (k h) d", d=DH),
                    w_seq_sb[:].rearrange("p k (h d) -> p (k h) d", d=DH),
                    a12[:, s:s + 1, :].to_broadcast([P, KD * H, DH]), ALU.mult))
            for s in range(2):
                nc.vector.tensor_reduce(wa[:, :, s * H:(s + 1) * H], wa_prod[:, s].rearrange("p k (h d) -> p k h d", d=DH),
                                        AX.X, ALU.add).then_inc(wa_ready, 1)

            def norm(t, i):
                nc.vector.tensor_scalar(xn[i][:], x_rows[:, bass.ds(t, 1), :].rearrange("p a s -> p (a s)"),
                                        mean_var[:, bass.ds(t, 1), 0:1].rearrange("p a s -> p (a s)"),
                                        rstd[:, bass.ds(t, 1)], ALU.subtract, ALU.mult).then_inc(xn_ready, 1)

            def evict_scores(t, i):
                dve.wait_ge(proj_done, 2 + t + 1)
                nc.vector.tensor_copy(s12[:, bass.ds(t, 1), :].rearrange("p a s -> p (a s)"), psum[4 + i][:, 0:2 * H])\
                    .then_inc(s12_ready, 1)
                nc.vector.tensor_copy(s1_t[:, bass.ds(P * t, P)], psum[6 + i][0:H, 0:P]).then_inc(s12_ready, 1)

            norm(0, 0)
            norm(1, 1)
            with dve.Fori(0, T // 2 - 1) as tp:
                for i in range(2):
                    dve.wait_ge(xn_turned, 2 * tp + i + 1)
                    norm(2 * tp + i + 2, i)
                    evict_scores(2 * tp + i, i)
            evict_scores(T - 2, 0)
            evict_scores(T - 1, 1)

            dve.wait_ge(s12_ready, ONE + 2 * T)
            s1_all, s2_all = s12[:, :, 0:H], s12[:, :, H:2 * H]
            nc.vector.tensor_reduce(smax[:], s2_all.rearrange("p t h -> p h t"), AX.X, ALU.max).then_inc(smax_ready, 1)
            nc.vector.tensor_scalar(neg_s2[:], s2_all, -1.0, None, ALU.mult).then_inc(shifted_ready, 1)
            dve.wait_ge(guard_ready, 1)
            guard_bc = guard[:].unsqueeze(1).to_broadcast([P, T, H])
            nc.vector.tensor_tensor(shifted[:, 0], s2_all, guard_bc, ALU.subtract).then_inc(shifted_ready, 1)
            step(nc.vector.tensor_tensor(shifted[:, 1], s1_all, guard_bc, ALU.add))
            step(nc.vector.tensor_scalar(shifted[:, 2], shifted[:, 1], 0.0, None, ALU.min))
            nc.vector.tensor_scalar(shifted[:, 1], shifted[:, 1], 0.0, None, ALU.max).then_inc(shifted_ready, 1)

            SETUP_STEPS = steps[0]
            SPLIT, SCALE = 5, 3

            def split_values(h, i, base):
                v = vals[i][:].rearrange("p t s a d -> p (t s) a d")
                w = weighted[:].rearrange("p t s d -> p (t s) d")
                r = residue[:].rearrange("p t s d -> p (t s) d")
                dve.wait_ge(vals_ready, h)
                wt = weight[:, :, bass.ds(h, 1), :].rearrange("p t a s -> p t (a s)")
                nc.vector.tensor_tensor(
                    weighted[:, :, :, 0:DH], seq[:, :, bass.ds(DH * h, DH)].unsqueeze(2).to_broadcast([P, T, 2, DH]),
                    wt.unsqueeze(3).to_broadcast([P, T, 2, DH]), ALU.mult).then_inc(dve_step, 1)
                nc.vector.tensor_copy(weighted[:, :, :, DH], wt).then_inc(dve_step, 1)
                dve.wait_ge(dve_step, base + 2)
                nc.vector.tensor_copy(v[:, :, 0, :], w).then_inc(dve_step, 1)
                dve.wait_ge(dve_step, base + 3)
                nc.vector.tensor_tensor(r, w, v[:, :, 0, :], ALU.subtract).then_inc(dve_step, 1)
                dve.wait_ge(dve_step, base + 4)
                nc.vector.tensor_copy(v[:, :, 1, :], r).then_inc(dve_step, 1)
                dve.wait_ge(dve_step, base + 5)
                nc.vector.tensor_tensor(v[:, :, 2, :], r, v[:, :, 1, :], ALU.subtract).then_inc(vals_ready, 1)

            def cut(h, i, j):
                if j % GROUP == 0:
                    dve.wait_ge(bank_passed, BANKS * (NG * h + j // GROUP + 1))
                m, g = masks[j % RING], signs[:, j % SIGNS, :]
                if j in SIGN_ON_DVE:
                    dve.wait_ge(neg_cut, T * h + j + 1)
                    nc.vector.tensor_scalar(g, s1_bc[i][:], neg_s2[:, j, bass.ds(h, 1)], EDGE, ALU.is_lt, ALU.mult)\
                        .then_inc(signs_dve, 1)
                    dve.wait_ge(signs_dve, N_DVE * h + up_to(SIGN_ON_DVE, j))
                else:
                    dve.wait_ge(signs_act, N_ACT * h + up_to(act_tiles, j))
                nc.vector.tensor_tensor(m[:, 0, :].bitcast(I32), edges[:, j, :].bitcast(I32), g.bitcast(I32),
                                        ALU.bitwise_and).then_inc(neg_cut, 1)
                if j not in POS_ON_POOL:
                    dve.wait_ge(neg_cut, SIGNS + T * h + j + 1)
                    nc.vector.tensor_tensor(m[:, 1, :].bitcast(I32), edges[:, j, :].bitcast(I32), m[:, 0, :].bitcast(I32),
                                            ALU.bitwise_xor).then_inc(pos_dve, 1)

            def empty_banks(h, base):
                dve.wait_ge(head_done, ONE + h)
                for b in range(BANKS):
                    dve.wait_ge(bank_passed, BANKS * (2 + NG * h + NG - 1) + b + 1)
                    nc.vector.tensor_reduce(
                        sums[:, b * Q_PER_BANK:(b + 1) * Q_PER_BANK].rearrange("p q s d -> p (q s) d"),
                        psum[b][:, 0:2 * Q_PER_BANK * SIDE].rearrange("p (g a d) -> p g d a", a=PART, d=DV),
                        AX.X, ALU.add).then_inc(bank_free, 1)
                dve.wait_ge(bank_free, BANKS * (h + 2))
                rs = row_scale[:, :, bass.ds(h, 1), :].rearrange("p t a s -> p t (a s)")
                nc.vector.tensor_tensor(den2[:], sums[:, :, :, DH], rs, ALU.mult).then_inc(dve_step, 1)
                dve.wait_ge(dve_step, base + 1)
                nc.vector.tensor_reduce(den[:], den2[:], AX.X, ALU.add).then_inc(dve_step, 1)
                dve.wait_ge(dve_step, base + 2)
                nc.vector.reciprocal(rden[:], den[:]).then_inc(dve_step, 1)
                dve.wait_ge(dve_step, base + 3)
                nc.vector.tensor_tensor(scale_n[:], rs, rden[:].unsqueeze(2).to_broadcast([P, T, 2]), ALU.mult)\
                    .then_inc(scale_ready, 1)

            def wait_s1(hp, i):
                dve.wait_ge(s1_in[i], 16 * hp + 16)

            dve.sem_inc(neg_cut, SIGNS)
            dve.sem_inc(bank_free, BANKS)
            dve.wait_ge(weights_ready, 4)
            dve.wait_ge(seq_ready, ONE + T)
            dve.wait_ge(edges_ready, T)
            wait_s1(0, 0)
            split_values(0, 0, SETUP_STEPS)
            for j in range(GROUP):
                cut(0, 0, j)

            def head(h, hp_next, i, is_last):
                for j in range(GROUP, 2 * GROUP):
                    cut(h, i, j)
                if not is_last:
                    split_next(h, i)
                for j in range(2 * GROUP, T):
                    cut(h, i, j)
                if not is_last:
                    wait_s1(hp_next, 1 - i)
                    for j in range(GROUP):
                        cut(h + 1, 1 - i, j)
                empty_banks(h, SETUP_STEPS + SPLIT + (SPLIT + SCALE) * h + (0 if is_last else SPLIT))

            def split_next(h, i):
                dve.wait_ge(bank_passed, BANKS * (NG * h + 2))
                split_values(h + 1, 1 - i, SETUP_STEPS + SPLIT + (SPLIT + SCALE) * h)
            with dve.Fori(0, H // 2 - 1) as hp:
                for i in range(2):
                    head(2 * hp + i, hp + i, i, False)
            head(H - 2, H // 2 - 1, 0, False)
            head(H - 1, 0, 1, True)
            steps[0] += (SPLIT + SCALE) * H

            def low(t, i):
                dve.wait_ge(y_done, 2 + t + 1)
                dve.wait_ge(x2_ready, t + 1)
                nc.vector.tensor_tensor(y[:, i, :], psum[2 + i][:, :], b_out_sb[:], ALU.add).then_inc(y_bank_free, 1)
                dve.wait_ge(y_bank_free, 2 + t + 1)
                nc.vector.tensor_scalar(y_low[:, i, :], y[:, i, :], 0.0, None, ALU.min).then_inc(y_low_ready, 1)

            def add_x(t, i):
                nc.vector.scalar_tensor_tensor(out=x_plus[:, i, :], in0=y[:, i, :], scalar=0.0,
                                               in1=x2[:, bass.ds(t, 1), :].rearrange("p a s -> p (a s)"),
                                               op0=ALU.max, op1=ALU.add).then_inc(x_plus_ready, 1)
                dve.wait_ge(y_exp_ready, t + 1)
                dve.wait_ge(x_plus_ready, t + 1)
                nc.vector.scalar_tensor_tensor(out=x2[:, bass.ds(t, 1), :].rearrange("p a s -> p (a s)"),
                                               in0=y_exp[:, i, :], scalar=-1.0, in1=x_plus[:, i, :],
                                               op0=ALU.add, op1=ALU.add).then_inc(x2_ready, 1)
                dve.wait_ge(x2_ready, 2 + t + 1)
                nc.vector.bn_stats(stats2[:, bass.ds(t, 1), :].rearrange("p a s -> p (a s)"),
                                   x2[:, bass.ds(t, 1), :].rearrange("p a s -> p (a s)")).then_inc(stats2_ready, 1)

            dve.sem_inc(x2_ready, 2)
            dve.sem_inc(y_bank_free, 2)
            dve.wait_ge(head_done, ONE + H)
            dve.wait_ge(w_out_in, 32)
            dve.wait_ge(x2_in, 64)
            low(0, 0)
            with dve.Fori(0, T // 2 - 1) as tp:
                for i in range(2):
                    low(2 * tp + i + 1, 1 - i)
                    add_x(2 * tp + i, i)
            low(T - 1, 1)
            add_x(T - 2, 0)
            add_x(T - 1, 1)
            dve.wait_ge(stats2_ready, T)
            for t in range(T):
                nc.vector.bn_aggr(mean_var2[:, t, :], stats2[:, t, :]).then_inc(stats2_ready, 1)
            dve.wait_ge(stats2_ready, 2 * T)
            nc.vector.tensor_scalar(mean_var2[:, :, 1], mean_var2[:, :, 1], EPS, None, ALU.add).then_inc(std2_ready, 1)
            dve.wait_ge(std2_ready, 2)
            step(nc.vector.reciprocal(rstd2[:], std2[:]))

            def norm2(t, i):
                dve.wait_ge(xn2_turned, t + 1)
                nc.vector.tensor_scalar(xn2[i][:], x2[:, bass.ds(t, 1), :].rearrange("p a s -> p (a s)"),
                                        mean_var2[:, bass.ds(t, 1), 0:1].rearrange("p a s -> p (a s)"),
                                        rstd2[:, bass.ds(t, 1)], ALU.subtract, ALU.mult).then_inc(xn2_ready, 1)
            with dve.Fori(0, T // 2) as tp:
                for i in range(2):
                    norm2(2 * tp + i, i)

            e = {n: v[:] for n, v in ent.items()}
            flat = {n: v[:].rearrange("p t e -> p (t e)") for n, v in ent.items()}

            def over_e(a):
                return a.unsqueeze(2).to_broadcast([P, T, E])

            def over_t(a):
                return a.unsqueeze(1).to_broadcast([P, T, E])

            dve.wait_ge(k_ready, 1)
            step(nc.vector.tensor_copy(k_row[:], k_int[:]))
            nc.vector.memset(keep[:], 1.0).then_inc(k_ready, 1)
            step(nc.vector.reciprocal(inv_k[:], k_row[:]))
            dve.wait_ge(k_ready, 2)
            step(nc.vector.memset(keep[:, :, 0:1], 0.0))
            dve.wait_ge(u_done, T)
            step(nc.vector.tensor_copy(e["u"], psum[7][:, 0:T * E].rearrange("p (t e) -> p t e", e=E)))
            step(nc.vector.tensor_reduce(col["sum"][:], e["u"], AX.X, ALU.add))
            step(nc.vector.tensor_scalar(col["mean"][:], col["sum"][:], 1.0 / E, None, ALU.mult))
            step(nc.vector.tensor_tensor(e["c"], e["u"], over_e(col["mean"][:]), ALU.subtract))
            step(nc.vector.tensor_tensor(e["sq"], e["c"], e["c"], ALU.mult))
            step(nc.vector.tensor_reduce(col["sum"][:], e["sq"], AX.X, ALU.add))
            nc.vector.tensor_scalar(col["var"][:], col["sum"][:], 1.0 / E, EPS, ALU.mult, ALU.add).then_inc(var_ready, 1)
            dve.wait_ge(var_std_ready, 1)
            step(nc.vector.reciprocal(col["rstd"][:], col["std"][:]))
            step(nc.vector.tensor_tensor(e["v"], e["c"], over_e(col["rstd"][:]), ALU.mult))
            step(nc.vector.tensor_scalar(e["v"], e["v"], 0.5, None, ALU.mult))
            step(nc.vector.tensor_reduce(col["max"][:], e["v"], AX.X, ALU.max))
            step(nc.vector.tensor_tensor(e["z"], e["v"], over_e(col["max"][:]), ALU.subtract))
            for t in range(T):
                i = nc.vector.max(e["sorted"][:, t, 0:8], e["z"][:, t, :])
            step(i)
            for t in range(T):
                i = nc.vector.match_replace(e["rest"][:, t, :], e["sorted"][:, t, 0:8], e["z"][:, t, :], -1e30)
            step(i)
            for t in range(T):
                i = nc.vector.max(e["sorted"][:, t, 8:16], e["rest"][:, t, :])
            step(i)
            step(nc.vector.tensor_tensor(e["sorted2"], e["sorted"], e["sorted"], ALU.mult))
            kf = keep[:].rearrange("p t e -> p (t e)")
            step(nc.vector.tensor_tensor_scan(flat["cum"], kf, flat["sorted"], 0.0, ALU.mult, ALU.add))
            step(nc.vector.tensor_tensor_scan(flat["cum2"], kf, flat["sorted2"], 0.0, ALU.mult, ALU.add))
            step(nc.vector.tensor_tensor(e["mean"], e["cum"], over_t(inv_k[:]), ALU.mult))
            step(nc.vector.tensor_tensor(e["msq"], e["cum2"], over_t(inv_k[:]), ALU.mult))
            step(nc.vector.tensor_tensor(e["cum"], e["mean"], e["mean"], ALU.mult))
            step(nc.vector.tensor_tensor(e["msq"], e["msq"], e["cum"], ALU.subtract))
            step(nc.vector.tensor_tensor(e["msq"], over_t(inv_k[:]), e["msq"], ALU.subtract))
            nc.vector.tensor_scalar(e["delta"], e["msq"], 0.0, None, ALU.max).then_inc(delta_ready, 1)
            dve.wait_ge(root_ready, 1)
            step(nc.vector.tensor_tensor(e["tau"], e["mean"], e["root"], ALU.subtract))
            step(nc.vector.tensor_tensor(e["in_support"], e["tau"], e["sorted"], ALU.is_le))
            step(nc.vector.tensor_reduce(col["support"][:], e["in_support"], AX.X, ALU.add))
            step(nc.vector.tensor_tensor(e["pick"], over_t(k_row[:]), over_e(col["support"][:]), ALU.is_equal))
            step(nc.vector.tensor_tensor(e["pick"], e["pick"], e["tau"], ALU.mult))
            step(nc.vector.tensor_reduce(col["tau"][:], e["pick"], AX.X, ALU.add))
            step(nc.vector.tensor_tensor(e["z"], e["z"], over_e(col["tau"][:]), ALU.subtract))
            step(nc.vector.tensor_scalar(e["z"], e["z"], 0.0, None, ALU.max))
            step(nc.vector.tensor_tensor(e["a"], e["z"], e["z"], ALU.mult))
            with dve.Fori(0, T // 2) as tp:
                for i in range(2):
                    dve.wait_ge(a_turned, 2 * tp + i + 1)
                    nc.vector.tensor_copy(a_col[i][:], ent["a"][:, bass.ds(2 * tp + i, 1), :].rearrange("p a s -> p (a s)"))\
                        .then_inc(a_col_ready, 1)

            dve.wait_ge(z1_pre_ready, ONE + KR * C)
            dve.wait_ge(ffn_in, FFN_LOADS)

            def rows_out(c, ts):
                for t in ts:
                    n = TPC * c + t
                    dve.wait_ge(o_done, n + 1)
                    dve.wait_ge(out_saved[t % 2], 16 + 16 * ((TPC // 2) * c + t // 2))
                    nc.vector.tensor_tensor(out_rows[:, t % 2, :], psum[6 + t % 2][:, :],
                                            x2[:, bass.ds(n, 1), :].rearrange("p a s -> p (a s)"), ALU.add)\
                        .then_inc(o_ready, 1)

            TPC = T // C
            with dve.Fori(0, C // 2) as cp:
                for i in range(2):
                    c = 2 * cp + i
                    for k in range(KR):
                        dve.wait_ge(gate1_done, KR * c + k + 1)
                        nc.vector.scalar_tensor_tensor(out=z1[i][:, k, :], in0=z1_pre[:, k, bass.ds(CT * c, CT)],
                                                       scalar=bias1[:, k:k + 1], in1=psum[0][:, :],
                                                       op0=ALU.add, op1=ALU.mult).then_inc(z1_ready, 1)
                    dve.wait_ge(gate2_ready, ONE + KR * (c + 1))
                    dve.wait_ge(h_used, HR + KO * (c + 1))
                    for k in range(KR):
                        nc.vector.scalar_tensor_tensor(out=z2[i][:, k, :], in0=psum[4 + k][:, :],
                                                       scalar=bias2[:, k:k + 1], in1=gate2[i][:, k, :],
                                                       op0=ALU.add, op1=ALU.mult).then_inc(z2_ready, 1)
                    rows_out(c, range(TPC))

        @block.tensor
        def _(pe):
            mm = nc.tensor.matmul

            def turn_xn(t, i):
                pe.wait_ge(xn_ready, t + 1)
                for k in range(KD):
                    m = nc.tensor.transpose(psum[i][:, k * P:(k + 1) * P], xn[i][:, k * P:(k + 1) * P], ident[:])
                m.then_inc(xn_turned, 1)

            def project(t, i):
                pe.wait_ge(xn_t_ready, t + 1)
                for k in range(KD):
                    mm(psum[2 + i][:, :], xn_t[i][:, k, :], w_seq_sb[:, k, :], start=(k == 0), stop=(k == KD - 1))
                for k in range(KD):
                    mm(psum[4 + i][:, 0:2 * H], xn_t[i][:, k, :], wa[:, k, :], start=(k == 0), stop=(k == KD - 1))
                for k in range(KD):
                    m = mm(psum[6 + i][0:H, 0:P], wa[:, k, 0:H], xn_t[i][:, k, :], start=(k == 0), stop=(k == KD - 1))
                m.then_inc(proj_done, 1)

            pe.sem_inc(proj_done, 2)
            pe.wait_ge(ident_ready, 2)
            pe.wait_ge(w_seq_in, 16)
            turn_xn(0, 0)
            turn_xn(1, 1)
            pe.wait_ge(wa_ready, 2)
            project(0, 0)
            with pe.Fori(0, T // 2 - 1) as tp:
                for i in range(2):
                    pe.wait_ge(xn_t_ready, 2 * tp + i + 1)
                    turn_xn(2 * tp + i + 2, i)
                    pe.wait_ge(seq_ready, ONE + 2 * tp + i)
                    pe.wait_ge(s12_ready, ONE + 2 * (2 * tp + i))
                    project(2 * tp + i + 1, 1 - i)
            pe.wait_ge(seq_ready, ONE + T - 2)
            pe.wait_ge(s12_ready, ONE + 2 * (T - 2))
            project(T - 1, 1)

            def group(h, i, g):
                js = range(g * GROUP, (g + 1) * GROUP)
                if g == 0:
                    pe.wait_ge(vals_ready, h + 1)
                pe.wait_ge(neg_cut, SIGNS + T * h + js[-1] + 1)
                if up_to(pos_dve_tiles, js[-1]):
                    pe.wait_ge(pos_dve, N_PDVE * h + up_to(pos_dve_tiles, js[-1]))
                if up_to(POS_ON_POOL, js[-1]):
                    pe.wait_ge(pos_pool, N_POOL * h + up_to(POS_ON_POOL, js[-1]))
                for b in range(BANKS):
                    if g == 0:
                        pe.wait_ge(bank_free, BANKS * h + b + 1)
                    if g == 0 or b == 0:
                        pe.sem_inc(pe_passed_waits)
                    for j in js:
                        for q in range(Q_PER_BANK):
                            for s in range(2):
                                at = (q * 2 + s) * SIDE
                                n = b * Q_PER_BANK + q
                                m = mm(psum[b][:, at:at + SIDE], masks[j % RING][:, s, n * P:(n + 1) * P].bitcast(F8),
                                       vals[i][:, j, s].rearrange("p a d -> p (a d)"),
                                       start=(j == 0 and q == 0 and s == 0), stop=(j == T - 1), skip_group_check=True)
                    m.then_inc(bank_passed, 1)

            pe.sem_inc(bank_passed, 2 * BANKS)
            pe.wait_ge(seq_ready, ONE + T)
            with pe.Fori(0, H // 2) as hp:
                for i in range(2):
                    for g in range(NG):
                        group(2 * hp + i, i, g)

            def turn_h(t, i):
                pe.wait_ge(h_copied, t + 1)
                pe.wait_ge(h_t_ready, t + 1)
                for k in range(KD):
                    m = nc.tensor.transpose(psum[i][:, k * P:(k + 1) * P], h_copy[i][:, k * P:(k + 1) * P], ident[:])
                m.then_inc(h_turned, 1)

            def out_project(t, i):
                pe.wait_ge(h_t_ready, 2 + t + 1)
                pe.wait_ge(y_bank_free, t + 1)
                for k in range(KD):
                    m = mm(psum[2 + i][:, :], h_t[i][:, k, :], w_out_sb[:, k, :], start=(k == 0), stop=(k == KD - 1))
                m.then_inc(y_done, 1)

            pe.wait_ge(bank_free, BANKS * (H + 1))
            pe.wait_ge(w_out_in, 32)
            pe.sem_inc(h_turned, 2)
            pe.sem_inc(h_t_ready, 2)
            pe.sem_inc(y_done, 2)
            turn_h(0, 0)
            with pe.Fori(0, T // 2 - 1) as tp:
                for i in range(2):
                    turn_h(2 * tp + i + 1, 1 - i)
                    out_project(2 * tp + i, i)
            turn_h(T - 1, 1)
            out_project(T - 2, 0)
            out_project(T - 1, 1)

            pe.sem_inc(xn2_turned, 2)
            pe.sem_inc(a_turned, 2)
            pe.wait_ge(ffn_in, FFN_LOADS)

            def turn_xn2(t, i):
                pe.wait_ge(xn2_ready, t + 1)
                for k in range(KD):
                    m = nc.tensor.transpose(psum[i][:, k * P:(k + 1) * P], xn2[i][:, k * P:(k + 1) * P], ident[:])
                m.then_inc(xn2_turned, 1)
            turn_xn2(0, 0)
            turn_xn2(1, 1)
            with pe.Fori(1, T // 2) as tp:
                for i in range(2):
                    pe.wait_ge(xn2_t_ready, 2 * tp + i - 1)
                    turn_xn2(2 * tp + i, i)
            pe.wait_ge(xn2_t_ready, T)
            for t in range(T):
                for k in range(KD):
                    m = mm(psum[7][:, t * E:(t + 1) * E], xn2_t[:, k, t * P:(t + 1) * P], proj_sb[:, k, :],
                           start=(k == 0), stop=(k == KD - 1))
                m.then_inc(u_done, 1)
            with pe.Fori(0, C) as c:
                for r in range(KR):
                    if r == 0:
                        pe.wait_ge(z1_pre_ready, ONE + KR * c)
                    for k in range(KD):
                        m = mm(psum[4 + r][:, :], win1_sb[:, k, r * P:(r + 1) * P], xn2_t[:, k, bass.ds(CT * c, CT)],
                               start=(k == 0), stop=(k == KD - 1))
                    m.then_inc(z1_pre_done, 1)
            def turn_a(t, i):
                pe.wait_ge(a_col_ready, t + 1)
                nc.tensor.transpose(psum[i][0:E, 0:P], a_col[i][:], ident[:]).then_inc(a_turned, 1)
            turn_a(0, 0)
            turn_a(1, 1)
            with pe.Fori(1, T // 2) as tp:
                for i in range(2):
                    pe.wait_ge(a_t_ready, 2 * tp + i - 1)
                    turn_a(2 * tp + i, i)

            pe.sem_inc(h_used, HR)
            pe.wait_ge(a_t_ready, T)
            TPC = T // C
            with pe.Fori(0, C // 2) as cp:
                for i in range(2):
                    c = 2 * cp + i
                    for r in range(KR):
                        if r == 0:
                            pe.wait_ge(gate2_ready, ONE + KR * c)
                        else:
                            pe.wait_ge(z1_ready, KR * c + r)
                        pe.sem_inc(pe_passed_waits)
                        mm(psum[0][:, :], c1_sb[:, r * P:(r + 1) * P], a_t[:, bass.ds(CT * c, CT)], start=True, stop=True)\
                            .then_inc(gate1_done, 1)
                    for r in range(KR):
                        if r == 0:
                            pe.wait_ge(z1_ready, KR * (c + 1))
                        else:
                            pe.wait_ge(gate2_ready, ONE + KR * c + r)
                        pe.sem_inc(pe_passed_waits)
                        mm(psum[0][:, :], c2_sb[:, r * P:(r + 1) * P], a_t[:, bass.ds(CT * c, CT)], start=True, stop=True)\
                            .then_inc(gate2_done, 1)

                    def up(o):
                        n = KO * c + o
                        if o >= 3:
                            pe.wait_ge(h_ready, ONE + n - 2)
                        else:
                            pe.wait_ge(h_ready, ONE + KO * c)
                        for k in range(KR):
                            m = mm(psum[1 + o % 3][:, :], wout1_sb[:, k, o * P:(o + 1) * P], z1[i][:, k, :],
                                   start=(k == 0), stop=(k == KR - 1))
                        m.then_inc(h_done, 1)

                    def down(o):
                        pe.wait_ge(h_ready, ONE + KO * c + o + 1)
                        for r in range(KR):
                            m = mm(psum[4 + r][:, :], win2_sb[:, o, r * P:(r + 1) * P], h_ring[o % HR][:],
                                   start=(o == 0), stop=(o == KO - 1))
                        m.then_inc(h_used, 1)
                    pe.wait_ge(z2_ready, ONE + KR * c)
                    up(0)
                    up(1)
                    for o in range(2, KO):
                        up(o)
                        down(o - 2)
                    down(KO - 2)
                    down(KO - 1)
                    pe.wait_ge(z2_ready, ONE + KR * (c + 1))
                    for t in range(TPC):
                        pe.wait_ge(o_ready, ONE + TPC * c + t - 1) if t >= 1 else pe.wait_ge(o_ready, ONE + TPC * c)
                        for k in range(KR):
                            m = mm(psum[6 + t % 2][:, :], z2[i][:, k, t * P:(t + 1) * P], wout2_sb[:, k, :],
                                   start=(k == 0), stop=(k == KR - 1))
                        m.then_inc(o_done, 1)


_INS = ['x', 'adj', 'L0_gnn_W_seq', 'L0_gnn_a1', 'L0_gnn_a2', 'L0_gnn_W_out', 'L0_gnn_b_out', 'L0_ffn_proj', 'L0_ffn_C1',
        'L0_ffn_Win1', 'L0_ffn_Wout1', 'L0_ffn_C2', 'L0_ffn_Win2', 'L0_ffn_Wout2']
_TRANSPOSED = ('adj', 'L0_ffn_Wout1', 'L0_ffn_Wout2')


def kernel(**inputs):
    import numpy as _np
    import concourse.bacc as _bacc
    from concourse import mybir as _mybir
    from concourse.bass_utils import run_bass_kernel_spmd as _run

    nc = _bacc.Bacc("TRN2", target_bir_lowering=False, num_devices=1)
    arrays, args = {}, []
    for name in _INS:
        a = _np.asarray(inputs[name])
        a = _np.ascontiguousarray(a.T if name in _TRANSPOSED else a)
        arrays[f"in_{name}_dram"] = a
        args.append(nc.dram_tensor(f"in_{name}_dram", a.shape, _mybir.dt.from_np(a.dtype), kind="ExternalInput").ap())
    n, d = inputs['x'].shape
    args.append(nc.dram_tensor("out_0_dram", (n, d), _mybir.dt.float32, kind="ExternalOutput").ap())
    gat_ffn(nc, *args)
    r = _run(nc, [arrays], core_ids=[0])
    return r.results[0]["out_0_dram"]
```

```python
from contextlib import ExitStack

import concourse.bass as bass
from concourse import mybir

F32 = mybir.dt.float32
F32R = mybir.dt.float32r
BF16 = mybir.dt.bfloat16
F8 = mybir.dt.float8e4
I8 = mybir.dt.int8
I32 = mybir.dt.int32
ALU = mybir.AluOpType
ACT = mybir.ActivationFunctionType
AX = mybir.AxisListType
P = 128


def gat_ffn(nc, x, adj_t, w_seq, a1, a2, w_out, b_out, proj, c1, win1, wout1_t, c2, win2, wout2_t, out):
    N, D = x.shape
    DH = a1.shape[0]
    H = D // DH
    T = N // P
    KD = D // P
    E, R = c1.shape
    KR = R // P
    O = win2.shape[0] - 1
    KO = O // P
    C = 4
    CT = N // C
    EPS = 1e-5
    EDGE = 8.0

    DV = DH + 1
    PART = 3
    SIDE = PART * DV
    GROUP = 2
    AHEAD = 6
    NG = T // GROUP
    RING = 8
    GROUPS_FREE = RING // GROUP
    SIGNS = 8
    BANKS = 8
    Q_PER_BANK = T // BANKS

    SIGN_ON_DVE = (9, 13)
    POS_ON_POOL = (0, 1, 3, 8, 9, 11, 12, 13, 15)
    act_tiles = [j for j in range(T) if j not in SIGN_ON_DVE]
    pos_dve_tiles = [j for j in range(T) if j not in POS_ON_POOL]
    N_ACT, N_DVE = len(act_tiles), len(SIGN_ON_DVE)
    N_POOL, N_PDVE = len(POS_ON_POOL), len(pos_dve_tiles)

    def up_to(tiles, j):
        return sum(k <= j for k in tiles)

    s1_dram = nc.dram_tensor("s1_rows", [H, N], F32, kind="Internal").ap()

    with ExitStack() as ctx:
        def sem(name):
            return ctx.enter_context(nc.semaphore(name))

        psum = [ctx.enter_context(nc.psum_tensor(f"bank{b}", [P, 512], F32)) for b in range(BANKS)]

        SBUF_FIRST, SBUF_END = 16512, 229344
        size_of = {F32: 4, F32R: 4, BF16: 2, I8: 1, I32: 4}
        at = [SBUF_FIRST]

        def place(name, shape, dt=F32, over=None):
            size = size_of[dt]
            for n in shape[1:]:
                size *= n
            size = -(-size // 32) * 32
            offset = at[0] if over is None else over
            if over is None:
                at[0] += size
            assert offset + size <= SBUF_END, (name, offset + size - SBUF_END)
            return nc.alloc_sbuf_tensor_at(name, shape, dt, offset=offset)

        ident = place("ident", [P, P])
        ROWS_AT = at[0]
        rows = place("rows", [P, T, D])
        x_rows = rows
        hidden = rows

        SEQ_AT = at[0]
        seq = place("seq", [P, T, D])
        EDGES_AT = at[0]
        edges = place("edges", [P, T, N], I8)
        weight = place("weight", [P, T, H, 2])
        row_scale = place("row_scale", [P, T, H, 2])
        s12 = place("s12", [P, T, 2 * H])
        neg_s2 = place("neg_s2", [P, T, H])
        guard = place("guard", [P, H])
        SETUP_AT = at[0]
        signs = place("signs", [P, SIGNS, N], I8)
        masks = [place(f"masks{i}", [P, 2, N], I8) for i in range(RING)]
        s1_bc = [place(f"s1_bc{i}", [P, N]) for i in range(2)]
        vals = [place(f"vals{i}", [P, T, 2, PART, DV], BF16) for i in range(2)]
        weighted = place("weighted", [P, T, 2, DV])
        residue = place("residue", [P, T, 2, DV])
        sums = place("sums", [P, T, 2, DV])
        scaled = place("scaled", [P, T, 2, DH])
        den2 = place("den2", [P, T, 2])
        den = place("den", [P, T])
        rden = place("rden", [P, T])
        scale_n = place("scale_n", [P, T, 2])

        at[0] = SETUP_AT
        w_seq_sb = place("w_seq_sb", [P, KD, D])
        a12 = place("a12", [P, 2, DH])
        wa = place("wa", [P, KD, 2 * H])
        wa_prod = place("wa_prod", [P, 2, KD, D])
        adj_stage = place("adj_stage", [P, 2, N])
        xn = [place(f"xn{i}", [P, D]) for i in range(2)]
        xn_t = [place(f"xn_t{i}", [P, KD, P]) for i in range(2)]
        s1_t = place("s1_t", [H, N])
        stats = place("stats", [P, T, 6])
        mean_var = place("mean_var", [P, T, 2])
        std = place("std", [P, T])
        rstd = place("rstd", [P, T])
        smax = place("smax", [P, H])
        shifted = place("shifted", [P, 3, T, H])

        HALF = KR * CT
        xn2_lo = place("xn2_lo", [P, KD, CT], F32R, ROWS_AT)
        z1_pre = place("z1_pre", [P, C, KR, CT], F32, ROWS_AT + 2 * 4 * HALF)
        z1_eighths = place("z1_parts", [P, 2 * C, HALF], F32R, ROWS_AT)

        def z1_parts(c):
            first = 0 if isinstance(c, int) and c == 0 else 9 - 3 * c
            return [z1_eighths[:, bass.ds(first + part, 1), :].rearrange("p a n -> p (a n)") for part in range(2)]

        at[0] = SEQ_AT
        STAGE_AT = at[0]
        PIECE = 2 * D
        stage = [place(f"stage{i}", [P, PIECE]) for i in range(2)]
        W_OUT_AT = at[0]
        w_out_hi = place("w_out_hi", [P, KD, D], F32R)
        w_out_lo = place("w_out_lo", [P, KD, D], F32R)
        b_hi = place("b_hi", [1, D], F32R)
        b_lo = place("b_lo", [1, D], F32R)
        ones = place("ones", [1, P], F32R)
        wout2_hi = place("wout2_hi", [P, KR, D], F32R, W_OUT_AT)
        wout2_lo = place("wout2_lo", [P, KR, D], F32R, W_OUT_AT + 4 * KR * D)
        proj_sb = place("proj_sb", [P, KD, E])
        bias1 = place("bias1", [P, KR])
        bias2 = place("bias2", [P, KR])
        keep = place("keep", [P, T, E])
        c_raw = place("c_raw", [3 * E, 2, R])
        assert at[0] <= EDGES_AT
        at[0] = EDGES_AT
        x2 = place("x2", [P, T, D])
        win1_hi = place("win1_hi", [P, KD, R], F32R)
        win1_lo = place("win1_lo", [P, KD, R], F32R)
        wout1_hi = place("wout1_hi", [P, KR, O], F32R)
        wout1_lo = place("wout1_lo", [P, KR, O], F32R)
        win2_hi = place("win2_hi", [P, KO, R], F32R)
        win2_lo = place("win2_lo", [P, KO, R], F32R)
        a_all = place("a_all", [P, T, 3 * E], F32R)
        u_sb = place("u_sb", [P, T, E])
        c_hl = place("c_hl", [3 * E, 2, R], F32R)
        k_int = place("k_int", [P, E], I32)
        k_row = place("k_row", [P, E])
        inv_k = place("inv_k", [P, E])
        col_all = {n: place(f"col_{n}", [P, T]) for n in ("sum", "mean", "var", "std", "rstd", "max", "support", "tau")}
        stats2 = place("stats2", [P, T, 6])
        mean_var2 = place("mean_var2", [P, T, 2])
        std2 = place("std2", [P, T])
        rstd2 = place("rstd2", [P, T])
        WORK_AT = at[0]
        hq = [place(f"hq{i}", [P, D]) for i in range(2)]
        h_hi = [place(f"h_hi{i}", [P, KD, P], F32R) for i in range(2)]
        h_lo = [place(f"h_lo{i}", [P, KD, P], F32R) for i in range(2)]
        y_exp = place("y_exp", [P, 2, D])
        x_plus = place("x_plus", [P, 2, D])
        xn2 = [place(f"xn2_{i}", [P, D]) for i in range(2)]
        xn2_hi = place("xn2_hi", [P, KD, CT], F32R)
        ENT_TILES = (range(0, T // C), range(T // C, T))
        ENT_AT_BYTE = (ROWS_AT + 5 * 4 * HALF, WORK_AT + 4 * KR * CT)
        ent, col = [], []
        for part, tiles in enumerate(ENT_TILES):
            e = {}
            for i, n in enumerate(("z", "sq", "rest", "sorted", "cum", "mean", "msq", "root", "tau", "pick")):
                e[n] = place(f"ent{part}_{n}", [P, len(tiles), E], F32, ENT_AT_BYTE[part] + 4 * E * len(tiles) * i)
            e["sorted2"], e["cum2"], e["a"] = e["sq"], e["rest"], e["mean"]
            ent.append(e)
            col.append({n: col_all[n][:, tiles[0]:tiles[-1] + 1] for n in col_all})
        HR = 4
        a_col = place("a_col", [P, T // C, 3 * E], F32, W_OUT_AT + 8 * KD * D + 4 * CT)
        gate2 = place("gate2", [P, KR, CT], F32, STAGE_AT)
        out_rows = place("out_rows", [P, 2, D], F32, STAGE_AT + 4 * KR * CT)
        at[0] = WORK_AT
        z_tmp = place("z_tmp", [P, KR, CT])
        z2_hi = place("z2_hi", [P, KR, CT], F32R)
        z2_lo = place("z2_lo", [P, KR, CT], F32R)
        h_full = [place(f"h_full{i}", [P, CT]) for i in range(2)]
        hr_hi = [place(f"hr_hi{i}", [P, CT], F32R) for i in range(HR)]
        hr_lo = [place(f"hr_lo{i}", [P, CT], F32R) for i in range(HR)]
        a_t = place("a_t", [3 * E, CT], F32R, W_OUT_AT + 8 * KD * D)

        w_out_v = w_out.rearrange("(k p) n -> p k n", p=P)
        wout1_v = wout1_t.rearrange("(k p) n -> p k n", p=P)
        win2_v = win2[0:O, :].rearrange("(k p) n -> p k n", p=P)

        def flat_kn(a):
            return a.rearrange("p k n -> p (k n)")

        pieces = []
        for k in range(0, KD, 2):
            pieces.append((w_out_v[:, k:k + 2, :], flat_kn(w_out_hi[:, k:k + 2, :]), flat_kn(w_out_lo[:, k:k + 2, :])))
        pieces.append((b_out.rearrange("(a n) -> a n", a=1), b_hi[:], b_lo[:]))
        W_OUT_PIECES = len(pieces)
        pieces.append((win1[0:D, :].rearrange("(k p) n -> p k n", p=P), flat_kn(win1_hi[:]), flat_kn(win1_lo[:])))
        WIN1_PIECES = len(pieces)
        for half in range(O // PIECE):
            for k in range(KR):
                o = slice(half * PIECE, (half + 1) * PIECE)
                pieces.append((wout1_v[:, k, o], wout1_hi[:, k, o], wout1_lo[:, k, o]))
        WOUT1_PIECES = len(pieces)
        for k in range(0, KO, PIECE // R):
            o = slice(k, k + PIECE // R)
            pieces.append((win2_v[:, o, :], flat_kn(win2_hi[:, o, :]), flat_kn(win2_lo[:, o, :])))
        WIN2_PIECES = len(pieces)
        pieces.append((wout2_t.rearrange("(k p) n -> p k n", p=P), flat_kn(wout2_hi[:]), flat_kn(wout2_lo[:])))

        def stage_of(n):
            hi = pieces[n][1]
            return stage[n % 2][0:hi.shape[0], 0:hi.shape[1]]

        ONE = 1
        x_in = [sem(f"x_in{q}") for q in range(4)]
        w_seq_in = sem("w_seq_in")
        a_in = sem("a_in")
        adj_in = [sem(f"adj_in{i}") for i in range(2)]
        s1_saved = sem("s1_saved")
        s1_in = [sem(f"s1_in{i}") for i in range(2)]
        x2_in = [sem(f"x2_in{q}") for q in range(4)]
        out_saved = [sem(f"out_saved{i}") for i in range(2)]
        ident_ready = sem("ident_ready")
        dve_step = sem("dve_step")
        std_ready = sem("std_ready")
        wa_ready = sem("wa_ready")
        xn_ready = sem("xn_ready")
        xn_turned = sem("xn_turned")
        xn_t_ready = sem("xn_t_ready")
        proj_done = sem("proj_done")
        seq_ready = sem("seq_ready")
        s12_ready = sem("s12_ready")
        edges_ready = sem("edges_ready")
        smax_ready = sem("smax_ready")
        guard_ready = sem("guard_ready")
        shifted_ready = sem("shifted_ready")
        weights_ready = sem("weights_ready")
        signs_act = sem("signs_act")
        signs_dve = sem("signs_dve")
        neg_cut = sem("neg_cut")
        pos_dve = sem("pos_dve")
        pos_pool = sem("pos_pool")
        bank_passed = sem("bank_passed")
        weighted_ready = sem("weighted_ready")
        vals_ready = sem("vals_ready")
        pe_passed_waits = sem("pe_passed_waits")
        sp_passed_waits = sem("sp_passed_waits")
        bank_free = sem("bank_free")
        scale_ready = sem("scale_ready")
        scaled_ready = sem("scaled_ready")
        head_done = sem("head_done")
        piece_in = [sem(f"piece_in{i}") for i in range(2)]
        w_hi_ready = sem("w_hi_ready")
        w_lo_ready = sem("w_lo_ready")
        small_in = sem("small_in")
        small_ready = sem("small_ready")
        hq_in = [sem(f"hq_in{i}") for i in range(2)]
        h_turned = sem("h_turned")
        h_hi_ready = sem("h_hi_ready")
        h_lo_ready = sem("h_lo_ready")
        y_done = sem("y_done")
        y_low_ready = sem("y_low_ready")
        y_exp_ready = sem("y_exp_ready")
        x_plus_ready = sem("x_plus_ready")
        x2_ready = sem("x2_ready")
        stats2_ready = sem("stats2_ready")
        mean_var2_ready = sem("mean_var2_ready")
        var2_ready = sem("var2_ready")
        std2_ready = sem("std2_ready")
        rstd2_ready = sem("rstd2_ready")
        xn2_ready = sem("xn2_ready")
        xn2_turned = sem("xn2_turned")
        xn2_hi_ready = sem("xn2_hi_ready")
        xn2_lo_ready = sem("xn2_lo_ready")
        u_done = sem("u_done")
        u_ready = sem("u_ready")
        z1_pre_done = sem("z1_pre_done")
        z1_pre_ready = sem("z1_pre_ready")
        k_ready = sem("k_ready")
        ent_step = sem("ent_step")
        var_ready = sem("var_ready")
        var_std_ready = sem("var_std_ready")
        delta_ready = sem("delta_ready")
        root_ready = sem("root_ready")
        a_ready = sem("a_ready")
        a_col_ready = sem("a_col_ready")
        a_turned = sem("a_turned")
        a_t_ready = sem("a_t_ready")
        gate1_done = sem("gate1_done")
        gate2_done = sem("gate2_done")
        gate2_ready = sem("gate2_ready")
        z1_tmp_ready = sem("z1_tmp_ready")
        z1_hi_ready = sem("z1_hi_ready")
        z1_ready = sem("z1_ready")
        h_done = sem("h_done")
        h_full_ready = sem("h_full_ready")
        h_hi_cut = sem("h_hi_cut")
        h_split = sem("h_split")
        h_used = sem("h_used")
        z2_tmp_ready = sem("z2_tmp_ready")
        z2_hi_ready = sem("z2_hi_ready")
        z2_ready = sem("z2_ready")
        o_done = sem("o_done")
        o_ready = sem("o_ready")

        x_view = x.rearrange("(t p) d -> p t d", p=P)
        adj_view = adj_t.rearrange("(t p) n -> t p n", p=P)
        out_view = out.rearrange("(t p) d -> t p d", p=P)
        TQ = T // 4

        block = ctx.enter_context(nc.Block())

        @block.sync
        def _(sp):
            for i in range(2):
                sp.sem_inc(out_saved[i], 16)
            for q in range(4):
                sp.dma_start(x_rows[:, q * TQ:(q + 1) * TQ, :], x_view[:, q * TQ:(q + 1) * TQ, :]).then_inc(x_in[q], 16)
            sp.dma_start(w_seq_sb[:], w_seq.rearrange("(k p) n -> p k n", p=P)).then_inc(w_seq_in, 16)
            sp.dma_start(a12[:, 0, :], a1.partition_broadcast(P)).then_inc(a_in, 16)
            sp.dma_start(a12[:, 1, :], a2.partition_broadcast(P)).then_inc(a_in, 16)
            for i in range(2):
                sp.dma_start(adj_stage[:, i, :], adj_view[i]).then_inc(adj_in[i], 16)
            with sp.Fori(1, T // 2) as tp:
                for i in range(2):
                    sp.wait_ge(edges_ready, 2 * tp + i - 1)
                    sp.sem_inc(sp_passed_waits)
                    sp.dma_start(adj_stage[:, i, :], adj_view[bass.ds(2 * tp + i, 1)].rearrange("a p n -> (a p) n"))\
                        .then_inc(adj_in[i], 16)
            sp.wait_ge(s12_ready, ONE + 2 * T)
            sp.dma_start(s1_dram, s1_t[:]).then_inc(s1_saved, 16)
            sp.wait_ge(s1_saved, 16)
            sp.wait_ge(edges_ready, T)
            sp.wait_ge(weights_ready, 4)

            def load_s1(h, i):
                sp.dma_start(s1_bc[i][:], s1_dram[bass.ds(h, 1), :].rearrange("a n -> (a n)").partition_broadcast(P))\
                    .then_inc(s1_in[i], 16)
            load_s1(0, 0)
            load_s1(1, 1)
            with sp.Fori(1, H // 2) as hp:
                for i in range(2):
                    sp.wait_ge(neg_cut, SIGNS + T * (2 * hp + i - 1))
                    sp.sem_inc(sp_passed_waits)
                    load_s1(2 * hp + i, i)

            def load_piece(n):
                if n >= 2:
                    sp.wait_ge(w_lo_ready, n - 1)
                src, slot = pieces[n][0], stage_of(n)
                if len(src.shape) == 3:
                    slot = slot.rearrange("p (k n) -> p k n", k=src.shape[1])
                sp.dma_start(slot, src).then_inc(piece_in[n % 2], 16)

            sp.wait_ge(vals_ready, H)
            for n in range(W_OUT_PIECES):
                load_piece(n)
            sp.dma_start(proj_sb[:], proj.rearrange("(k p) n -> p k n", p=P)).then_inc(small_in, 16)
            for k in range(KR):
                sp.dma_start(bias1[:, k:k + 1], win1[D:D + 1, k * P:(k + 1) * P].rearrange("a p -> p a")).then_inc(small_in, 16)
                sp.dma_start(bias2[:, k:k + 1], win2[O:O + 1, k * P:(k + 1) * P].rearrange("a p -> p a")).then_inc(small_in, 16)
            sp.wait_ge(neg_cut, SIGNS + T * H)
            sp.wait_ge(pos_dve, N_PDVE * H)
            sp.wait_ge(pos_pool, N_POOL * H)
            for q in range(2):
                sp.dma_start(x2[:, q * TQ:(q + 1) * TQ, :], x_view[:, q * TQ:(q + 1) * TQ, :]).then_inc(x2_in[q], 16)
            sp.wait_ge(head_done, ONE + H)

            def load_hidden(tp):
                for i in range(2):
                    if tp > 0:
                        sp.wait_ge(h_turned, 2 * tp + i - 1)
                    sp.dma_start(hq[i][:], hidden[:, 2 * tp + i, :]).then_inc(hq_in[i], 16)
            load_hidden(0)
            for s in range(3):
                sp.dma_start(c_raw[s * E:(s + 1) * E, 0, :], c1).then_inc(small_in, 16)
                sp.dma_start(c_raw[s * E:(s + 1) * E, 1, :], c2).then_inc(small_in, 16)
            load_piece(W_OUT_PIECES)
            load_piece(W_OUT_PIECES + 1)
            n = W_OUT_PIECES + 2
            for tp in range(1, T // 2):
                load_hidden(tp)
                if tp % 2:
                    for _ in range(2 if tp > 1 else 0):
                        load_piece(n)
                        n += 1
                elif tp // 2 + 1 < 4:
                    q = tp // 2 + 1
                    sp.dma_start(x2[:, q * TQ:(q + 1) * TQ, :], x_view[:, q * TQ:(q + 1) * TQ, :]).then_inc(x2_in[q], 16)
            for n in range(n, len(pieces)):
                load_piece(n)

            with sp.Fori(0, T // 2) as tp:
                for i in range(2):
                    sp.wait_ge(o_ready, ONE + 2 * tp + i + 1)
                    sp.sem_inc(sp_passed_waits)
                    sp.dma_start(out_view[bass.ds(2 * tp + i, 1)].rearrange("a p n -> (a p) n"), out_rows[:, i, :])\
                        .then_inc(out_saved[i], 16)
            for i in range(2):
                sp.wait_ge(out_saved[i], 16 + 16 * T // 2)

        TPC = T // C
        SMALL_LOADS = 16 * (1 + 2 * KR + 6)
        FINAL_AT = {3: 0, 4: 1, 5: 2, 6: 3}
        GATE2_AT = {7: 0, 8: 1}
        TURN_A_AT = 9
        GATE1_AT = {11: 0, 13: 1}
        ENT_AT = (0, 2, 4, 6)
        ENT_ROOT_AT = (1, 5)

        @block.gpsimd
        def _(pool):
            pool.sem_inc(head_done, ONE)
            nc.gpsimd.memset(ident[:], 1.0).then_inc(ident_ready, 1)
            pool.wait_ge(ident_ready, 1)
            nc.gpsimd.affine_select(out=ident[:], in_=ident[:], compare_op=ALU.is_equal, fill=0.0, base=0,
                                    pattern=[[-1, P]], channel_multiplier=1).then_inc(ident_ready, 1)
            pool.wait_ge(smax_ready, 1)
            nc.gpsimd.partition_all_reduce(guard[:], smax[:], P, bass.bass_isa.ReduceOp.max).then_inc(guard_ready, 1)

            def cut_pos(h, j):
                if j not in POS_ON_POOL:
                    return
                if j % GROUP == min(k for k in POS_ON_POOL if k // GROUP == j // GROUP) % GROUP:
                    pool.wait_ge(bank_passed, BANKS * (NG * h + j // GROUP + 1))
                pool.wait_ge(neg_cut, SIGNS + T * h + j + 1)
                m = masks[j % RING]
                nc.gpsimd.tensor_tensor(m[:, 1, :].bitcast(I32), edges[:, j, :].bitcast(I32), m[:, 0, :].bitcast(I32),
                                        ALU.subtract).then_inc(pos_pool, 1)

            def weigh(h):
                if not isinstance(h, int):
                    pool.wait_ge(vals_ready, h)
                wt = weight[:, :, bass.ds(h, 1), :].rearrange("p t a s -> p t (a s)")
                nc.gpsimd.tensor_tensor(
                    weighted[:, :, :, 0:DH], seq[:, :, bass.ds(DH * h, DH)].unsqueeze(2).to_broadcast([P, T, 2, DH]),
                    wt.unsqueeze(3).to_broadcast([P, T, 2, DH]), ALU.mult).then_inc(weighted_ready, 1)
                nc.gpsimd.tensor_copy(weighted[:, :, :, DH], wt).then_inc(weighted_ready, 1)

            def combine(h):
                pool.wait_ge(scale_ready, h + 1)
                nc.gpsimd.tensor_tensor(scaled[:], sums[:, :, :, 0:DH], scale_n[:].unsqueeze(3).to_broadcast([P, T, 2, DH]),
                                        ALU.mult).then_inc(scaled_ready, 1)
                pool.wait_ge(scaled_ready, h + 1)
                nc.gpsimd.tensor_tensor(hidden[:, :, bass.ds(DH * h, DH)], scaled[:, :, 0, :], scaled[:, :, 1, :],
                                        ALU.add).then_inc(head_done, 1)

            def lo_piece(n):
                pool.wait_ge(w_hi_ready, n + 1)
                nc.gpsimd.tensor_tensor(pieces[n][2], stage_of(n), pieces[n][1].bitcast(F32), ALU.subtract)\
                    .then_inc(w_lo_ready, 1)

            def head(h, is_last):
                if not is_last:
                    weigh(h + 1)
                for j in range(AHEAD, T):
                    cut_pos(h, j)
                if is_last:
                    for n in range(W_OUT_PIECES):
                        lo_piece(n)
                else:
                    for j in range(AHEAD):
                        cut_pos(h + 1, j)
                    combine(h)

            pool.wait_ge(weights_ready, 4)
            pool.wait_ge(seq_ready, ONE + T)
            weigh(0)
            pool.wait_ge(edges_ready, T)
            for j in range(AHEAD):
                cut_pos(0, j)
            with pool.Fori(0, H - 1) as h:
                head(h, False)
            head(H - 1, True)

            nc.gpsimd.iota(k_int[:], pattern=[[1, E]], base=1, channel_multiplier=0).then_inc(k_ready, 1)

            def copy_a(c):
                pool.wait_ge(a_ready, min(c, 1) + 1)
                if c > 0:
                    pool.wait_ge(a_turned, c)
                nc.gpsimd.tensor_copy(a_col[:], a_all[:, c * TPC:(c + 1) * TPC, :].bitcast(F32)).then_inc(a_col_ready, 1)

            for n in range(W_OUT_PIECES, WOUT1_PIECES + 3):
                lo_piece(n)
            pool.wait_ge(y_done, 2 + T)
            copy_a(0)
            for n in range(WOUT1_PIECES + 3, len(pieces)):
                lo_piece(n)
            for c in range(1, C):
                copy_a(c)

        @block.scalar
        def _(act):
            act.sem_inc(seq_ready, ONE)
            act.sem_inc(gate2_ready, ONE)
            act.sem_inc(h_full_ready, ONE)
            act.wait_ge(dve_step, T + 1 + T)
            nc.scalar.activation(std[:], mean_var[:, :, 1], ACT.Sqrt).then_inc(std_ready, 1)

            def copy_xn_t(t, i):
                act.wait_ge(xn_turned, t + 1)
                act.wait_ge(proj_done, t + 1)
                nc.scalar.activation(xn_t[i][:].rearrange("p k n -> p (k n)"), psum[i][:, :], ACT.Copy).then_inc(xn_t_ready, 1)

            def adj_tile(tp, i):
                act.wait_ge(adj_in[i], 16 * tp + 16)
                nc.scalar.activation(edges[:, bass.ds(2 * tp + i, 1), :].rearrange("p a n -> p (a n)"), adj_stage[:, i, :],
                                     ACT.Copy, scale=EDGE).then_inc(edges_ready, 1)

            def evict_seq(t, i):
                act.wait_ge(proj_done, 2 + t + 1)
                nc.scalar.activation(seq[:, bass.ds(t, 1), :].rearrange("p a d -> p (a d)"), psum[2 + i][:, :], ACT.Copy)\
                    .then_inc(seq_ready, 1)

            copy_xn_t(0, 0)
            with act.Fori(0, T // 2 - 1) as tp:
                for i in range(2):
                    copy_xn_t(2 * tp + i + 1, 1 - i)
                    evict_seq(2 * tp + i, i)
                    adj_tile(tp, i)
            copy_xn_t(T - 1, 1)
            evict_seq(T - 2, 0)
            adj_tile(T // 2 - 1, 0)
            evict_seq(T - 1, 1)
            adj_tile(T // 2 - 1, 1)

            act.wait_ge(shifted_ready, 3)
            nc.scalar.activation(weight[:, :, :, 0], shifted[:, 0], ACT.Exp, scale=0.2).then_inc(weights_ready, 1)
            nc.scalar.activation(weight[:, :, :, 1], shifted[:, 0], ACT.Exp).then_inc(weights_ready, 1)
            nc.scalar.activation(row_scale[:, :, :, 0], shifted[:, 1], ACT.Exp, scale=-0.8).then_inc(weights_ready, 1)
            nc.scalar.activation(row_scale[:, :, :, 1], shifted[:, 2], ACT.Exp, scale=0.8).then_inc(weights_ready, 1)

            def sign(h, i, j):
                if j in SIGN_ON_DVE:
                    return
                act.wait_ge(neg_cut, T * h + j + 1)
                nc.scalar.activation(signs[:, j % SIGNS, :], s1_bc[i][:], ACT.Sign,
                                     bias=s12[:, j, bass.ds(H + h, 1)]).then_inc(signs_act, 1)

            def wait_s1(hp, i):
                act.wait_ge(s1_in[i], 16 * hp + 16)

            act.wait_ge(s12_ready, ONE + 2 * T)
            wait_s1(0, 0)
            for j in range(AHEAD):
                sign(0, 0, j)
            with act.Fori(0, H // 2 - 1) as hp:
                for i in range(2):
                    for j in range(AHEAD, T):
                        sign(2 * hp + i, i, j)
                    wait_s1(hp + i, 1 - i)
                    for j in range(AHEAD):
                        sign(2 * hp + i + 1, 1 - i, j)
            for j in range(AHEAD, T):
                sign(H - 2, 0, j)
            wait_s1(H // 2 - 1, 1)
            def hi_piece(n):
                act.wait_ge(piece_in[n % 2], 16 * (n // 2 + 1))
                nc.scalar.activation(pieces[n][1], stage_of(n), ACT.Copy).then_inc(w_hi_ready, 1)

            for j in range(T):
                sign(H - 1, 1, j)
                if j >= T - W_OUT_PIECES:
                    hi_piece(j - (T - W_OUT_PIECES))

            def copy_h_hi(t, i):
                act.wait_ge(h_turned, t + 1)
                act.wait_ge(y_done, t + 1)
                nc.scalar.activation(flat_kn(h_hi[i][:]), psum[i][:, :], ACT.Copy).then_inc(h_hi_ready, 1)

            def exp_y(t, i):
                act.wait_ge(y_done, 2 + t + 1)
                act.wait_ge(x2_ready, t + 1)
                nc.scalar.activation(y_exp[:, i, :], psum[2 + i][:, :], ACT.Relu, scale=-1.0).then_inc(y_low_ready, 1)
                act.wait_ge(y_low_ready, 2 + t + 1)
                nc.scalar.activation(y_exp[:, i, :], y_exp[:, i, :], ACT.Exp, scale=-1.0).then_inc(y_exp_ready, 1)

            def copy_xn2_hi(n, i, column):
                act.wait_ge(xn2_turned, 2 + n + 1)
                nc.scalar.activation(xn2_hi[:, :, bass.ds(column, P)], psum[4 + i][:, :].rearrange("p (k n) -> p k n", k=KD),
                                     ACT.Copy).then_inc(xn2_hi_ready, 1)

            def project_quarter(q):
                with act.Fori(q * TPC // 2, (q + 1) * TPC // 2 - (q == C - 1)) as tp:
                    for i in range(2):
                        t = 2 * tp + i
                        copy_h_hi(t + 1, 1 - i)
                        exp_y(t, i)
                        if q > 0:
                            copy_xn2_hi(t - TPC, i, P * (t - q * TPC))
                if q == C - 1:
                    copy_h_hi(T - 1, 1)
                    for i in range(2):
                        exp_y(T - 2 + i, i)
                        copy_xn2_hi(T - 2 + i - TPC, i, P * (TPC - 2 + i))

            def deviation(q):
                act.wait_ge(var2_ready, q + 1)
                ts = slice(q * TPC, (q + 1) * TPC)
                nc.scalar.activation(std2[:, ts], mean_var2[:, ts, 1], ACT.Sqrt).then_inc(std2_ready, 1)

            def norm_quarter(q):
                for t in range(TPC):
                    copy_xn2_hi(q * TPC + t, t % 2, t * P)
                    if t == 1:
                        copy_a_t(0)

            def z1_pre_quarter(q):
                for k in range(KR):
                    if k == 1:
                        act.wait_ge(u_done, 2 * (q + 1))
                        nc.scalar.activation(u_sb[:, q * TPC:(q + 1) * TPC, :].rearrange("p t e -> p (t e)"),
                                             psum[7][:, 0:TPC * E], ACT.Copy).then_inc(u_ready, 1)
                    act.wait_ge(z1_pre_done, KR * q + k + 1)
                    nc.scalar.activation(z1_pre[:, q, k, :], psum[6][:, :], ACT.Copy).then_inc(z1_pre_ready, 1)

            def ent_root(part, which):
                if which == 0:
                    act.wait_ge(var_ready, part + 1)
                    nc.scalar.activation(col[part]["std"], col[part]["var"], ACT.Sqrt).then_inc(var_std_ready, 1)
                else:
                    act.wait_ge(delta_ready, part + 1)
                    nc.scalar.activation(ent[part]["root"][:], ent[part]["msq"][:], ACT.Sqrt).then_inc(root_ready, 1)

            def copy_a_t(c):
                act.wait_ge(a_turned, c + 1)
                nc.scalar.activation(a_t[:], psum[0][0:3 * E, :], ACT.Copy).then_inc(a_t_ready, 1)

            act.sem_inc(y_low_ready, 2)
            copy_h_hi(0, 0)
            n = W_OUT_PIECES
            for q in range(C):
                if q > 1:
                    z1_pre_quarter(q - 2)
                project_quarter(q)
                deviation(q)
                if q == 2:
                    ent_root(0, 0)
                    ent_root(0, 1)
                for _ in range(2):
                    hi_piece(n)
                    n += 1
            z1_pre_quarter(C - 2)
            hi_piece(n)
            n += 1
            norm_quarter(C - 1)
            z1_pre_quarter(C - 1)
            while n < len(pieces):
                hi_piece(n)
                n += 1

            def chunk(c, first, is_last):
                for o in range(KO):
                    n = KO * c + o
                    act.wait_ge(h_done, n + 1)
                    act.wait_ge(h_split, n + 1)
                    nc.scalar.activation(h_full[o % 2][:], psum[1 + o % 3][:, :], ACT.Gelu).then_inc(h_full_ready, 1)
                    if o in GATE2_AT:
                        k = GATE2_AT[o]
                        act.wait_ge(gate2_done, KR * c + k + 1)
                        if k == 0:
                            act.wait_ge(z2_tmp_ready, ONE + KR * c)
                            if first:
                                act.wait_ge(w_lo_ready, len(pieces))
                        nc.scalar.activation(gate2[:, k, :], psum[0][:, :], ACT.Copy).then_inc(gate2_ready, 1)
                    if o == TURN_A_AT and not is_last:
                        copy_a_t(c + 1)
                    if first and o in ENT_ROOT_AT:
                        ent_root(1, ENT_ROOT_AT.index(o))

            chunk(0, True, False)
            with act.Fori(1, C - 1) as c:
                chunk(c, False, False)
            chunk(C - 1, False, True)

        @block.vector
        def _(dve):
            dve.sem_inc(s12_ready, ONE)
            steps = [0]

            def step(instruction):
                steps[0] += 1
                instruction.then_inc(dve_step, 1)
                dve.wait_ge(dve_step, steps[0])

            for q in range(4):
                dve.wait_ge(x_in[q], 16)
                with dve.Fori(q * TQ, (q + 1) * TQ) as t:
                    nc.vector.bn_stats(stats[:, bass.ds(t, 1), :].rearrange("p a s -> p (a s)"),
                                       x_rows[:, bass.ds(t, 1), :].rearrange("p a s -> p (a s)")).then_inc(dve_step, 1)
            dve.wait_ge(dve_step, T)
            for t in range(T):
                nc.vector.bn_aggr(mean_var[:, t, :], stats[:, t, :]).then_inc(dve_step, 1)
            dve.wait_ge(dve_step, 2 * T)
            steps[0] = 2 * T
            step(nc.vector.tensor_scalar(mean_var[:, :, 1], mean_var[:, :, 1], EPS, None, ALU.add))
            dve.wait_ge(std_ready, 1)
            step(nc.vector.reciprocal(rstd[:], std[:]))

            dve.wait_ge(w_seq_in, 16)
            dve.wait_ge(a_in, 32)
            for s in range(2):
                step(nc.vector.tensor_tensor(
                    wa_prod[:, s].rearrange("p k (h d) -> p (k h) d", d=DH),
                    w_seq_sb[:].rearrange("p k (h d) -> p (k h) d", d=DH),
                    a12[:, s:s + 1, :].to_broadcast([P, KD * H, DH]), ALU.mult))
            for s in range(2):
                nc.vector.tensor_reduce(wa[:, :, s * H:(s + 1) * H], wa_prod[:, s].rearrange("p k (h d) -> p k h d", d=DH),
                                        AX.X, ALU.add).then_inc(wa_ready, 1)

            def norm(t, i):
                nc.vector.tensor_scalar(xn[i][:], x_rows[:, bass.ds(t, 1), :].rearrange("p a s -> p (a s)"),
                                        mean_var[:, bass.ds(t, 1), 0:1].rearrange("p a s -> p (a s)"),
                                        rstd[:, bass.ds(t, 1)], ALU.subtract, ALU.mult).then_inc(xn_ready, 1)

            def evict_scores(t, i):
                dve.wait_ge(proj_done, 2 + t + 1)
                nc.vector.tensor_copy(s12[:, bass.ds(t, 1), :].rearrange("p a s -> p (a s)"), psum[4 + i][:, 0:2 * H])\
                    .then_inc(s12_ready, 1)
                nc.vector.tensor_copy(s1_t[:, bass.ds(P * t, P)], psum[6 + i][0:H, 0:P]).then_inc(s12_ready, 1)

            norm(0, 0)
            norm(1, 1)
            with dve.Fori(0, T // 2 - 1) as tp:
                for i in range(2):
                    dve.wait_ge(xn_turned, 2 * tp + i + 1)
                    norm(2 * tp + i + 2, i)
                    evict_scores(2 * tp + i, i)
            evict_scores(T - 2, 0)
            evict_scores(T - 1, 1)

            dve.wait_ge(s12_ready, ONE + 2 * T)
            s1_all, s2_all = s12[:, :, 0:H], s12[:, :, H:2 * H]
            nc.vector.tensor_reduce(smax[:], s2_all.rearrange("p t h -> p h t"), AX.X, ALU.max).then_inc(smax_ready, 1)
            nc.vector.tensor_scalar(neg_s2[:], s2_all, -1.0, None, ALU.mult).then_inc(shifted_ready, 1)
            dve.wait_ge(guard_ready, 1)
            guard_bc = guard[:].unsqueeze(1).to_broadcast([P, T, H])
            nc.vector.tensor_tensor(shifted[:, 0], s2_all, guard_bc, ALU.subtract).then_inc(shifted_ready, 1)
            step(nc.vector.tensor_tensor(shifted[:, 1], s1_all, guard_bc, ALU.add))
            step(nc.vector.tensor_scalar(shifted[:, 2], shifted[:, 1], 0.0, None, ALU.min))
            nc.vector.tensor_scalar(shifted[:, 1], shifted[:, 1], 0.0, None, ALU.max).then_inc(shifted_ready, 1)

            SETUP_STEPS = steps[0]
            SPLIT_AT = 11
            SPLIT, SCALE = 3, 3

            def split_values(h, i, base):
                v = vals[i][:].rearrange("p t s a d -> p (t s) a d")
                w = weighted[:].rearrange("p t s d -> p (t s) d")
                r = residue[:].rearrange("p t s d -> p (t s) d")
                dve.wait_ge(weighted_ready, 2 * (h + 1))
                nc.vector.tensor_copy(v[:, :, 0, :], w).then_inc(dve_step, 1)
                dve.wait_ge(dve_step, base + 1)
                nc.vector.tensor_tensor(r, w, v[:, :, 0, :], ALU.subtract).then_inc(dve_step, 1)
                dve.wait_ge(dve_step, base + 2)
                nc.vector.tensor_copy(v[:, :, 1, :], r).then_inc(dve_step, 1)
                dve.wait_ge(dve_step, base + 3)
                nc.vector.tensor_tensor(v[:, :, 2, :], r, v[:, :, 1, :], ALU.subtract).then_inc(vals_ready, 1)

            def cut(h, i, j):
                if j % GROUP == 0:
                    dve.wait_ge(bank_passed, BANKS * (NG * h + j // GROUP + 1))
                m, g = masks[j % RING], signs[:, j % SIGNS, :]
                if j in SIGN_ON_DVE:
                    dve.wait_ge(neg_cut, T * h + j + 1)
                    nc.vector.tensor_scalar(g, s1_bc[i][:], neg_s2[:, j, bass.ds(h, 1)], EDGE, ALU.is_lt, ALU.mult)\
                        .then_inc(signs_dve, 1)
                    dve.wait_ge(signs_dve, N_DVE * h + up_to(SIGN_ON_DVE, j))
                else:
                    dve.wait_ge(signs_act, N_ACT * h + up_to(act_tiles, j))
                nc.vector.tensor_tensor(m[:, 0, :].bitcast(I32), edges[:, j, :].bitcast(I32), g.bitcast(I32),
                                        ALU.bitwise_and).then_inc(neg_cut, 1)
                if j not in POS_ON_POOL:
                    dve.wait_ge(neg_cut, SIGNS + T * h + j + 1)
                    nc.vector.tensor_tensor(m[:, 1, :].bitcast(I32), edges[:, j, :].bitcast(I32), m[:, 0, :].bitcast(I32),
                                            ALU.bitwise_xor).then_inc(pos_dve, 1)

            def empty_banks(h, base):
                dve.wait_ge(head_done, ONE + h)
                for b in range(BANKS):
                    dve.wait_ge(bank_passed, BANKS * (GROUPS_FREE + NG * h + NG - 1) + b + 1)
                    nc.vector.tensor_reduce(
                        sums[:, b * Q_PER_BANK:(b + 1) * Q_PER_BANK].rearrange("p q s d -> p (q s) d"),
                        psum[b][:, 0:2 * Q_PER_BANK * SIDE].rearrange("p (g a d) -> p g d a", a=PART, d=DV),
                        AX.X, ALU.add).then_inc(bank_free, 1)
                dve.wait_ge(bank_free, BANKS * (h + 2))
                rs = row_scale[:, :, bass.ds(h, 1), :].rearrange("p t a s -> p t (a s)")
                nc.vector.tensor_tensor(den2[:], sums[:, :, :, DH], rs, ALU.mult).then_inc(dve_step, 1)
                dve.wait_ge(dve_step, base + 1)
                nc.vector.tensor_reduce(den[:], den2[:], AX.X, ALU.add).then_inc(dve_step, 1)
                dve.wait_ge(dve_step, base + 2)
                nc.vector.reciprocal(rden[:], den[:]).then_inc(dve_step, 1)
                dve.wait_ge(dve_step, base + 3)
                nc.vector.tensor_tensor(scale_n[:], rs, rden[:].unsqueeze(2).to_broadcast([P, T, 2]), ALU.mult)\
                    .then_inc(scale_ready, 1)

            def wait_s1(hp, i):
                dve.wait_ge(s1_in[i], 16 * hp + 16)

            dve.sem_inc(neg_cut, SIGNS)
            dve.sem_inc(bank_free, BANKS)
            dve.wait_ge(weights_ready, 4)
            dve.wait_ge(seq_ready, ONE + T)
            dve.wait_ge(edges_ready, T)
            wait_s1(0, 0)
            split_values(0, 0, SETUP_STEPS)
            for j in range(AHEAD):
                cut(0, 0, j)

            def head(h, hp_next, i, is_last):
                for j in range(AHEAD, T):
                    cut(h, i, j)
                    if j == SPLIT_AT and not is_last:
                        split_next(h, i)
                if not is_last:
                    wait_s1(hp_next, 1 - i)
                    for j in range(AHEAD):
                        cut(h + 1, 1 - i, j)
                empty_banks(h, SETUP_STEPS + SPLIT + (SPLIT + SCALE) * h + (0 if is_last else SPLIT))

            def split_next(h, i):
                dve.wait_ge(bank_passed, BANKS * (NG * h + GROUPS_FREE))
                split_values(h + 1, 1 - i, SETUP_STEPS + SPLIT + (SPLIT + SCALE) * h)
            with dve.Fori(0, H // 2 - 1) as hp:
                for i in range(2):
                    head(2 * hp + i, hp + i, i, False)
            head(H - 2, H // 2 - 1, 0, False)
            head(H - 1, 0, 1, True)
            dve.wait_ge(scale_ready, H)
            nc.vector.tensor_tensor(scaled[:], sums[:, :, :, 0:DH], scale_n[:].unsqueeze(3).to_broadcast([P, T, 2, DH]),
                                    ALU.mult).then_inc(scaled_ready, 1)
            dve.wait_ge(scaled_ready, H)
            nc.vector.tensor_tensor(hidden[:, :, DH * (H - 1):DH * H], scaled[:, :, 0, :], scaled[:, :, 1, :], ALU.add)\
                .then_inc(head_done, 1)

            dve.wait_ge(head_done, ONE + H)
            nc.vector.memset(ones[:].bitcast(F32), 1.0).then_inc(small_ready, 1)

            def small_parts():
                dve.wait_ge(small_in, SMALL_LOADS)
                nc.vector.tensor_copy(c_hl[:], c_raw[:]).then_inc(small_ready, 1)
                dve.wait_ge(small_ready, 2)
                nc.vector.tensor_tensor(c_hl[2 * E:3 * E], c_raw[2 * E:3 * E], c_hl[2 * E:3 * E].bitcast(F32), ALU.subtract)\
                    .then_inc(small_ready, 1)

            def cut_h_lo(t, i):
                dve.wait_ge(h_hi_ready, t + 1)
                nc.vector.tensor_tensor(flat_kn(h_lo[i][:]), psum[i][:, :], flat_kn(h_hi[i][:]).bitcast(F32), ALU.subtract)\
                    .then_inc(h_lo_ready, 1)

            def add_x(t, i):
                row = x2[:, bass.ds(t, 1), :].rearrange("p a s -> p (a s)")
                dve.wait_ge(y_low_ready, 2 + t + 1)
                dve.wait_ge(x2_ready, t + 1)
                nc.vector.scalar_tensor_tensor(out=x_plus[:, i, :], in0=psum[2 + i][:, :], scalar=0.0, in1=row,
                                               op0=ALU.max, op1=ALU.add).then_inc(x_plus_ready, 1)
                dve.wait_ge(y_exp_ready, t + 1)
                dve.wait_ge(x_plus_ready, 2 + t + 1)
                nc.vector.scalar_tensor_tensor(out=row, in0=y_exp[:, i, :], scalar=-1.0, in1=x_plus[:, i, :],
                                               op0=ALU.add, op1=ALU.add).then_inc(x2_ready, 1)
                dve.wait_ge(x2_ready, 2 + t + 1)
                nc.vector.bn_stats(stats2[:, bass.ds(t, 1), :].rearrange("p a s -> p (a s)"), row).then_inc(stats2_ready, 1)

            def norm(n, i):
                dve.wait_ge(xn2_turned, n + 1)
                nc.vector.tensor_scalar(xn2[i][:], x2[:, bass.ds(n, 1), :].rearrange("p a s -> p (a s)"),
                                        mean_var2[:, bass.ds(n, 1), 0:1].rearrange("p a s -> p (a s)"),
                                        rstd2[:, bass.ds(n, 1)], ALU.subtract, ALU.mult).then_inc(xn2_ready, 1)

            def cut_xn2_lo(n, i, column):
                dve.wait_ge(xn2_hi_ready, n + 1)
                nc.vector.tensor_tensor(
                    xn2_lo[:, :, bass.ds(column, P)], psum[4 + i][:, :].rearrange("p (k n) -> p k n", k=KD),
                    xn2_hi[:, :, bass.ds(column, P)].bitcast(F32), ALU.subtract)\
                    .then_inc(xn2_lo_ready, 1)

            def project_quarter(q):
                dve.wait_ge(x2_in[q], 16)
                with dve.Fori(q * TPC // 2, (q + 1) * TPC // 2 - (q == C - 1)) as tp:
                    for i in range(2):
                        t = 2 * tp + i
                        if q > 0:
                            norm(t - TPC, i)
                        cut_h_lo(t + 1, 1 - i)
                        add_x(t, i)
                        if q > 0:
                            cut_xn2_lo(t - TPC, i, P * (t - q * TPC))
                if q == C - 1:
                    cut_h_lo(T - 1, 1)
                    for i in range(2):
                        norm(T - 2 + i - TPC, i)
                        add_x(T - 2 + i, i)
                        cut_xn2_lo(T - 2 + i - TPC, i, P * (TPC - 2 + i))

            def moments(q):
                dve.wait_ge(stats2_ready, (q + 1) * TPC)
                for t in range(q * TPC, (q + 1) * TPC):
                    nc.vector.bn_aggr(mean_var2[:, t, :], stats2[:, t, :]).then_inc(mean_var2_ready, 1)
                dve.wait_ge(mean_var2_ready, (q + 1) * TPC)
                ts = slice(q * TPC, (q + 1) * TPC)
                nc.vector.tensor_scalar(mean_var2[:, ts, 1], mean_var2[:, ts, 1], EPS, None, ALU.add).then_inc(var2_ready, 1)
                dve.wait_ge(std2_ready, q + 1)
                nc.vector.reciprocal(rstd2[:, ts], std2[:, ts]).then_inc(rstd2_ready, 1)
                dve.wait_ge(rstd2_ready, q + 1)

            ent_steps = [0]

            def step(instruction):
                ent_steps[0] += 1
                instruction.then_inc(ent_step, 1)
                dve.wait_ge(ent_step, ent_steps[0])

            def over_e(a):
                return a.unsqueeze(2).to_broadcast([P, a.shape[1], E])

            def over_t(a, part):
                return a.unsqueeze(1).to_broadcast([P, len(ENT_TILES[part]), E])

            def views(part):
                e = {n: v[:] for n, v in ent[part].items()}
                return e, {n: v.rearrange("p t e -> p (t e)") for n, v in e.items()}, col[part]

            def ent_constants():
                dve.wait_ge(k_ready, 1)
                step(nc.vector.tensor_copy(k_row[:], k_int[:]))
                step(nc.vector.memset(keep[:], 1.0))
                step(nc.vector.reciprocal(inv_k[:], k_row[:]))
                step(nc.vector.memset(keep[:, :, 0:1], 0.0))

            def ent_norm(part):
                e, _, col = views(part)
                dve.wait_ge(u_ready, (1, C)[part])
                u = u_sb[:, ENT_TILES[part][0]:ENT_TILES[part][-1] + 1, :]
                step(nc.vector.tensor_reduce(col["sum"], u, AX.X, ALU.add))
                step(nc.vector.tensor_scalar(col["mean"], col["sum"], 1.0 / E, None, ALU.mult))
                step(nc.vector.tensor_tensor(e["z"], u, over_e(col["mean"]), ALU.subtract))
                step(nc.vector.tensor_tensor(e["sq"], e["z"], e["z"], ALU.mult))
                step(nc.vector.tensor_reduce(col["sum"], e["sq"], AX.X, ALU.add))
                nc.vector.tensor_scalar(col["var"], col["sum"], 1.0 / E, EPS, ALU.mult, ALU.add).then_inc(var_ready, 1)

            def ent_sort(part):
                e, _, col = views(part)
                dve.wait_ge(var_std_ready, part + 1)
                step(nc.vector.reciprocal(col["rstd"], col["std"]))
                step(nc.vector.tensor_tensor(e["z"], e["z"], over_e(col["rstd"]), ALU.mult))
                step(nc.vector.tensor_scalar(e["z"], e["z"], 0.5, None, ALU.mult))
                step(nc.vector.tensor_reduce(col["max"], e["z"], AX.X, ALU.max))
                step(nc.vector.tensor_tensor(e["z"], e["z"], over_e(col["max"]), ALU.subtract))
                for t in range(len(ENT_TILES[part])):
                    i = nc.vector.max(e["sorted"][:, t, 0:8], e["z"][:, t, :])
                step(i)
                for t in range(len(ENT_TILES[part])):
                    i = nc.vector.match_replace(e["rest"][:, t, :], e["sorted"][:, t, 0:8], e["z"][:, t, :], -1e30)
                step(i)
                for t in range(len(ENT_TILES[part])):
                    i = nc.vector.max(e["sorted"][:, t, 8:16], e["rest"][:, t, :])
                step(i)

            def ent_delta(part):
                e, flat, col = views(part)
                step(nc.vector.tensor_tensor(e["sorted2"], e["sorted"], e["sorted"], ALU.mult))
                kf = keep[:, 0:len(ENT_TILES[part])].rearrange("p t e -> p (t e)")
                step(nc.vector.tensor_tensor_scan(flat["cum"], kf, flat["sorted"], 0.0, ALU.mult, ALU.add))
                step(nc.vector.tensor_tensor_scan(flat["cum2"], kf, flat["sorted2"], 0.0, ALU.mult, ALU.add))
                step(nc.vector.tensor_tensor(e["mean"], e["cum"], over_t(inv_k[:], part), ALU.mult))
                step(nc.vector.tensor_tensor(e["msq"], e["cum2"], over_t(inv_k[:], part), ALU.mult))
                step(nc.vector.tensor_tensor(e["cum"], e["mean"], e["mean"], ALU.mult))
                step(nc.vector.tensor_tensor(e["msq"], e["msq"], e["cum"], ALU.subtract))
                step(nc.vector.tensor_tensor(e["msq"], over_t(inv_k[:], part), e["msq"], ALU.subtract))
                nc.vector.tensor_scalar(e["msq"], e["msq"], 0.0, None, ALU.max).then_inc(delta_ready, 1)

            def ent_values(part):
                e, _, col = views(part)
                dve.wait_ge(root_ready, part + 1)
                step(nc.vector.tensor_tensor(e["tau"], e["mean"], e["root"], ALU.subtract))
                step(nc.vector.tensor_tensor(e["sq"], e["tau"], e["sorted"], ALU.is_le))
                step(nc.vector.tensor_reduce(col["support"], e["sq"], AX.X, ALU.add))
                step(nc.vector.tensor_tensor(e["pick"], over_t(k_row[:], part), over_e(col["support"]), ALU.is_equal))
                step(nc.vector.tensor_tensor(e["pick"], e["pick"], e["tau"], ALU.mult))
                step(nc.vector.tensor_reduce(col["tau"], e["pick"], AX.X, ALU.add))
                step(nc.vector.tensor_tensor(e["z"], e["z"], over_e(col["tau"]), ALU.subtract))
                step(nc.vector.tensor_scalar(e["z"], e["z"], 0.0, None, ALU.max))
                step(nc.vector.tensor_tensor(e["a"], e["z"], e["z"], ALU.mult))
                a = a_all[:, ENT_TILES[part][0]:ENT_TILES[part][-1] + 1, :]
                step(nc.vector.tensor_copy(a[:, :, 0:E], e["a"]))
                step(nc.vector.tensor_copy(a[:, :, 2 * E:3 * E], e["a"]))
                nc.vector.tensor_tensor(a[:, :, E:2 * E], e["a"], a[:, :, 0:E].bitcast(F32), ALU.subtract).then_inc(a_ready, 1)

            dve.sem_inc(x_plus_ready, 2)
            dve.sem_inc(x2_ready, 2)
            cut_h_lo(0, 0)
            for q in range(C):
                project_quarter(q)
                moments(q)
                if q == 1:
                    small_parts()
                    ent_constants()
                if q == 2:
                    ent_norm(0)
                    ent_sort(0)
                    ent_delta(0)
                    ent_values(0)
            last = (C - 1) * TPC
            norm(last, 0)
            for t in range(TPC):
                if t + 1 < TPC:
                    norm(last + t + 1, (t + 1) % 2)
                cut_xn2_lo(last + t, t % 2, t * P)

            def start_z1(c, k):
                dve.wait_ge(gate1_done, KR * c + k + 1)
                nc.vector.scalar_tensor_tensor(out=z_tmp[:, k, :], in0=z1_pre[:, bass.ds(c, 1), k, :].rearrange("p a n -> p (a n)"),
                                               scalar=bias1[:, k:k + 1], in1=psum[0][:, :],
                                               op0=ALU.add, op1=ALU.mult).then_inc(z1_tmp_ready, 1)

            def split_z1(c):
                hi, lo = z1_parts(c)
                dve.wait_ge(z1_tmp_ready, KR * (c + 1))
                nc.vector.tensor_copy(hi, z_tmp[:].rearrange("p k n -> p (k n)")).then_inc(z1_hi_ready, 1)
                dve.wait_ge(z1_hi_ready, c + 1)
                nc.vector.tensor_tensor(lo, z_tmp[:].rearrange("p k n -> p (k n)"), hi.bitcast(F32), ALU.subtract).then_inc(z1_ready, 1)

            def start_z2(c):
                dve.wait_ge(gate2_ready, ONE + KR * (c + 1))
                dve.wait_ge(h_used, HR + KO * (c + 1))
                for k in range(KR):
                    nc.vector.scalar_tensor_tensor(out=z_tmp[:, k, :], in0=psum[4 + k][:, :], scalar=bias2[:, k:k + 1],
                                                   in1=gate2[:, k, :], op0=ALU.add, op1=ALU.mult).then_inc(z2_tmp_ready, 1)

            def split_z2(c):
                dve.wait_ge(z2_tmp_ready, ONE + KR * (c + 1))
                dve.wait_ge(o_done, ONE + TPC * c)
                nc.vector.tensor_copy(z2_hi[:], z_tmp[:]).then_inc(z2_hi_ready, 1)
                dve.wait_ge(z2_hi_ready, c + 1)
                nc.vector.tensor_tensor(z2_lo[:], z_tmp[:], z2_hi[:].bitcast(F32), ALU.subtract).then_inc(z2_ready, 1)

            def rows_out(c, t):
                n = TPC * c + t
                dve.wait_ge(o_done, ONE + n + 1)
                dve.wait_ge(out_saved[t % 2], 16 + 16 * ((TPC // 2) * c + t // 2))
                nc.vector.tensor_tensor(out_rows[:, t % 2, :], psum[6 + t % 2][:, :],
                                        x2[:, bass.ds(n, 1), :].rearrange("p a s -> p (a s)"), ALU.add).then_inc(o_ready, 1)

            def split_h(c, o):
                n = KO * c + o
                dve.wait_ge(h_full_ready, ONE + n + 1)
                dve.wait_ge(h_used, n + 1)
                nc.vector.tensor_copy(hr_hi[o % HR][:], h_full[o % 2][:]).then_inc(h_hi_cut, 1)
                dve.wait_ge(h_hi_cut, n + 1)
                nc.vector.tensor_tensor(hr_lo[o % HR][:], h_full[o % 2][:], hr_hi[o % HR][:].bitcast(F32), ALU.subtract)\
                    .then_inc(h_split, 1)

            def chunk(c, first, is_last):
                if not first:
                    dve.wait_ge(z1_ready, c + 1)
                    start_z2(c - 1)
                for o in range(KO):
                    split_h(c, o)
                    if o == 0 and not first:
                        split_z2(c - 1)
                    if o in FINAL_AT and not first:
                        rows_out(c - 1, FINAL_AT[o])
                    if first and o in ENT_AT:
                        (ent_norm, ent_sort, ent_delta, ent_values)[ENT_AT.index(o)](1)
                    if o in GATE1_AT and not is_last:
                        k = GATE1_AT[o]
                        if k == 0:
                            dve.wait_ge(z1_ready, c + 1)
                            if not first:
                                dve.wait_ge(z2_ready, c)
                        start_z1(c + 1, k)
                        if k == KR - 1:
                            split_z1(c + 1)

            dve.sem_inc(h_split, 2)
            dve.sem_inc(z2_tmp_ready, ONE)
            dve.sem_inc(o_ready, ONE)
            for k in range(KR):
                start_z1(0, k)
            dve.wait_ge(z1_pre_done, KR * C)
            split_z1(0)
            chunk(0, True, False)
            dve.wait_ge(w_lo_ready, len(pieces))
            with dve.Fori(1, C - 1) as c:
                chunk(c, False, False)
            chunk(C - 1, False, True)
            start_z2(C - 1)
            split_z2(C - 1)
            for t in range(TPC):
                rows_out(C - 1, t)

        @block.tensor
        def _(pe):
            mm = nc.tensor.matmul

            def turn_xn(t, i):
                pe.wait_ge(xn_ready, t + 1)
                for k in range(KD):
                    m = nc.tensor.transpose(psum[i][:, k * P:(k + 1) * P], xn[i][:, k * P:(k + 1) * P], ident[:])
                m.then_inc(xn_turned, 1)

            def project(t, i):
                pe.wait_ge(xn_t_ready, t + 1)
                for k in range(KD):
                    mm(psum[2 + i][:, :], xn_t[i][:, k, :], w_seq_sb[:, k, :], start=(k == 0), stop=(k == KD - 1))
                for k in range(KD):
                    mm(psum[4 + i][:, 0:2 * H], xn_t[i][:, k, :], wa[:, k, :], start=(k == 0), stop=(k == KD - 1))
                for k in range(KD):
                    m = mm(psum[6 + i][0:H, 0:P], wa[:, k, 0:H], xn_t[i][:, k, :], start=(k == 0), stop=(k == KD - 1))
                m.then_inc(proj_done, 1)

            pe.sem_inc(proj_done, 2)
            pe.wait_ge(ident_ready, 2)
            pe.wait_ge(w_seq_in, 16)
            turn_xn(0, 0)
            turn_xn(1, 1)
            pe.wait_ge(wa_ready, 2)
            project(0, 0)
            with pe.Fori(0, T // 2 - 1) as tp:
                for i in range(2):
                    pe.wait_ge(xn_t_ready, 2 * tp + i + 1)
                    turn_xn(2 * tp + i + 2, i)
                    pe.wait_ge(seq_ready, ONE + 2 * tp + i)
                    pe.wait_ge(s12_ready, ONE + 2 * (2 * tp + i))
                    project(2 * tp + i + 1, 1 - i)
            pe.wait_ge(seq_ready, ONE + T - 2)
            pe.wait_ge(s12_ready, ONE + 2 * (T - 2))
            project(T - 1, 1)

            def group(h, i, g):
                js = range(g * GROUP, (g + 1) * GROUP)
                if g == 0:
                    pe.wait_ge(vals_ready, h + 1)
                pe.wait_ge(neg_cut, SIGNS + T * h + js[-1] + 1)
                if up_to(pos_dve_tiles, js[-1]):
                    pe.wait_ge(pos_dve, N_PDVE * h + up_to(pos_dve_tiles, js[-1]))
                if up_to(POS_ON_POOL, js[-1]):
                    pe.wait_ge(pos_pool, N_POOL * h + up_to(POS_ON_POOL, js[-1]))
                for b in range(BANKS):
                    if g == 0:
                        pe.wait_ge(bank_free, BANKS * h + b + 1)
                    if g == 0 or b == 0:
                        pe.sem_inc(pe_passed_waits)
                    for j in js:
                        for q in range(Q_PER_BANK):
                            for s in range(2):
                                at = (q * 2 + s) * SIDE
                                n = b * Q_PER_BANK + q
                                m = mm(psum[b][:, at:at + SIDE], masks[j % RING][:, s, n * P:(n + 1) * P].bitcast(F8),
                                       vals[i][:, j, s].rearrange("p a d -> p (a d)"),
                                       start=(j == 0 and q == 0 and s == 0), stop=(j == T - 1), skip_group_check=True)
                    m.then_inc(bank_passed, 1)

            pe.sem_inc(bank_passed, GROUPS_FREE * BANKS)
            pe.wait_ge(seq_ready, ONE + T)
            with pe.Fori(0, H // 2) as hp:
                for i in range(2):
                    for g in range(NG):
                        group(2 * hp + i, i, g)

            HI_LO = ((0, 0), (1, 0), (0, 1))

            def turn_h(t, i, saved):
                pe.wait_ge(hq_in[i], saved)
                pe.wait_ge(h_lo_ready, t + 1)
                for k in range(KD):
                    m = nc.tensor.transpose(psum[i][:, k * P:(k + 1) * P], hq[i][:, k * P:(k + 1) * P], ident[:])
                m.then_inc(h_turned, 1)

            def out_project(t, i):
                pe.wait_ge(h_lo_ready, 2 + t + 1)
                pe.wait_ge(x_plus_ready, t + 1)
                left, right = (h_hi[i], h_lo[i]), (w_out_hi, w_out_lo)
                for k in range(KD):
                    for l, r in HI_LO:
                        mm(psum[2 + i][:, :], left[l][:, k, :], right[r][:, k, :], start=(k == 0 and l == r), stop=False)
                mm(psum[2 + i][:, :], ones[:], b_hi[:], start=False, stop=False)
                mm(psum[2 + i][:, :], ones[:], b_lo[:], start=False, stop=True).then_inc(y_done, 1)

            def turn_xn2(n, i):
                pe.wait_ge(xn2_ready, n + 1)
                pe.wait_ge(xn2_lo_ready, n + 1)
                for k in range(KD):
                    m = nc.tensor.transpose(psum[4 + i][:, k * P:(k + 1) * P], xn2[i][:, k * P:(k + 1) * P], ident[:])
                m.then_inc(xn2_turned, 1)

            def project_quarter(q):
                with pe.Fori(q * TPC // 2, (q + 1) * TPC // 2 - (q == C - 1)) as tp:
                    for i in range(2):
                        t = 2 * tp + i
                        turn_h(t + 1, 1 - i, 16 * (tp + i) + 16)
                        out_project(t, i)
                        if q > 0:
                            turn_xn2(t - TPC, i)
                if q == C - 1:
                    turn_h(T - 1, 1, 16 * (T // 2))
                    for i in range(2):
                        out_project(T - 2 + i, i)
                        turn_xn2(T - 2 + i - TPC, i)

            def z1_pre_part(q, r):
                left, right = (win1_hi, win1_lo), (xn2_hi, xn2_lo)
                if KR * q + r > 0:
                    pe.wait_ge(z1_pre_ready, KR * q + r)
                for k in range(KD):
                    for l, s in HI_LO:
                        rhs = (xn2_hi, xn2_lo)[s][:, k, :]
                        m = mm(psum[6][:, :], left[l][:, k, r * P:(r + 1) * P], rhs, start=(k == 0 and l == s),
                               stop=(k == KD - 1 and s == 1))
                m.then_inc(z1_pre_done, 1)

            def scores(q, tiles):
                for t in tiles:
                    pe.wait_ge(xn2_lo_ready, 2 + q * TPC + t + 1)
                    column = slice(t * P, (t + 1) * P)
                    for k in range(KD):
                        mm(psum[7][:, t * E:(t + 1) * E], xn2_hi[:, k, column].bitcast(F32), proj_sb[:, k, :],
                           start=(k == 0), stop=False)
                        m = mm(psum[7][:, t * E:(t + 1) * E], xn2_lo[:, k, column].bitcast(F32), proj_sb[:, k, :],
                               start=False, stop=(k == KD - 1))
                m.then_inc(u_done, 1)

            def turn_a(c):
                pe.wait_ge(a_col_ready, c + 1)
                pe.sem_inc(pe_passed_waits)
                for t in range(TPC):
                    m = nc.tensor.transpose(psum[0][0:3 * E, t * P:(t + 1) * P], a_col[:, t, :], ident[:])
                m.then_inc(a_turned, 1)

            def gate(which, r, done):
                mm(psum[0][:, :], c_hl[:, which, r * P:(r + 1) * P], a_t[:], start=True, stop=True).then_inc(done, 1)

            def gate1(c, r):
                if r == 0:
                    pe.wait_ge(a_t_ready, c + 1)
                else:
                    pe.wait_ge(z1_tmp_ready, KR * c + r)
                gate(0, r, gate1_done)

            def first_factor(q):
                pe.wait_ge(w_lo_ready, WIN1_PIECES)
                if q == 0:
                    pe.wait_ge(small_in, SMALL_LOADS)
                else:
                    pe.wait_ge(u_ready, q)
                scores(q, range(TPC - 1))
                if q == C - 1:
                    gate1(0, 0)
                pe.wait_ge(xn2_lo_ready, 2 + (q + 1) * TPC)
                z1_pre_part(q, 0)
                if q == C - 1:
                    gate1(0, 1)
                scores(q, [TPC - 1])
                z1_pre_part(q, 1)

            pe.sem_inc(h_lo_ready, 2)
            pe.sem_inc(y_done, 2)
            pe.sem_inc(xn2_turned, 2)
            pe.sem_inc(xn2_lo_ready, 2)
            pe.wait_ge(bank_free, BANKS * (H + 1))
            turn_h(0, 0, 16)
            pe.wait_ge(w_lo_ready, W_OUT_PIECES)
            pe.wait_ge(small_ready, 1)
            for q in range(C):
                project_quarter(q)
                if q > 0:
                    first_factor(q - 1)
            for t in range(TPC):
                turn_xn2((C - 1) * TPC + t, t % 2)
                if t == 1:
                    turn_a(0)
            pe.wait_ge(small_ready, 3)
            first_factor(C - 1)

            def final(c, t):
                pe.wait_ge(z2_ready, c + 1)
                pe.wait_ge(o_ready, ONE + TPC * c + max(t - 1, 0))
                left, right = (z2_hi, z2_lo), (wout2_hi, wout2_lo)
                for k in range(KR):
                    for l, s in HI_LO:
                        m = mm(psum[6 + t % 2][:, :], left[l][:, k, t * P:(t + 1) * P], right[s][:, k, :],
                               start=(k == 0 and l == s), stop=(k == KR - 1 and s == 1))
                m.then_inc(o_done, 1)

            def chunk(c, first, is_last):
                z1 = [part.rearrange("p (k n) -> p k n", k=KR) for part in z1_parts(c)]

                def up(o):
                    if o == 0:
                        pe.wait_ge(z1_ready, c + 1)
                    pe.wait_ge(h_full_ready, ONE + KO * c + max(o - 2, 0))
                    if first and o % (PIECE // P) == 0:
                        pe.wait_ge(w_lo_ready, WIN1_PIECES + KR * (o // (PIECE // P) + 1))
                    pe.sem_inc(pe_passed_waits)
                    left = (wout1_hi, wout1_lo)
                    for k in range(KR):
                        for l, s in HI_LO:
                            m = mm(psum[1 + o % 3][:, :], left[l][:, k, o * P:(o + 1) * P], z1[s][:, k, :],
                                   start=(k == 0 and l == s), stop=(k == KR - 1 and s == 1))
                    m.then_inc(h_done, 1)

                def down(o):
                    pe.wait_ge(h_split, 2 + KO * c + o + 1)
                    if o == 0:
                        pe.wait_ge(z2_tmp_ready, ONE + KR * c)
                    if first and o % (PIECE // R) == 0:
                        pe.wait_ge(w_lo_ready, WOUT1_PIECES + o // (PIECE // R) + 1)
                    left, right = (win2_hi, win2_lo), (hr_hi[o % HR], hr_lo[o % HR])
                    for r in range(KR):
                        for l, s in HI_LO:
                            m = mm(psum[4 + r][:, :], left[l][:, o, r * P:(r + 1) * P], right[s][:],
                                   start=(o == 0 and l == s), stop=(o == KO - 1 and s == 1))
                    m.then_inc(h_used, 1)

                up(0)
                up(1)
                for o in range(2, KO):
                    up(o)
                    down(o - 2)
                    if o in FINAL_AT and not first:
                        final(c - 1, FINAL_AT[o])
                    if o in GATE2_AT:
                        k = GATE2_AT[o]
                        if k == 0:
                            pe.wait_ge(z1_tmp_ready, KR * (c + 1))
                        else:
                            pe.wait_ge(gate2_ready, ONE + KR * c + k)
                        gate(1, k, gate2_done)
                    if o == TURN_A_AT and not is_last:
                        pe.wait_ge(gate2_ready, ONE + KR * (c + 1))
                        turn_a(c + 1)
                    if o in GATE1_AT and not is_last:
                        gate1(c + 1, GATE1_AT[o])
                down(KO - 2)
                down(KO - 1)

            pe.sem_inc(h_used, HR)
            pe.sem_inc(o_done, ONE)
            chunk(0, True, False)
            pe.wait_ge(w_lo_ready, len(pieces))
            with pe.Fori(1, C - 1) as c:
                chunk(c, False, False)
            chunk(C - 1, False, True)
            for t in range(TPC):
                final(C - 1, t)


_INS = ['x', 'adj', 'L0_gnn_W_seq', 'L0_gnn_a1', 'L0_gnn_a2', 'L0_gnn_W_out', 'L0_gnn_b_out', 'L0_ffn_proj', 'L0_ffn_C1',
        'L0_ffn_Win1', 'L0_ffn_Wout1', 'L0_ffn_C2', 'L0_ffn_Win2', 'L0_ffn_Wout2']
_TRANSPOSED = ('adj', 'L0_ffn_Wout1', 'L0_ffn_Wout2')


def kernel(**inputs):
    import numpy as _np
    import concourse.bacc as _bacc
    from concourse import mybir as _mybir
    from concourse.bass_utils import run_bass_kernel_spmd as _run

    nc = _bacc.Bacc("TRN2", target_bir_lowering=False, num_devices=1)
    arrays, args = {}, []
    for name in _INS:
        a = _np.asarray(inputs[name])
        a = _np.ascontiguousarray(a.T if name in _TRANSPOSED else a)
        arrays[f"in_{name}_dram"] = a
        args.append(nc.dram_tensor(f"in_{name}_dram", a.shape, _mybir.dt.from_np(a.dtype), kind="ExternalInput").ap())
    n, d = inputs['x'].shape
    args.append(nc.dram_tensor("out_0_dram", (n, d), _mybir.dt.float32, kind="ExternalOutput").ap())
    gat_ffn(nc, *args)
    r = _run(nc, [arrays], core_ids=[0])
    return r.results[0]["out_0_dram"]
```

```python
from contextlib import ExitStack

import concourse.bass as bass
from concourse import mybir

F32 = mybir.dt.float32
F32R = mybir.dt.float32r
BF16 = mybir.dt.bfloat16
F8 = mybir.dt.float8e4
I8 = mybir.dt.int8
I32 = mybir.dt.int32
ALU = mybir.AluOpType
ACT = mybir.ActivationFunctionType
AX = mybir.AxisListType
P = 128


def gat_ffn(nc, x, adj_t, w_seq, a1, a2, w_out, b_out, proj, c1, win1, wout1_t, c2, win2, wout2_t, out):
    N, D = x.shape
    DH = a1.shape[0]
    H = D // DH
    T = N // P
    KD = D // P
    E, R = c1.shape
    KR = R // P
    O = win2.shape[0] - 1
    KO = O // P
    C = 4
    CT = N // C
    EPS = 1e-5
    EDGE = 8.0

    DV = DH + 1
    PART = 3
    SIDE = PART * DV
    GROUP = 2
    AHEAD = 6
    NG = T // GROUP
    RING = 8
    GROUPS_FREE = RING // GROUP
    SIGNS = 8
    BANKS = 8
    Q_PER_BANK = T // BANKS

    SIGN_ON_DVE = (1, 10)
    POS_ON_POOL = (0, 2, 3, 5, 9, 11, 13, 14, 15)
    act_tiles = [j for j in range(T) if j not in SIGN_ON_DVE]
    pos_dve_tiles = [j for j in range(T) if j not in POS_ON_POOL]
    N_ACT, N_DVE = len(act_tiles), len(SIGN_ON_DVE)
    N_POOL, N_PDVE = len(POS_ON_POOL), len(pos_dve_tiles)

    def up_to(tiles, j):
        return sum(k <= j for k in tiles)

    s1_dram = nc.dram_tensor("s1_rows", [H, N], F32, kind="Internal").ap()

    with ExitStack() as ctx:
        def sem(name):
            return ctx.enter_context(nc.semaphore(name))

        psum = [ctx.enter_context(nc.psum_tensor(f"bank{b}", [P, 512], F32)) for b in range(BANKS)]

        SBUF_FIRST, SBUF_END = 16512, 229344
        size_of = {F32: 4, F32R: 4, BF16: 2, I8: 1, I32: 4}
        at = [SBUF_FIRST]

        def place(name, shape, dt=F32, over=None):
            size = size_of[dt]
            for n in shape[1:]:
                size *= n
            size = -(-size // 32) * 32
            offset = at[0] if over is None else over
            if over is None:
                at[0] += size
            assert offset + size <= SBUF_END, (name, offset + size - SBUF_END)
            return nc.alloc_sbuf_tensor_at(name, shape, dt, offset=offset)

        ident = place("ident", [P, P])
        ROWS_AT = at[0]
        rows = place("rows", [P, T, D])
        x_rows = rows
        hidden = rows

        SEQ_AT = at[0]
        seq = place("seq", [P, T, D])
        EDGES_AT = at[0]
        edges = place("edges", [P, T, N], I8)
        weight = place("weight", [P, T, H, 2])
        row_scale = place("row_scale", [P, T, H, 2])
        s12 = place("s12", [P, T, 2 * H])
        neg_s2 = place("neg_s2", [P, T, H])
        guard = place("guard", [P, H])
        SETUP_AT = at[0]
        signs = place("signs", [P, SIGNS, N], I8)
        masks = [place(f"masks{i}", [P, 2, N], I8) for i in range(RING)]
        s1_bc = [place(f"s1_bc{i}", [P, N]) for i in range(2)]
        vals = [place(f"vals{i}", [P, T, 2, PART, DV], BF16) for i in range(2)]
        weighted = place("weighted", [P, T, 2, DV])
        residue = place("residue", [P, T, 2, DV])
        sums = place("sums", [P, T, 2, DV])
        scaled = place("scaled", [P, T, 2, DH])
        den2 = place("den2", [P, T, 2])
        den = place("den", [P, T])
        rden = place("rden", [P, T])
        scale_n = place("scale_n", [P, T, 2])

        SMALL_AT = at[0]

        SIGNS_AT = SETUP_AT
        MASKS_AT = SIGNS_AT + SIGNS * N
        S1_AT = MASKS_AT + RING * 2 * N
        VALS_AT = S1_AT + 2 * 4 * N
        WEIGHTED_AT = VALS_AT + 2 * 2 * T * 2 * SIDE
        w_seq_sb = place("w_seq_sb", [P, KD, D], F32, SIGNS_AT)
        s1_t = place("s1_t", [H, N], F32, SIGNS_AT + 4 * KD * D)
        adj_stage = place("adj_stage", [P, 2, N], F32, MASKS_AT)
        wa_prod = place("wa_prod", [P, 2, KD, D], F32, S1_AT)
        at[0] = VALS_AT
        xn = [place(f"xn{i}", [P, D]) for i in range(2)]
        xn_hi = [place(f"xn_hi{i}", [P, KD, P], F32R) for i in range(2)]
        xn_lo = [place(f"xn_lo{i}", [P, KD, P], F32R) for i in range(2)]
        assert at[0] <= WEIGHTED_AT
        at[0] = WEIGHTED_AT
        w_seq_hi = place("w_seq_hi", [P, KD, D], F32R)
        w_seq_lo = place("w_seq_lo", [P, KD, D], F32R)
        at[0] = SMALL_AT
        a12 = place("a12", [P, 2, DH])
        wa = place("wa", [P, KD, 2 * H])
        wa_hl = place("wa_hl", [P, KD, 2, 2 * H], F32R)
        stats = place("stats", [P, T, 6])
        mean_var = place("mean_var", [P, T, 2])
        std = place("std", [P, T])
        rstd = place("rstd", [P, T])
        smax = place("smax", [P, H])
        shifted = place("shifted", [P, 3, T, H])

        HALF = KR * CT
        xn2_lo = place("xn2_lo", [P, KD, CT], F32R, ROWS_AT)
        z1_pre = place("z1_pre", [P, C, KR, CT], F32, ROWS_AT + 2 * 4 * HALF)
        z1_eighths = place("z1_parts", [P, 2 * C, HALF], F32R, ROWS_AT)

        def z1_parts(c):
            first = 0 if isinstance(c, int) and c == 0 else 9 - 3 * c
            return [z1_eighths[:, bass.ds(first + part, 1), :].rearrange("p a n -> p (a n)") for part in range(2)]

        at[0] = SEQ_AT
        STAGE_AT = at[0]
        PIECE = 2 * D
        stage = [place(f"stage{i}", [P, PIECE]) for i in range(2)]
        W_OUT_AT = at[0]
        w_out_hi = place("w_out_hi", [P, KD, D], F32R)
        w_out_lo = place("w_out_lo", [P, KD, D], F32R)
        b_hi = place("b_hi", [1, D], F32R)
        b_lo = place("b_lo", [1, D], F32R)
        ones = place("ones", [1, P], F32R)
        wout2_hi = place("wout2_hi", [P, KR, D], F32R, W_OUT_AT)
        wout2_lo = place("wout2_lo", [P, KR, D], F32R, W_OUT_AT + 4 * KR * D)
        proj_sb = place("proj_sb", [P, KD, E])
        proj_hl = place("proj_hl", [P, KD, 2, E], F32R)
        k_int = place("k_int", [P, E], I32)
        k_row = place("k_row", [P, E])
        inv_k = place("inv_k", [P, E])
        std2 = place("std2", [P, T])
        rstd2 = place("rstd2", [P, T])
        col_all = {n: place(f"col_{n}", [P, T]) for n in ("sum", "mean", "var", "std")}
        col_all.update(rstd=col_all["std"], max=col_all["mean"], support=col_all["sum"], tau=col_all["var"])
        bias1 = place("bias1", [P, KR])
        bias2 = place("bias2", [P, KR])
        c_raw = place("c_raw", [3 * E, 2, R])
        assert at[0] <= EDGES_AT
        at[0] = EDGES_AT
        x2 = place("x2", [P, T, D])
        win1_hi = place("win1_hi", [P, KD, R], F32R)
        win1_lo = place("win1_lo", [P, KD, R], F32R)
        wout1_hi = place("wout1_hi", [P, KR, O], F32R)
        wout1_lo = place("wout1_lo", [P, KR, O], F32R)
        win2_hi = place("win2_hi", [P, KO, R], F32R)
        win2_lo = place("win2_lo", [P, KO, R], F32R)
        a_all = place("a_all", [P, T, 3 * E], F32R)
        u_sb = place("u_sb", [P, T, E])
        keep = place("keep", [P, T - T // C, E])
        c_hl = place("c_hl", [3 * E, 2, R], F32R)
        stats2 = place("stats2", [P, T, 6])
        mean_var2 = place("mean_var2", [P, T, 2])
        WORK_AT = at[0]
        hq = [place(f"hq{i}", [P, D]) for i in range(2)]
        h_hi = [place(f"h_hi{i}", [P, KD, P], F32R) for i in range(2)]
        h_lo = [place(f"h_lo{i}", [P, KD, P], F32R) for i in range(2)]
        y_exp = place("y_exp", [P, 2, D])
        x_plus = place("x_plus", [P, 2, D])
        xn2 = [place(f"xn2_{i}", [P, D]) for i in range(2)]
        xn2_hi = place("xn2_hi", [P, KD, CT], F32R)
        ENT_TILES = (range(0, T // C), range(T // C, T))
        ENT_AT_BYTE = (ROWS_AT + 5 * 4 * HALF, WORK_AT + 4 * KR * CT)
        ent, col = [], []
        for part, tiles in enumerate(ENT_TILES):
            e = {}
            for i, n in enumerate(("z", "sq", "rest", "sorted", "cum", "mean", "msq", "root", "tau", "pick")):
                e[n] = place(f"ent{part}_{n}", [P, len(tiles), E], F32, ENT_AT_BYTE[part] + 4 * E * len(tiles) * i)
            e["sorted2"], e["cum2"], e["a"] = e["sq"], e["rest"], e["mean"]
            ent.append(e)
            col.append({n: col_all[n][:, tiles[0]:tiles[-1] + 1] for n in col_all})
        HR = 4
        a_col = place("a_col", [P, T // C, 3 * E], F32, W_OUT_AT + 8 * KD * D + 4 * CT)
        gate2 = place("gate2", [P, KR, CT], F32, STAGE_AT)
        out_rows = place("out_rows", [P, 2, D], F32, STAGE_AT + 4 * KR * CT)
        at[0] = WORK_AT
        z_tmp = place("z_tmp", [P, KR, CT])
        z2_hi = place("z2_hi", [P, KR, CT], F32R)
        z2_lo = place("z2_lo", [P, KR, CT], F32R)
        h_full = [place(f"h_full{i}", [P, CT]) for i in range(2)]
        hr_hi = [place(f"hr_hi{i}", [P, CT], F32R) for i in range(HR)]
        hr_lo = [place(f"hr_lo{i}", [P, CT], F32R) for i in range(HR)]
        a_t = place("a_t", [3 * E, CT], F32R, W_OUT_AT + 8 * KD * D)

        w_out_v = w_out.rearrange("(k p) n -> p k n", p=P)
        wout1_v = wout1_t.rearrange("(k p) n -> p k n", p=P)
        win2_v = win2[0:O, :].rearrange("(k p) n -> p k n", p=P)

        def flat_kn(a):
            return a.rearrange("p k n -> p (k n)")

        pieces = []
        for k in range(0, KD, 2):
            pieces.append((w_out_v[:, k:k + 2, :], flat_kn(w_out_hi[:, k:k + 2, :]), flat_kn(w_out_lo[:, k:k + 2, :])))
        pieces.append((b_out.rearrange("(a n) -> a n", a=1), b_hi[:], b_lo[:]))
        W_OUT_PIECES = len(pieces)
        pieces.append((win1[0:D, :].rearrange("(k p) n -> p k n", p=P), flat_kn(win1_hi[:]), flat_kn(win1_lo[:])))
        WIN1_PIECES = len(pieces)
        for half in range(O // PIECE):
            for k in range(KR):
                o = slice(half * PIECE, (half + 1) * PIECE)
                pieces.append((wout1_v[:, k, o], wout1_hi[:, k, o], wout1_lo[:, k, o]))
        WOUT1_PIECES = len(pieces)
        for k in range(0, KO, PIECE // R):
            o = slice(k, k + PIECE // R)
            pieces.append((win2_v[:, o, :], flat_kn(win2_hi[:, o, :]), flat_kn(win2_lo[:, o, :])))
        WIN2_PIECES = len(pieces)
        pieces.append((wout2_t.rearrange("(k p) n -> p k n", p=P), flat_kn(wout2_hi[:]), flat_kn(wout2_lo[:])))

        def stage_of(n):
            hi = pieces[n][1]
            return stage[n % 2][0:hi.shape[0], 0:hi.shape[1]]

        ONE = 1
        x_in = [sem(f"x_in{q}") for q in range(4)]
        w_seq_in = sem("w_seq_in")
        a_in = sem("a_in")
        adj_in = [sem(f"adj_in{i}") for i in range(2)]
        s1_saved = sem("s1_saved")
        s1_in = [sem(f"s1_in{i}") for i in range(2)]
        x2_in = [sem(f"x2_in{q}") for q in range(4)]
        out_saved = [sem(f"out_saved{i}") for i in range(2)]
        ident_ready = sem("ident_ready")
        dve_step = sem("dve_step")
        stats_ready = sem("stats_ready")
        moments_ready = sem("moments_ready")
        std_ready = sem("std_ready")
        w_seq_hi_ready = sem("w_seq_hi_ready")
        w_seq_lo_ready = sem("w_seq_lo_ready")
        wa_prod_ready = sem("wa_prod_ready")
        wa_ready = sem("wa_ready")
        wa_hi_ready = sem("wa_hi_ready")
        wa_hl_ready = sem("wa_hl_ready")
        xn_ready = sem("xn_ready")
        xn_turned = sem("xn_turned")
        xn_hi_ready = sem("xn_hi_ready")
        xn_lo_ready = sem("xn_lo_ready")
        s1_turned = sem("s1_turned")
        s1_t_ready = sem("s1_t_ready")
        proj_done = sem("proj_done")
        seq_ready = sem("seq_ready")
        s12_ready = sem("s12_ready")
        edges_ready = sem("edges_ready")
        smax_ready = sem("smax_ready")
        guard_ready = sem("guard_ready")
        shifted_ready = sem("shifted_ready")
        weights_ready = sem("weights_ready")
        signs_act = sem("signs_act")
        signs_dve = sem("signs_dve")
        neg_cut = sem("neg_cut")
        pos_dve = sem("pos_dve")
        pos_pool = sem("pos_pool")
        bank_passed = sem("bank_passed")
        weighted_ready = sem("weighted_ready")
        vals_ready = sem("vals_ready")
        pe_passed_waits = sem("pe_passed_waits")
        sp_passed_waits = sem("sp_passed_waits")
        bank_free = sem("bank_free")
        scale_ready = sem("scale_ready")
        scaled_ready = sem("scaled_ready")
        head_done = sem("head_done")
        piece_in = [sem(f"piece_in{i}") for i in range(2)]
        w_hi_ready = sem("w_hi_ready")
        w_lo_ready = sem("w_lo_ready")
        small_in = sem("small_in")
        ones_ready = sem("ones_ready")
        small_ready = sem("small_ready")
        hq_in = [sem(f"hq_in{i}") for i in range(2)]
        h_turned = sem("h_turned")
        h_hi_ready = sem("h_hi_ready")
        h_lo_ready = sem("h_lo_ready")
        y_done = sem("y_done")
        y_low_ready = sem("y_low_ready")
        y_exp_ready = sem("y_exp_ready")
        x_plus_ready = sem("x_plus_ready")
        x2_ready = sem("x2_ready")
        stats2_ready = sem("stats2_ready")
        mean_var2_ready = sem("mean_var2_ready")
        var2_ready = sem("var2_ready")
        std2_ready = sem("std2_ready")
        rstd2_ready = sem("rstd2_ready")
        xn2_ready = sem("xn2_ready")
        xn2_turned = sem("xn2_turned")
        xn2_hi_ready = sem("xn2_hi_ready")
        xn2_lo_ready = sem("xn2_lo_ready")
        u_done = sem("u_done")
        u_ready = sem("u_ready")
        z1_pre_done = sem("z1_pre_done")
        z1_pre_ready = sem("z1_pre_ready")
        k_ready = sem("k_ready")
        ent_step = sem("ent_step")
        var_ready = sem("var_ready")
        var_std_ready = sem("var_std_ready")
        delta_ready = sem("delta_ready")
        root_ready = sem("root_ready")
        a_ready = sem("a_ready")
        a_col_ready = sem("a_col_ready")
        a_turned = sem("a_turned")
        a_t_ready = sem("a_t_ready")
        gate1_done = sem("gate1_done")
        gate2_done = sem("gate2_done")
        gate2_ready = sem("gate2_ready")
        z1_tmp_ready = sem("z1_tmp_ready")
        z1_hi_ready = sem("z1_hi_ready")
        z1_ready = sem("z1_ready")
        h_done = sem("h_done")
        h_full_ready = sem("h_full_ready")
        h_hi_cut = sem("h_hi_cut")
        h_split = sem("h_split")
        h_used = sem("h_used")
        z2_tmp_ready = sem("z2_tmp_ready")
        z2_hi_ready = sem("z2_hi_ready")
        z2_ready = sem("z2_ready")
        o_done = sem("o_done")
        o_ready = sem("o_ready")

        x_view = x.rearrange("(t p) d -> p t d", p=P)
        adj_view = adj_t.rearrange("(t p) n -> t p n", p=P)
        out_view = out.rearrange("(t p) d -> t p d", p=P)
        TQ = T // 4

        block = ctx.enter_context(nc.Block())

        @block.sync
        def _(sp):
            for i in range(2):
                sp.sem_inc(out_saved[i], 16)
            def load_x(q):
                sp.dma_start(x_rows[:, q * TQ:(q + 1) * TQ, :], x_view[:, q * TQ:(q + 1) * TQ, :]).then_inc(x_in[q], 16)
            load_x(0)
            sp.dma_start(w_seq_sb[:], w_seq.rearrange("(k p) n -> p k n", p=P)).then_inc(w_seq_in, 16)
            sp.dma_start(a12[:, 0, :], a1.partition_broadcast(P)).then_inc(a_in, 16)
            sp.dma_start(a12[:, 1, :], a2.partition_broadcast(P)).then_inc(a_in, 16)
            load_x(1)
            load_x(2)
            for i in range(2):
                sp.dma_start(adj_stage[:, i, :], adj_view[i]).then_inc(adj_in[i], 16)
            load_x(3)
            with sp.Fori(1, T // 2) as tp:
                for i in range(2):
                    sp.wait_ge(edges_ready, 2 * tp + i - 1)
                    sp.sem_inc(sp_passed_waits)
                    sp.dma_start(adj_stage[:, i, :], adj_view[bass.ds(2 * tp + i, 1)].rearrange("a p n -> (a p) n"))\
                        .then_inc(adj_in[i], 16)
            sp.wait_ge(wa_ready, 2)
            def load_first_s1(h, quarters):
                tokens = slice(quarters[0] * CT, (quarters[-1] + 1) * CT)
                sp.dma_start(s1_bc[h][:, tokens], s1_dram[h, tokens].partition_broadcast(P)).then_inc(s1_in[h], 16)

            for q in range(C):
                tokens = slice(q * CT, (q + 1) * CT)
                sp.wait_ge(s1_t_ready, q + 1)
                sp.dma_start(s1_dram[:, tokens], s1_t[:, tokens]).then_inc(s1_saved, 16)
                if q == C - 2:
                    sp.wait_ge(s1_saved, 16 * (q + 1))
                    load_first_s1(0, range(C - 1))
            sp.wait_ge(s1_saved, 16 * C)
            load_first_s1(0, [C - 1])
            for part in (range(C - 1), [C - 1]):
                load_first_s1(1, part)

            def load_s1(h, i):
                sp.dma_start(s1_bc[i][:], s1_dram[bass.ds(h, 1), :].rearrange("a n -> (a n)").partition_broadcast(P))\
                    .then_inc(s1_in[i], 16)
            with sp.Fori(1, H // 2) as hp:
                for i in range(2):
                    sp.wait_ge(neg_cut, SIGNS + T * (2 * hp + i - 1))
                    sp.sem_inc(sp_passed_waits)
                    load_s1(2 * hp + i, i)

            def load_piece(n):
                if n >= 2:
                    sp.wait_ge(w_lo_ready, n - 1)
                src, slot = pieces[n][0], stage_of(n)
                if len(src.shape) == 3:
                    slot = slot.rearrange("p (k n) -> p k n", k=src.shape[1])
                sp.dma_start(slot, src).then_inc(piece_in[n % 2], 16)

            sp.wait_ge(vals_ready, H)
            for n in range(W_OUT_PIECES):
                load_piece(n)
            sp.dma_start(proj_sb[:], proj.rearrange("(k p) n -> p k n", p=P)).then_inc(small_in, 16)
            for k in range(KR):
                sp.dma_start(bias1[:, k:k + 1], win1[D:D + 1, k * P:(k + 1) * P].rearrange("a p -> p a")).then_inc(small_in, 16)
                sp.dma_start(bias2[:, k:k + 1], win2[O:O + 1, k * P:(k + 1) * P].rearrange("a p -> p a")).then_inc(small_in, 16)
            sp.wait_ge(neg_cut, SIGNS + T * H)
            sp.wait_ge(pos_dve, N_PDVE * H)
            sp.wait_ge(pos_pool, N_POOL * H)
            for q in range(2):
                sp.dma_start(x2[:, q * TQ:(q + 1) * TQ, :], x_view[:, q * TQ:(q + 1) * TQ, :]).then_inc(x2_in[q], 16)
            sp.wait_ge(head_done, ONE + H)

            def load_hidden(tp):
                for i in range(2):
                    if tp > 0:
                        sp.wait_ge(h_turned, 2 * tp + i - 1)
                    sp.dma_start(hq[i][:], hidden[:, 2 * tp + i, :]).then_inc(hq_in[i], 16)
            load_hidden(0)
            for s in range(3):
                sp.dma_start(c_raw[s * E:(s + 1) * E, 0, :], c1).then_inc(small_in, 16)
                sp.dma_start(c_raw[s * E:(s + 1) * E, 1, :], c2).then_inc(small_in, 16)
            load_piece(W_OUT_PIECES)
            load_piece(W_OUT_PIECES + 1)
            n = W_OUT_PIECES + 2
            for tp in range(1, T // 2):
                load_hidden(tp)
                if tp % 2:
                    for _ in range(2 if tp > 1 else 0):
                        load_piece(n)
                        n += 1
                elif tp // 2 + 1 < 4:
                    q = tp // 2 + 1
                    sp.dma_start(x2[:, q * TQ:(q + 1) * TQ, :], x_view[:, q * TQ:(q + 1) * TQ, :]).then_inc(x2_in[q], 16)
            for n in range(n, len(pieces)):
                load_piece(n)

            with sp.Fori(0, T // 2) as tp:
                for i in range(2):
                    sp.wait_ge(o_ready, ONE + 2 * tp + i + 1)
                    sp.sem_inc(sp_passed_waits)
                    sp.dma_start(out_view[bass.ds(2 * tp + i, 1)].rearrange("a p n -> (a p) n"), out_rows[:, i, :])\
                        .then_inc(out_saved[i], 16)
            for i in range(2):
                sp.wait_ge(out_saved[i], 16 + 16 * T // 2)

        TPC = T // C
        SMALL_LOADS = 16 * (1 + 2 * KR + 6)
        FINAL_AT = {3: 0, 4: 1, 5: 2, 6: 3}
        GATE2_AT = {7: 0, 8: 1}
        TURN_A_AT = 9
        GATE1_AT = {11: 0, 13: 1}
        ENT_AT = (0, 3, 6)
        ENT_ROOT_AT = 4

        def weigh(engine, h):
            wt = weight[:, :, bass.ds(h, 1), :].rearrange("p t a s -> p t (a s)")
            engine.tensor_tensor(
                weighted[:, :, :, 0:DH], seq[:, :, bass.ds(DH * h, DH)].unsqueeze(2).to_broadcast([P, T, 2, DH]),
                wt.unsqueeze(3).to_broadcast([P, T, 2, DH]), ALU.mult).then_inc(weighted_ready, 1)
            engine.tensor_copy(weighted[:, :, :, DH], wt).then_inc(weighted_ready, 1)

        @block.gpsimd
        def _(pool):
            pool.sem_inc(head_done, ONE)
            nc.gpsimd.memset(ident[:], 1.0).then_inc(ident_ready, 1)
            pool.wait_ge(ident_ready, 1)
            nc.gpsimd.affine_select(out=ident[:], in_=ident[:], compare_op=ALU.is_equal, fill=0.0, base=0,
                                    pattern=[[-1, P]], channel_multiplier=1).then_inc(ident_ready, 1)
            pool.wait_ge(w_seq_in, 16)
            pool.wait_ge(a_in, 32)
            for s in range(2):
                nc.gpsimd.tensor_tensor(
                    wa_prod[:, s].rearrange("p k (h d) -> p (k h) d", d=DH),
                    w_seq_sb[:].rearrange("p k (h d) -> p (k h) d", d=DH),
                    a12[:, s:s + 1, :].to_broadcast([P, KD * H, DH]), ALU.mult).then_inc(wa_prod_ready, 1)
            pool.wait_ge(smax_ready, 1)
            nc.gpsimd.partition_all_reduce(guard[:], smax[:], P, bass.bass_isa.ReduceOp.max).then_inc(guard_ready, 1)

            def cut_pos(h, j):
                if j not in POS_ON_POOL:
                    return
                if j % GROUP == min(k for k in POS_ON_POOL if k // GROUP == j // GROUP) % GROUP:
                    pool.wait_ge(bank_passed, BANKS * (NG * h + j // GROUP + 1))
                pool.wait_ge(neg_cut, SIGNS + T * h + j + 1)
                m = masks[j % RING]
                nc.gpsimd.tensor_tensor(m[:, 1, :].bitcast(I32), edges[:, j, :].bitcast(I32), m[:, 0, :].bitcast(I32),
                                        ALU.subtract).then_inc(pos_pool, 1)

            def combine(h):
                pool.wait_ge(scale_ready, h + 1)
                nc.gpsimd.tensor_tensor(scaled[:], sums[:, :, :, 0:DH], scale_n[:].unsqueeze(3).to_broadcast([P, T, 2, DH]),
                                        ALU.mult).then_inc(scaled_ready, 1)
                pool.wait_ge(scaled_ready, h + 1)
                nc.gpsimd.tensor_tensor(hidden[:, :, bass.ds(DH * h, DH)], scaled[:, :, 0, :], scaled[:, :, 1, :],
                                        ALU.add).then_inc(head_done, 1)

            def lo_piece(n):
                pool.wait_ge(w_hi_ready, n + 1)
                nc.gpsimd.tensor_tensor(pieces[n][2], stage_of(n), pieces[n][1].bitcast(F32), ALU.subtract)\
                    .then_inc(w_lo_ready, 1)

            def head(h, is_last):
                if not is_last:
                    pool.wait_ge(vals_ready, h + 1)
                    weigh(nc.gpsimd, h + 1)
                for j in range(AHEAD, T):
                    cut_pos(h, j)
                if is_last:
                    for n in range(W_OUT_PIECES):
                        lo_piece(n)
                else:
                    for j in range(AHEAD):
                        cut_pos(h + 1, j)
                    combine(h)

            pool.wait_ge(weights_ready, 4)
            pool.wait_ge(seq_ready, 2 + T)
            for j in range(AHEAD):
                cut_pos(0, j)
            with pool.Fori(0, H - 1) as h:
                head(h, False)
            head(H - 1, True)

            nc.gpsimd.iota(k_int[:], pattern=[[1, E]], base=1, channel_multiplier=0).then_inc(k_ready, 1)

            def copy_a(c):
                pool.wait_ge(a_ready, min(c, 1) + 1)
                if c > 0:
                    pool.wait_ge(a_turned, c)
                nc.gpsimd.tensor_copy(a_col[:], a_all[:, c * TPC:(c + 1) * TPC, :].bitcast(F32)).then_inc(a_col_ready, 1)

            def small_parts():
                pool.wait_ge(small_in, SMALL_LOADS)
                nc.gpsimd.tensor_copy(proj_hl[:, :, 0, :], proj_sb[:]).then_inc(small_ready, 1)
                nc.gpsimd.tensor_copy(c_hl[:], c_raw[:]).then_inc(small_ready, 1)
                pool.wait_ge(small_ready, 2)
                nc.gpsimd.tensor_tensor(proj_hl[:, :, 1, :], proj_sb[:], proj_hl[:, :, 0, :].bitcast(F32), ALU.subtract)\
                    .then_inc(small_ready, 1)
                pool.wait_ge(small_ready, 3)
                nc.gpsimd.tensor_tensor(c_hl[2 * E:3 * E], c_raw[2 * E:3 * E], c_hl[2 * E:3 * E].bitcast(F32), ALU.subtract)\
                    .then_inc(small_ready, 1)

            lo_piece(W_OUT_PIECES)
            small_parts()
            pool.wait_ge(small_ready, 4)
            for n in range(W_OUT_PIECES + 1, WOUT1_PIECES + 3):
                lo_piece(n)
            pool.wait_ge(y_done, 2 + T)
            copy_a(0)
            for n in range(WOUT1_PIECES + 3, len(pieces)):
                lo_piece(n)
            for c in range(1, C):
                copy_a(c)

        @block.scalar
        def _(act):
            act.sem_inc(seq_ready, 2)
            act.sem_inc(gate2_ready, ONE)
            act.sem_inc(h_full_ready, ONE)
            def deviation(q):
                act.wait_ge(moments_ready, (TPC + 1) * (q + 1))
                ts = slice(q * TPC, (q + 1) * TPC)
                nc.scalar.activation(std[:, ts], mean_var[:, ts, 1], ACT.Sqrt).then_inc(std_ready, 1)

            def copy_xn_hi(t, i):
                act.wait_ge(xn_turned, t + 1)
                act.wait_ge(proj_done, t + 1)
                nc.scalar.activation(flat_kn(xn_hi[i][:]), psum[i][:, :], ACT.Copy).then_inc(xn_hi_ready, 1)

            def adj_tile(tp, i):
                act.wait_ge(adj_in[i], 16 * tp + 16)
                nc.scalar.activation(edges[:, bass.ds(2 * tp + i, 1), :].rearrange("p a n -> p (a n)"), adj_stage[:, i, :],
                                     ACT.Copy, scale=EDGE).then_inc(edges_ready, 1)

            def evict_seq(t, i):
                act.wait_ge(proj_done, 2 + t + 1)
                nc.scalar.activation(seq[:, bass.ds(t, 1), :].rearrange("p a d -> p (a d)"), psum[2 + i][:, :], ACT.Copy)\
                    .then_inc(seq_ready, 1)

            deviation(0)
            copy_xn_hi(0, 0)
            act.wait_ge(w_seq_in, 16)
            nc.scalar.activation(flat_kn(w_seq_hi[:]), flat_kn(w_seq_sb[:]), ACT.Copy).then_inc(w_seq_hi_ready, 1)
            deviation(1)
            for q in range(C):
                if 0 < q < C - 1:
                    deviation(q + 1)
                with act.Fori(q * TPC // 2, (q + 1) * TPC // 2 - (q == C - 1)) as tp:
                    for i in range(2):
                        copy_xn_hi(2 * tp + i + 1, 1 - i)
                        evict_seq(2 * tp + i, i)
                        adj_tile(tp, i)
            copy_xn_hi(T - 1, 1)
            for i in range(2):
                evict_seq(T - 2 + i, i)
                adj_tile(T // 2 - 1, i)

            def sign(h, i, j):
                if j in SIGN_ON_DVE:
                    return
                act.wait_ge(neg_cut, T * h + j + 1)
                nc.scalar.activation(signs[:, j % SIGNS, :], s1_bc[i][:], ACT.Sign,
                                     bias=s12[:, j, bass.ds(H + h, 1)]).then_inc(signs_act, 1)

            def wait_s1(hp, i):
                act.wait_ge(s1_in[i], 16 * hp + 32)

            act.wait_ge(shifted_ready, 3)
            nc.scalar.activation(weight[:, :, :, 0], shifted[:, 0], ACT.Exp, scale=0.2).then_inc(weights_ready, 1)
            nc.scalar.activation(weight[:, :, :, 1], shifted[:, 0], ACT.Exp).then_inc(weights_ready, 1)
            nc.scalar.activation(row_scale[:, :, :, 0], shifted[:, 1], ACT.Exp, scale=-0.8).then_inc(weights_ready, 1)
            nc.scalar.activation(row_scale[:, :, :, 1], shifted[:, 2], ACT.Exp, scale=0.8).then_inc(weights_ready, 1)

            act.wait_ge(s12_ready, 2 + T)
            act.wait_ge(s1_saved, 16 * C)
            wait_s1(0, 0)
            for j in range(AHEAD):
                sign(0, 0, j)
            with act.Fori(0, H // 2 - 1) as hp:
                for i in range(2):
                    for j in range(AHEAD, T):
                        sign(2 * hp + i, i, j)
                    wait_s1(hp + i, 1 - i)
                    for j in range(AHEAD):
                        sign(2 * hp + i + 1, 1 - i, j)
            for j in range(AHEAD, T):
                sign(H - 2, 0, j)
            wait_s1(H // 2 - 1, 1)
            def hi_piece(n):
                act.wait_ge(piece_in[n % 2], 16 * (n // 2 + 1))
                nc.scalar.activation(pieces[n][1], stage_of(n), ACT.Copy).then_inc(w_hi_ready, 1)

            for j in range(T):
                sign(H - 1, 1, j)
                if j >= T - W_OUT_PIECES:
                    hi_piece(j - (T - W_OUT_PIECES))

            def copy_h_hi(t, i):
                act.wait_ge(h_turned, t + 1)
                act.wait_ge(y_done, t + 1)
                nc.scalar.activation(flat_kn(h_hi[i][:]), psum[i][:, :], ACT.Copy).then_inc(h_hi_ready, 1)

            def exp_y(t, i):
                act.wait_ge(y_done, 2 + t + 1)
                act.wait_ge(x2_ready, t + 1)
                nc.scalar.activation(y_exp[:, i, :], psum[2 + i][:, :], ACT.Relu, scale=-1.0).then_inc(y_low_ready, 1)
                act.wait_ge(y_low_ready, 2 + t + 1)
                nc.scalar.activation(y_exp[:, i, :], y_exp[:, i, :], ACT.Exp, scale=-1.0).then_inc(y_exp_ready, 1)

            def copy_xn2_hi(n, i, column):
                act.wait_ge(xn2_turned, 2 + n + 1)
                nc.scalar.activation(xn2_hi[:, :, bass.ds(column, P)], psum[4 + i][:, :].rearrange("p (k n) -> p k n", k=KD),
                                     ACT.Copy).then_inc(xn2_hi_ready, 1)

            def project_quarter(q):
                with act.Fori(q * TPC // 2, (q + 1) * TPC // 2 - (q == C - 1)) as tp:
                    for i in range(2):
                        t = 2 * tp + i
                        copy_h_hi(t + 1, 1 - i)
                        exp_y(t, i)
                        if q > 0:
                            copy_xn2_hi(t - TPC, i, P * (t - q * TPC))
                if q == C - 1:
                    copy_h_hi(T - 1, 1)
                    for i in range(2):
                        exp_y(T - 2 + i, i)
                        copy_xn2_hi(T - 2 + i - TPC, i, P * (TPC - 2 + i))

            def deviation(q):
                act.wait_ge(var2_ready, q + 1)
                ts = slice(q * TPC, (q + 1) * TPC)
                nc.scalar.activation(std2[:, ts], mean_var2[:, ts, 1], ACT.Sqrt).then_inc(std2_ready, 1)

            def norm_quarter(q):
                for t in range(TPC):
                    copy_xn2_hi(q * TPC + t, t % 2, t * P)
                    if t == 1:
                        copy_a_t(0)

            def z1_pre_quarter(q):
                for k in range(KR):
                    act.wait_ge(z1_pre_done, KR * q + k + 1)
                    nc.scalar.activation(z1_pre[:, q, k, :], psum[6][:, :], ACT.Copy).then_inc(z1_pre_ready, 1)

            def ent_root(part, which):
                if which == 0:
                    act.wait_ge(var_ready, part + 1)
                    nc.scalar.activation(col[part]["std"], col[part]["var"], ACT.Sqrt).then_inc(var_std_ready, 1)
                else:
                    act.wait_ge(delta_ready, part + 1)
                    nc.scalar.activation(ent[part]["root"][:], ent[part]["msq"][:], ACT.Sqrt).then_inc(root_ready, 1)

            def copy_a_t(c):
                act.wait_ge(a_turned, c + 1)
                nc.scalar.activation(a_t[:], psum[0][0:3 * E, :], ACT.Copy).then_inc(a_t_ready, 1)

            act.sem_inc(y_low_ready, 2)
            copy_h_hi(0, 0)
            n = W_OUT_PIECES
            for q in range(C):
                if q == 2:
                    z1_pre_quarter(0)
                project_quarter(q)
                deviation(q)
                if q == 2:
                    ent_root(0, 0)
                    z1_pre_quarter(1)
                    ent_root(0, 1)
                for _ in range(2):
                    hi_piece(n)
                    n += 1
            z1_pre_quarter(C - 2)
            hi_piece(n)
            n += 1
            norm_quarter(C - 1)
            z1_pre_quarter(C - 1)
            ent_root(1, 0)
            while n < len(pieces):
                hi_piece(n)
                n += 1

            def chunk(c, first, is_last):
                for o in range(KO):
                    n = KO * c + o
                    act.wait_ge(h_done, n + 1)
                    act.wait_ge(h_split, n + 1)
                    nc.scalar.activation(h_full[o % 2][:], psum[1 + o % 3][:, :], ACT.Gelu).then_inc(h_full_ready, 1)
                    if o in GATE2_AT:
                        k = GATE2_AT[o]
                        act.wait_ge(gate2_done, KR * c + k + 1)
                        if k == 0:
                            act.wait_ge(z2_tmp_ready, ONE + KR * c)
                            if first:
                                act.wait_ge(w_lo_ready, len(pieces))
                        nc.scalar.activation(gate2[:, k, :], psum[0][:, :], ACT.Copy).then_inc(gate2_ready, 1)
                    if o == TURN_A_AT and not is_last:
                        copy_a_t(c + 1)
                    if first and o == ENT_ROOT_AT:
                        ent_root(1, 1)

            chunk(0, True, False)
            with act.Fori(1, C - 1) as c:
                chunk(c, False, False)
            chunk(C - 1, False, True)

        @block.vector
        def _(dve):
            dve.sem_inc(s12_ready, 2)
            dve.sem_inc(xn_lo_ready, 2)
            steps = [0]

            def step(instruction):
                steps[0] += 1
                instruction.then_inc(dve_step, 1)
                dve.wait_ge(dve_step, steps[0])

            def row_stats(t):
                nc.vector.bn_stats(stats[:, bass.ds(t, 1), :].rearrange("p a s -> p (a s)"),
                                   x_rows[:, bass.ds(t, 1), :].rearrange("p a s -> p (a s)")).then_inc(stats_ready, 1)

            def moments(q):
                ts = slice(q * TPC, (q + 1) * TPC)
                dve.wait_ge(stats_ready, (q + 1) * TPC)
                for t in range(q * TPC, (q + 1) * TPC):
                    nc.vector.bn_aggr(mean_var[:, t, :], stats[:, t, :]).then_inc(moments_ready, 1)
                dve.wait_ge(moments_ready, (TPC + 1) * q + TPC)
                nc.vector.tensor_scalar(mean_var[:, ts, 1], mean_var[:, ts, 1], EPS, None, ALU.add).then_inc(moments_ready, 1)
                dve.wait_ge(std_ready, q + 1)
                step(nc.vector.reciprocal(rstd[:, ts], std[:, ts]))

            def norm(t, i):
                nc.vector.tensor_scalar(xn[i][:], x_rows[:, bass.ds(t, 1), :].rearrange("p a s -> p (a s)"),
                                        mean_var[:, bass.ds(t, 1), 0:1].rearrange("p a s -> p (a s)"),
                                        rstd[:, bass.ds(t, 1)], ALU.subtract, ALU.mult).then_inc(xn_ready, 1)

            def cut_xn_lo(t, i):
                dve.wait_ge(xn_hi_ready, t + 1)
                nc.vector.tensor_tensor(flat_kn(xn_lo[i][:]), psum[i][:, :], flat_kn(xn_hi[i][:]).bitcast(F32), ALU.subtract)\
                    .then_inc(xn_lo_ready, 1)

            def evict_scores(t, i):
                dve.wait_ge(proj_done, 2 + t + 1)
                nc.vector.tensor_reduce(s12[:, bass.ds(t, 1), :].rearrange("p a s -> p (a s)"),
                                        psum[4 + i][:, 0:4 * H].rearrange("p (s h) -> p h s", s=2), AX.X, ALU.add)\
                    .then_inc(s12_ready, 1)

            def evict_s1(q):
                dve.wait_ge(s1_turned, q + 1)
                nc.vector.tensor_copy(s1_t[:, q * CT:(q + 1) * CT], psum[6 + q % 2][0:H, :]).then_inc(s1_t_ready, 1)

            dve.wait_ge(x_in[0], 16)
            for t in range(TPC):
                row_stats(t)
            moments(0)
            norm(0, 0)
            norm(1, 1)
            cut_xn_lo(0, 0)
            dve.wait_ge(w_seq_hi_ready, 1)
            nc.vector.tensor_tensor(flat_kn(w_seq_lo[:]), flat_kn(w_seq_sb[:]), flat_kn(w_seq_hi[:]).bitcast(F32), ALU.subtract)\
                .then_inc(w_seq_lo_ready, 1)
            dve.wait_ge(x_in[1], 16)
            for t in range(TPC, 2 * TPC):
                row_stats(t)
            moments(1)
            for s in range(2):
                dve.wait_ge(wa_prod_ready, s + 1)
                nc.vector.tensor_reduce(wa[:, :, s * H:(s + 1) * H], wa_prod[:, s].rearrange("p k (h d) -> p k h d", d=DH),
                                        AX.X, ALU.add).then_inc(wa_ready, 1)
            dve.wait_ge(wa_ready, 2)
            nc.vector.tensor_copy(wa_hl[:, :, 0, :], wa[:]).then_inc(wa_hi_ready, 1)
            dve.wait_ge(wa_hi_ready, 1)
            nc.vector.tensor_tensor(wa_hl[:, :, 1, :], wa[:], wa_hl[:, :, 0, :].bitcast(F32), ALU.subtract).then_inc(wa_hl_ready, 1)
            for q in range(C):
                if 0 < q < C - 1:
                    moments(q + 1)
                if q < 2:
                    dve.wait_ge(x_in[q + 2], 16)
                with dve.Fori(q * TPC // 2, (q + 1) * TPC // 2 - (q == C - 1)) as tp:
                    for i in range(2):
                        cut_xn_lo(2 * tp + i + 1, 1 - i)
                        norm(2 * tp + i + 2, i)
                        if q < 2:
                            row_stats(2 * tp + i + 2 * TPC)
                        evict_scores(2 * tp + i, i)
                if q > 0:
                    evict_s1(q - 1)
            cut_xn_lo(T - 1, 1)
            for i in range(2):
                evict_scores(T - 2 + i, i)
            evict_s1(C - 1)

            dve.wait_ge(s12_ready, 2 + T)
            s1_all, s2_all = s12[:, :, 0:H], s12[:, :, H:2 * H]
            nc.vector.tensor_reduce(smax[:], s2_all.rearrange("p t h -> p h t"), AX.X, ALU.max).then_inc(smax_ready, 1)
            nc.vector.tensor_scalar(neg_s2[:], s2_all, -1.0, None, ALU.mult).then_inc(shifted_ready, 1)
            dve.wait_ge(guard_ready, 1)
            guard_bc = guard[:].unsqueeze(1).to_broadcast([P, T, H])
            nc.vector.tensor_tensor(shifted[:, 0], s2_all, guard_bc, ALU.subtract).then_inc(shifted_ready, 1)
            step(nc.vector.tensor_tensor(shifted[:, 1], s1_all, guard_bc, ALU.add))
            step(nc.vector.tensor_scalar(shifted[:, 2], shifted[:, 1], 0.0, None, ALU.min))
            nc.vector.tensor_scalar(shifted[:, 1], shifted[:, 1], 0.0, None, ALU.max).then_inc(shifted_ready, 1)

            SETUP_STEPS = steps[0]
            SPLIT_AT = 13
            SPLIT, SCALE = 3, 3

            def split_values(h, i, base):
                v = vals[i][:].rearrange("p t s a d -> p (t s) a d")
                w = weighted[:].rearrange("p t s d -> p (t s) d")
                r = residue[:].rearrange("p t s d -> p (t s) d")
                dve.wait_ge(weighted_ready, 2 * (h + 1))
                nc.vector.tensor_copy(v[:, :, 0, :], w).then_inc(dve_step, 1)
                dve.wait_ge(dve_step, base + 1)
                nc.vector.tensor_tensor(r, w, v[:, :, 0, :], ALU.subtract).then_inc(dve_step, 1)
                dve.wait_ge(dve_step, base + 2)
                nc.vector.tensor_copy(v[:, :, 1, :], r).then_inc(dve_step, 1)
                dve.wait_ge(dve_step, base + 3)
                nc.vector.tensor_tensor(v[:, :, 2, :], r, v[:, :, 1, :], ALU.subtract).then_inc(vals_ready, 1)

            def cut(h, i, j):
                if j % GROUP == 0:
                    dve.wait_ge(bank_passed, BANKS * (NG * h + j // GROUP + 1))
                m, g = masks[j % RING], signs[:, j % SIGNS, :]
                if j in SIGN_ON_DVE:
                    dve.wait_ge(neg_cut, T * h + j + 1)
                    nc.vector.tensor_scalar(g, s1_bc[i][:], neg_s2[:, j, bass.ds(h, 1)], EDGE, ALU.is_lt, ALU.mult)\
                        .then_inc(signs_dve, 1)
                    dve.wait_ge(signs_dve, N_DVE * h + up_to(SIGN_ON_DVE, j))
                else:
                    dve.wait_ge(signs_act, N_ACT * h + up_to(act_tiles, j))
                nc.vector.tensor_tensor(m[:, 0, :].bitcast(I32), edges[:, j, :].bitcast(I32), g.bitcast(I32),
                                        ALU.bitwise_and).then_inc(neg_cut, 1)
                if j not in POS_ON_POOL:
                    dve.wait_ge(neg_cut, SIGNS + T * h + j + 1)
                    nc.vector.tensor_tensor(m[:, 1, :].bitcast(I32), edges[:, j, :].bitcast(I32), m[:, 0, :].bitcast(I32),
                                            ALU.bitwise_xor).then_inc(pos_dve, 1)

            def empty_banks(h, base):
                dve.wait_ge(head_done, ONE + h)
                for b in range(BANKS):
                    dve.wait_ge(bank_passed, BANKS * (GROUPS_FREE + NG * h + NG - 1) + b + 1)
                    nc.vector.tensor_reduce(
                        sums[:, b * Q_PER_BANK:(b + 1) * Q_PER_BANK].rearrange("p q s d -> p (q s) d"),
                        psum[b][:, 0:2 * Q_PER_BANK * SIDE].rearrange("p (g a d) -> p g d a", a=PART, d=DV),
                        AX.X, ALU.add).then_inc(bank_free, 1)
                dve.wait_ge(bank_free, BANKS * (h + 2))
                rs = row_scale[:, :, bass.ds(h, 1), :].rearrange("p t a s -> p t (a s)")
                nc.vector.tensor_tensor(den2[:], sums[:, :, :, DH], rs, ALU.mult).then_inc(dve_step, 1)
                dve.wait_ge(dve_step, base + 1)
                nc.vector.tensor_reduce(den[:], den2[:], AX.X, ALU.add).then_inc(dve_step, 1)
                dve.wait_ge(dve_step, base + 2)
                nc.vector.reciprocal(rden[:], den[:]).then_inc(dve_step, 1)
                dve.wait_ge(dve_step, base + 3)
                nc.vector.tensor_tensor(scale_n[:], rs, rden[:].unsqueeze(2).to_broadcast([P, T, 2]), ALU.mult)\
                    .then_inc(scale_ready, 1)

            def wait_s1(hp, i):
                dve.wait_ge(s1_in[i], 16 * hp + 32)

            dve.sem_inc(neg_cut, SIGNS)
            dve.sem_inc(bank_free, BANKS)
            dve.wait_ge(weights_ready, 2)
            dve.wait_ge(seq_ready, 2 + T)
            weigh(nc.vector, 0)
            split_values(0, 0, SETUP_STEPS)
            dve.wait_ge(weights_ready, 4)
            wait_s1(0, 0)
            dve.wait_ge(edges_ready, T)
            for j in range(AHEAD):
                cut(0, 0, j)

            def head(h, hp_next, i, is_last):
                for j in range(AHEAD, T):
                    cut(h, i, j)
                    if j == SPLIT_AT and not is_last:
                        split_next(h, i)
                if not is_last:
                    wait_s1(hp_next, 1 - i)
                    for j in range(AHEAD):
                        cut(h + 1, 1 - i, j)
                empty_banks(h, SETUP_STEPS + SPLIT + (SPLIT + SCALE) * h + (0 if is_last else SPLIT))

            def split_next(h, i):
                dve.wait_ge(bank_passed, BANKS * (NG * h + GROUPS_FREE))
                split_values(h + 1, 1 - i, SETUP_STEPS + SPLIT + (SPLIT + SCALE) * h)
            with dve.Fori(0, H // 2 - 1) as hp:
                for i in range(2):
                    head(2 * hp + i, hp + i, i, False)
            head(H - 2, H // 2 - 1, 0, False)
            head(H - 1, 0, 1, True)
            dve.wait_ge(scale_ready, H)
            nc.vector.tensor_tensor(scaled[:], sums[:, :, :, 0:DH], scale_n[:].unsqueeze(3).to_broadcast([P, T, 2, DH]),
                                    ALU.mult).then_inc(scaled_ready, 1)
            dve.wait_ge(scaled_ready, H)
            nc.vector.tensor_tensor(hidden[:, :, DH * (H - 1):DH * H], scaled[:, :, 0, :], scaled[:, :, 1, :], ALU.add)\
                .then_inc(head_done, 1)

            dve.wait_ge(head_done, ONE + H)
            nc.vector.memset(ones[:].bitcast(F32), 1.0).then_inc(ones_ready, 1)

            def cut_h_lo(t, i):
                dve.wait_ge(h_hi_ready, t + 1)
                nc.vector.tensor_tensor(flat_kn(h_lo[i][:]), psum[i][:, :], flat_kn(h_hi[i][:]).bitcast(F32), ALU.subtract)\
                    .then_inc(h_lo_ready, 1)

            def add_x(t, i):
                row = x2[:, bass.ds(t, 1), :].rearrange("p a s -> p (a s)")
                dve.wait_ge(y_low_ready, 2 + t + 1)
                dve.wait_ge(x2_ready, t + 1)
                nc.vector.scalar_tensor_tensor(out=x_plus[:, i, :], in0=psum[2 + i][:, :], scalar=0.0, in1=row,
                                               op0=ALU.max, op1=ALU.add).then_inc(x_plus_ready, 1)
                dve.wait_ge(y_exp_ready, t + 1)
                dve.wait_ge(x_plus_ready, 2 + t + 1)
                nc.vector.scalar_tensor_tensor(out=row, in0=y_exp[:, i, :], scalar=-1.0, in1=x_plus[:, i, :],
                                               op0=ALU.add, op1=ALU.add).then_inc(x2_ready, 1)
                dve.wait_ge(x2_ready, 2 + t + 1)
                nc.vector.bn_stats(stats2[:, bass.ds(t, 1), :].rearrange("p a s -> p (a s)"), row).then_inc(stats2_ready, 1)

            def norm(n, i):
                dve.wait_ge(xn2_turned, n + 1)
                nc.vector.tensor_scalar(xn2[i][:], x2[:, bass.ds(n, 1), :].rearrange("p a s -> p (a s)"),
                                        mean_var2[:, bass.ds(n, 1), 0:1].rearrange("p a s -> p (a s)"),
                                        rstd2[:, bass.ds(n, 1)], ALU.subtract, ALU.mult).then_inc(xn2_ready, 1)

            def cut_xn2_lo(n, i, column):
                dve.wait_ge(xn2_hi_ready, n + 1)
                nc.vector.tensor_tensor(
                    xn2_lo[:, :, bass.ds(column, P)], psum[4 + i][:, :].rearrange("p (k n) -> p k n", k=KD),
                    xn2_hi[:, :, bass.ds(column, P)].bitcast(F32), ALU.subtract)\
                    .then_inc(xn2_lo_ready, 1)

            def project_quarter(q):
                dve.wait_ge(x2_in[q], 16)
                with dve.Fori(q * TPC // 2, (q + 1) * TPC // 2 - (q == C - 1)) as tp:
                    for i in range(2):
                        t = 2 * tp + i
                        if q > 0:
                            norm(t - TPC, i)
                        cut_h_lo(t + 1, 1 - i)
                        add_x(t, i)
                        if q > 0:
                            cut_xn2_lo(t - TPC, i, P * (t - q * TPC))
                if q == C - 1:
                    cut_h_lo(T - 1, 1)
                    for i in range(2):
                        norm(T - 2 + i - TPC, i)
                        add_x(T - 2 + i, i)
                        cut_xn2_lo(T - 2 + i - TPC, i, P * (TPC - 2 + i))

            def moments(q):
                dve.wait_ge(stats2_ready, (q + 1) * TPC)
                for t in range(q * TPC, (q + 1) * TPC):
                    nc.vector.bn_aggr(mean_var2[:, t, :], stats2[:, t, :]).then_inc(mean_var2_ready, 1)
                dve.wait_ge(mean_var2_ready, (q + 1) * TPC)
                ts = slice(q * TPC, (q + 1) * TPC)
                nc.vector.tensor_scalar(mean_var2[:, ts, 1], mean_var2[:, ts, 1], EPS, None, ALU.add).then_inc(var2_ready, 1)
                dve.wait_ge(std2_ready, q + 1)
                nc.vector.reciprocal(rstd2[:, ts], std2[:, ts]).then_inc(rstd2_ready, 1)
                dve.wait_ge(rstd2_ready, q + 1)

            ent_steps = [0]

            def step(instruction):
                ent_steps[0] += 1
                instruction.then_inc(ent_step, 1)
                dve.wait_ge(ent_step, ent_steps[0])

            def over_e(a):
                return a.unsqueeze(2).to_broadcast([P, a.shape[1], E])

            def over_t(a, part):
                return a.unsqueeze(1).to_broadcast([P, len(ENT_TILES[part]), E])

            def views(part):
                e = {n: v[:] for n, v in ent[part].items()}
                return e, {n: v.rearrange("p t e -> p (t e)") for n, v in e.items()}, col[part]

            def ent_constants():
                dve.wait_ge(k_ready, 1)
                step(nc.vector.tensor_copy(k_row[:], k_int[:]))
                step(nc.vector.memset(keep[:], 1.0))
                step(nc.vector.reciprocal(inv_k[:], k_row[:]))
                step(nc.vector.memset(keep[:, :, 0:1], 0.0))

            def ent_norm(part):
                e, _, col = views(part)
                dve.wait_ge(u_ready, (1, C)[part])
                u = u_sb[:, ENT_TILES[part][0]:ENT_TILES[part][-1] + 1, :]
                step(nc.vector.tensor_reduce(col["sum"], u, AX.X, ALU.add))
                step(nc.vector.tensor_scalar(col["mean"], col["sum"], 1.0 / E, None, ALU.mult))
                step(nc.vector.tensor_tensor(e["z"], u, over_e(col["mean"]), ALU.subtract))
                step(nc.vector.tensor_tensor(e["sq"], e["z"], e["z"], ALU.mult))
                step(nc.vector.tensor_reduce(col["sum"], e["sq"], AX.X, ALU.add))
                nc.vector.tensor_scalar(col["var"], col["sum"], 1.0 / E, EPS, ALU.mult, ALU.add).then_inc(var_ready, 1)

            def ent_sort(part):
                e, _, col = views(part)
                dve.wait_ge(var_std_ready, part + 1)
                step(nc.vector.reciprocal(col["rstd"], col["std"]))
                step(nc.vector.tensor_tensor(e["z"], e["z"], over_e(col["rstd"]), ALU.mult))
                step(nc.vector.tensor_scalar(e["z"], e["z"], 0.5, None, ALU.mult))
                step(nc.vector.tensor_reduce(col["max"], e["z"], AX.X, ALU.max))
                step(nc.vector.tensor_tensor(e["z"], e["z"], over_e(col["max"]), ALU.subtract))
                for t in range(len(ENT_TILES[part])):
                    i = nc.vector.max(e["sorted"][:, t, 0:8], e["z"][:, t, :])
                step(i)
                for t in range(len(ENT_TILES[part])):
                    i = nc.vector.match_replace(e["rest"][:, t, :], e["sorted"][:, t, 0:8], e["z"][:, t, :], -1e30)
                step(i)
                for t in range(len(ENT_TILES[part])):
                    i = nc.vector.max(e["sorted"][:, t, 8:16], e["rest"][:, t, :])
                step(i)

            def ent_delta(part):
                e, flat, col = views(part)
                step(nc.vector.tensor_tensor(e["sorted2"], e["sorted"], e["sorted"], ALU.mult))
                kf = keep[:, 0:len(ENT_TILES[part])].rearrange("p t e -> p (t e)")
                step(nc.vector.tensor_tensor_scan(flat["cum"], kf, flat["sorted"], 0.0, ALU.mult, ALU.add))
                step(nc.vector.tensor_tensor_scan(flat["cum2"], kf, flat["sorted2"], 0.0, ALU.mult, ALU.add))
                step(nc.vector.tensor_tensor(e["mean"], e["cum"], over_t(inv_k[:], part), ALU.mult))
                step(nc.vector.tensor_tensor(e["msq"], e["cum2"], over_t(inv_k[:], part), ALU.mult))
                step(nc.vector.tensor_tensor(e["cum"], e["mean"], e["mean"], ALU.mult))
                step(nc.vector.tensor_tensor(e["msq"], e["msq"], e["cum"], ALU.subtract))
                step(nc.vector.tensor_tensor(e["msq"], over_t(inv_k[:], part), e["msq"], ALU.subtract))
                nc.vector.tensor_scalar(e["msq"], e["msq"], 0.0, None, ALU.max).then_inc(delta_ready, 1)

            def ent_values(part):
                e, _, col = views(part)
                dve.wait_ge(root_ready, part + 1)
                step(nc.vector.tensor_tensor(e["tau"], e["mean"], e["root"], ALU.subtract))
                step(nc.vector.tensor_tensor(e["sq"], e["tau"], e["sorted"], ALU.is_le))
                step(nc.vector.tensor_reduce(col["support"], e["sq"], AX.X, ALU.add))
                step(nc.vector.tensor_tensor(e["pick"], over_t(k_row[:], part), over_e(col["support"]), ALU.is_equal))
                step(nc.vector.tensor_tensor(e["pick"], e["pick"], e["tau"], ALU.mult))
                step(nc.vector.tensor_reduce(col["tau"], e["pick"], AX.X, ALU.add))
                step(nc.vector.tensor_tensor(e["z"], e["z"], over_e(col["tau"]), ALU.subtract))
                step(nc.vector.tensor_scalar(e["z"], e["z"], 0.0, None, ALU.max))
                step(nc.vector.tensor_tensor(e["a"], e["z"], e["z"], ALU.mult))
                a = a_all[:, ENT_TILES[part][0]:ENT_TILES[part][-1] + 1, :]
                step(nc.vector.tensor_copy(a[:, :, 0:E], e["a"]))
                step(nc.vector.tensor_copy(a[:, :, 2 * E:3 * E], e["a"]))
                nc.vector.tensor_tensor(a[:, :, E:2 * E], e["a"], a[:, :, 0:E].bitcast(F32), ALU.subtract).then_inc(a_ready, 1)

            dve.sem_inc(x_plus_ready, 2)
            dve.sem_inc(x2_ready, 2)
            cut_h_lo(0, 0)
            def evict_u(q):
                dve.wait_ge(u_done, 2 * (q + 1))
                u = psum[7][:, 0:2 * TPC * E].rearrange("p (t s e) -> p t e s", s=2, e=E)
                nc.vector.tensor_reduce(u_sb[:, q * TPC:(q + 1) * TPC, :], u, AX.X, ALU.add)\
                    .then_inc(u_ready, 1)

            for q in range(C):
                project_quarter(q)
                moments(q)
                if q == 0:
                    ent_constants()
                if q == 1:
                    evict_u(0)
                if q == 2:
                    ent_norm(0)
                    evict_u(1)
                    ent_sort(0)
                    ent_delta(0)
                    ent_values(0)
            last = (C - 1) * TPC
            norm(last, 0)
            norm(last + 1, 1)
            evict_u(C - 2)
            for t in range(TPC):
                cut_xn2_lo(last + t, t % 2, t * P)
                if t + 2 < TPC:
                    norm(last + t + 2, t % 2)

            def start_z1(c, k):
                dve.wait_ge(gate1_done, KR * c + k + 1)
                nc.vector.scalar_tensor_tensor(out=z_tmp[:, k, :], in0=z1_pre[:, bass.ds(c, 1), k, :].rearrange("p a n -> p (a n)"),
                                               scalar=bias1[:, k:k + 1], in1=psum[0][:, :],
                                               op0=ALU.add, op1=ALU.mult).then_inc(z1_tmp_ready, 1)

            def split_z1(c):
                hi, lo = z1_parts(c)
                dve.wait_ge(z1_tmp_ready, KR * (c + 1))
                nc.vector.tensor_copy(hi, z_tmp[:].rearrange("p k n -> p (k n)")).then_inc(z1_hi_ready, 1)
                dve.wait_ge(z1_hi_ready, c + 1)
                nc.vector.tensor_tensor(lo, z_tmp[:].rearrange("p k n -> p (k n)"), hi.bitcast(F32), ALU.subtract).then_inc(z1_ready, 1)

            def start_z2(c):
                dve.wait_ge(gate2_ready, ONE + KR * (c + 1))
                dve.wait_ge(h_used, HR + KO * (c + 1))
                for k in range(KR):
                    nc.vector.scalar_tensor_tensor(out=z_tmp[:, k, :], in0=psum[4 + k][:, :], scalar=bias2[:, k:k + 1],
                                                   in1=gate2[:, k, :], op0=ALU.add, op1=ALU.mult).then_inc(z2_tmp_ready, 1)

            def split_z2(c):
                dve.wait_ge(z2_tmp_ready, ONE + KR * (c + 1))
                dve.wait_ge(o_done, ONE + TPC * c)
                nc.vector.tensor_copy(z2_hi[:], z_tmp[:]).then_inc(z2_hi_ready, 1)
                dve.wait_ge(z2_hi_ready, c + 1)
                nc.vector.tensor_tensor(z2_lo[:], z_tmp[:], z2_hi[:].bitcast(F32), ALU.subtract).then_inc(z2_ready, 1)

            def rows_out(c, t):
                n = TPC * c + t
                dve.wait_ge(o_done, ONE + n + 1)
                dve.wait_ge(out_saved[t % 2], 16 + 16 * ((TPC // 2) * c + t // 2))
                nc.vector.tensor_tensor(out_rows[:, t % 2, :], psum[6 + t % 2][:, :],
                                        x2[:, bass.ds(n, 1), :].rearrange("p a s -> p (a s)"), ALU.add).then_inc(o_ready, 1)

            def split_h(c, o):
                n = KO * c + o
                dve.wait_ge(h_full_ready, ONE + n + 1)
                dve.wait_ge(h_used, n + 1)
                nc.vector.tensor_copy(hr_hi[o % HR][:], h_full[o % 2][:]).then_inc(h_hi_cut, 1)
                dve.wait_ge(h_hi_cut, n + 1)
                nc.vector.tensor_tensor(hr_lo[o % HR][:], h_full[o % 2][:], hr_hi[o % HR][:].bitcast(F32), ALU.subtract)\
                    .then_inc(h_split, 1)

            def chunk(c, first, is_last):
                if not first:
                    dve.wait_ge(z1_ready, c + 1)
                    start_z2(c - 1)
                for o in range(KO):
                    split_h(c, o)
                    if o == 0 and not first:
                        split_z2(c - 1)
                    if o in FINAL_AT and not first:
                        rows_out(c - 1, FINAL_AT[o])
                    if first and o in ENT_AT:
                        (ent_sort, ent_delta, ent_values)[ENT_AT.index(o)](1)
                    if o in GATE1_AT and not is_last:
                        k = GATE1_AT[o]
                        if k == 0:
                            dve.wait_ge(z1_ready, c + 1)
                            if not first:
                                dve.wait_ge(z2_ready, c)
                        start_z1(c + 1, k)
                        if k == KR - 1:
                            split_z1(c + 1)

            dve.sem_inc(h_split, 2)
            dve.sem_inc(z2_tmp_ready, ONE)
            dve.sem_inc(o_ready, ONE)
            for k in range(KR):
                start_z1(0, k)
            evict_u(C - 1)
            ent_norm(1)
            dve.wait_ge(z1_pre_done, KR * C)
            split_z1(0)
            chunk(0, True, False)
            dve.wait_ge(w_lo_ready, len(pieces))
            with dve.Fori(1, C - 1) as c:
                chunk(c, False, False)
            chunk(C - 1, False, True)
            start_z2(C - 1)
            split_z2(C - 1)
            for t in range(TPC):
                rows_out(C - 1, t)

        @block.tensor
        def _(pe):
            mm = nc.tensor.matmul
            HI_LO = ((0, 0), (1, 0), (0, 1))

            def turn_xn(t, i):
                pe.wait_ge(xn_ready, t + 1)
                pe.wait_ge(xn_lo_ready, t + 1)
                for k in range(KD):
                    m = nc.tensor.transpose(psum[i][:, k * P:(k + 1) * P], xn[i][:, k * P:(k + 1) * P], ident[:])
                m.then_inc(xn_turned, 1)

            def project(t, i):
                pe.wait_ge(xn_lo_ready, 2 + t + 1)
                pe.wait_ge(seq_ready, t + 1)
                pe.wait_ge(s12_ready, t + 1)
                left, right = (xn_hi[i], xn_lo[i]), (w_seq_hi, w_seq_lo)
                for k in range(KD):
                    for l, r in HI_LO:
                        mm(psum[2 + i][:, :], left[l][:, k, :], right[r][:, k, :], start=(k == 0 and l == r),
                           stop=(k == KD - 1 and r == 1))
                pe.wait_ge(wa_hl_ready, 1)
                for k in range(KD):
                    for part in range(2):
                        m = mm(psum[4 + i][:, 0:4 * H], left[part][:, k, :], wa_hl[:, k].rearrange("p s h -> p (s h)"),
                               start=(k == 0 and part == 0), stop=(k == KD - 1 and part == 1))
                m.then_inc(proj_done, 1)

            def turn_s1(q):
                pe.wait_ge(s12_ready, 2 + (q + 1) * TPC)
                if q >= 2:
                    pe.wait_ge(s1_t_ready, q - 1)
                for t in range(TPC):
                    m = nc.tensor.transpose(psum[6 + q % 2][0:H, t * P:(t + 1) * P], s12[:, q * TPC + t, 0:H], ident[:])
                m.then_inc(s1_turned, 1)

            pe.sem_inc(proj_done, 2)
            pe.wait_ge(ident_ready, 2)
            turn_xn(0, 0)
            pe.wait_ge(w_seq_lo_ready, 1)
            for q in range(C):
                with pe.Fori(q * TPC // 2, (q + 1) * TPC // 2 - (q == C - 1)) as tp:
                    for i in range(2):
                        turn_xn(2 * tp + i + 1, 1 - i)
                        project(2 * tp + i, i)
                if q > 0:
                    turn_s1(q - 1)
            turn_xn(T - 1, 1)
            for i in range(2):
                project(T - 2 + i, i)
            turn_s1(C - 1)

            def group(h, i, g):
                js = range(g * GROUP, (g + 1) * GROUP)
                if g == 0:
                    pe.wait_ge(vals_ready, h + 1)
                pe.wait_ge(neg_cut, SIGNS + T * h + js[-1] + 1)
                if up_to(pos_dve_tiles, js[-1]):
                    pe.wait_ge(pos_dve, N_PDVE * h + up_to(pos_dve_tiles, js[-1]))
                if up_to(POS_ON_POOL, js[-1]):
                    pe.wait_ge(pos_pool, N_POOL * h + up_to(POS_ON_POOL, js[-1]))
                for b in range(BANKS):
                    if g == 0:
                        pe.wait_ge(bank_free, BANKS * h + b + 1)
                    if g == 0 or b == 0:
                        pe.sem_inc(pe_passed_waits)
                    for j in js:
                        for q in range(Q_PER_BANK):
                            for s in range(2):
                                at = (q * 2 + s) * SIDE
                                n = b * Q_PER_BANK + q
                                m = mm(psum[b][:, at:at + SIDE], masks[j % RING][:, s, n * P:(n + 1) * P].bitcast(F8),
                                       vals[i][:, j, s].rearrange("p a d -> p (a d)"),
                                       start=(j == 0 and q == 0 and s == 0), stop=(j == T - 1), skip_group_check=True)
                    m.then_inc(bank_passed, 1)

            pe.sem_inc(bank_passed, GROUPS_FREE * BANKS)
            pe.wait_ge(seq_ready, 2 + T)
            with pe.Fori(0, H // 2) as hp:
                for i in range(2):
                    for g in range(NG):
                        group(2 * hp + i, i, g)

            def turn_h(t, i, saved):
                pe.wait_ge(hq_in[i], saved)
                pe.wait_ge(h_lo_ready, t + 1)
                for k in range(KD):
                    m = nc.tensor.transpose(psum[i][:, k * P:(k + 1) * P], hq[i][:, k * P:(k + 1) * P], ident[:])
                m.then_inc(h_turned, 1)

            def out_project(t, i):
                pe.wait_ge(h_lo_ready, 2 + t + 1)
                pe.wait_ge(x_plus_ready, t + 1)
                left, right = (h_hi[i], h_lo[i]), (w_out_hi, w_out_lo)
                for k in range(KD):
                    for l, r in HI_LO:
                        mm(psum[2 + i][:, :], left[l][:, k, :], right[r][:, k, :], start=(k == 0 and l == r), stop=False)
                mm(psum[2 + i][:, :], ones[:], b_hi[:], start=False, stop=False)
                mm(psum[2 + i][:, :], ones[:], b_lo[:], start=False, stop=True).then_inc(y_done, 1)

            def turn_xn2(n, i):
                pe.wait_ge(xn2_ready, n + 1)
                pe.wait_ge(xn2_lo_ready, n + 1)
                for k in range(KD):
                    m = nc.tensor.transpose(psum[4 + i][:, k * P:(k + 1) * P], xn2[i][:, k * P:(k + 1) * P], ident[:])
                m.then_inc(xn2_turned, 1)

            def project_quarter(q):
                with pe.Fori(q * TPC // 2, (q + 1) * TPC // 2 - (q == C - 1)) as tp:
                    for i in range(2):
                        t = 2 * tp + i
                        turn_h(t + 1, 1 - i, 16 * (tp + i) + 16)
                        out_project(t, i)
                        if q > 0:
                            turn_xn2(t - TPC, i)
                if q == C - 1:
                    turn_h(T - 1, 1, 16 * (T // 2))
                    for i in range(2):
                        out_project(T - 2 + i, i)
                        turn_xn2(T - 2 + i - TPC, i)

            def z1_pre_part(q, r):
                left, right = (win1_hi, win1_lo), (xn2_hi, xn2_lo)
                if KR * q + r > 0:
                    pe.wait_ge(z1_pre_ready, KR * q + r)
                for k in range(KD):
                    for l, s in HI_LO:
                        rhs = (xn2_hi, xn2_lo)[s][:, k, :]
                        m = mm(psum[6][:, :], left[l][:, k, r * P:(r + 1) * P], rhs, start=(k == 0 and l == s),
                               stop=(k == KD - 1 and s == 1))
                m.then_inc(z1_pre_done, 1)

            def scores(q, tiles):
                for t in tiles:
                    pe.wait_ge(xn2_lo_ready, 2 + q * TPC + t + 1)
                    column = slice(t * P, (t + 1) * P)
                    for k in range(KD):
                        for part, left in enumerate((xn2_hi, xn2_lo)):
                            m = mm(psum[7][:, 2 * t * E:2 * (t + 1) * E], left[:, k, column],
                                   proj_hl[:, k].rearrange("p s e -> p (s e)"), start=(k == 0 and part == 0),
                                   stop=(k == KD - 1 and part == 1))
                m.then_inc(u_done, 1)

            def turn_a(c):
                pe.wait_ge(a_col_ready, c + 1)
                pe.sem_inc(pe_passed_waits)
                for t in range(TPC):
                    m = nc.tensor.transpose(psum[0][0:3 * E, t * P:(t + 1) * P], a_col[:, t, :], ident[:])
                m.then_inc(a_turned, 1)

            def gate(which, r, done):
                mm(psum[0][:, :], c_hl[:, which, r * P:(r + 1) * P], a_t[:], start=True, stop=True).then_inc(done, 1)

            def gate1(c, r):
                if r == 0:
                    pe.wait_ge(a_t_ready, c + 1)
                else:
                    pe.wait_ge(z1_tmp_ready, KR * c + r)
                gate(0, r, gate1_done)

            def first_factor(q):
                pe.wait_ge(w_lo_ready, WIN1_PIECES)
                if q == 0:
                    pe.wait_ge(small_ready, 4)
                else:
                    pe.wait_ge(u_ready, q)
                scores(q, range(TPC - 1))
                if q == C - 1:
                    gate1(0, 0)
                pe.wait_ge(xn2_lo_ready, 2 + (q + 1) * TPC)
                z1_pre_part(q, 0)
                if q == C - 1:
                    gate1(0, 1)
                scores(q, [TPC - 1])
                z1_pre_part(q, 1)

            pe.sem_inc(h_lo_ready, 2)
            pe.sem_inc(y_done, 2)
            pe.sem_inc(xn2_turned, 2)
            pe.sem_inc(xn2_lo_ready, 2)
            pe.wait_ge(bank_free, BANKS * (H + 1))
            turn_h(0, 0, 16)
            pe.wait_ge(w_lo_ready, W_OUT_PIECES)
            pe.wait_ge(ones_ready, 1)
            for q in range(C):
                project_quarter(q)
                if q > 0:
                    first_factor(q - 1)
            for t in range(TPC):
                turn_xn2((C - 1) * TPC + t, t % 2)
                if t == 1:
                    turn_a(0)
            first_factor(C - 1)

            def final(c, t):
                pe.wait_ge(z2_ready, c + 1)
                pe.wait_ge(o_ready, ONE + TPC * c + max(t - 1, 0))
                left, right = (z2_hi, z2_lo), (wout2_hi, wout2_lo)
                for k in range(KR):
                    for l, s in HI_LO:
                        m = mm(psum[6 + t % 2][:, :], left[l][:, k, t * P:(t + 1) * P], right[s][:, k, :],
                               start=(k == 0 and l == s), stop=(k == KR - 1 and s == 1))
                m.then_inc(o_done, 1)

            def chunk(c, first, is_last):
                z1 = [part.rearrange("p (k n) -> p k n", k=KR) for part in z1_parts(c)]

                def up(o):
                    if o == 0:
                        pe.wait_ge(z1_ready, c + 1)
                    pe.wait_ge(h_full_ready, ONE + KO * c + max(o - 2, 0))
                    if first and o % (PIECE // P) == 0:
                        pe.wait_ge(w_lo_ready, WIN1_PIECES + KR * (o // (PIECE // P) + 1))
                    pe.sem_inc(pe_passed_waits)
                    left = (wout1_hi, wout1_lo)
                    for k in range(KR):
                        for l, s in HI_LO:
                            m = mm(psum[1 + o % 3][:, :], left[l][:, k, o * P:(o + 1) * P], z1[s][:, k, :],
                                   start=(k == 0 and l == s), stop=(k == KR - 1 and s == 1))
                    m.then_inc(h_done, 1)

                def down(o):
                    pe.wait_ge(h_split, 2 + KO * c + o + 1)
                    if o == 0:
                        pe.wait_ge(z2_tmp_ready, ONE + KR * c)
                    if first and o % (PIECE // R) == 0:
                        pe.wait_ge(w_lo_ready, WOUT1_PIECES + o // (PIECE // R) + 1)
                    left, right = (win2_hi, win2_lo), (hr_hi[o % HR], hr_lo[o % HR])
                    for r in range(KR):
                        for l, s in HI_LO:
                            m = mm(psum[4 + r][:, :], left[l][:, o, r * P:(r + 1) * P], right[s][:],
                                   start=(o == 0 and l == s), stop=(o == KO - 1 and s == 1))
                    m.then_inc(h_used, 1)

                up(0)
                up(1)
                for o in range(2, KO):
                    up(o)
                    down(o - 2)
                    if o in FINAL_AT and not first:
                        final(c - 1, FINAL_AT[o])
                    if o in GATE2_AT:
                        k = GATE2_AT[o]
                        if k == 0:
                            pe.wait_ge(z1_tmp_ready, KR * (c + 1))
                        else:
                            pe.wait_ge(gate2_ready, ONE + KR * c + k)
                        gate(1, k, gate2_done)
                    if o == TURN_A_AT and not is_last:
                        pe.wait_ge(gate2_ready, ONE + KR * (c + 1))
                        turn_a(c + 1)
                    if o in GATE1_AT and not is_last:
                        gate1(c + 1, GATE1_AT[o])
                down(KO - 2)
                down(KO - 1)

            pe.sem_inc(h_used, HR)
            pe.sem_inc(o_done, ONE)
            chunk(0, True, False)
            pe.wait_ge(w_lo_ready, len(pieces))
            with pe.Fori(1, C - 1) as c:
                chunk(c, False, False)
            chunk(C - 1, False, True)
            for t in range(TPC):
                final(C - 1, t)


_INS = ['x', 'adj', 'L0_gnn_W_seq', 'L0_gnn_a1', 'L0_gnn_a2', 'L0_gnn_W_out', 'L0_gnn_b_out', 'L0_ffn_proj', 'L0_ffn_C1',
        'L0_ffn_Win1', 'L0_ffn_Wout1', 'L0_ffn_C2', 'L0_ffn_Win2', 'L0_ffn_Wout2']
_TRANSPOSED = ('adj', 'L0_ffn_Wout1', 'L0_ffn_Wout2')


def kernel(**inputs):
    import numpy as _np
    import concourse.bacc as _bacc
    from concourse import mybir as _mybir
    from concourse.bass_utils import run_bass_kernel_spmd as _run

    nc = _bacc.Bacc("TRN2", target_bir_lowering=False, num_devices=1)
    arrays, args = {}, []
    for name in _INS:
        a = _np.asarray(inputs[name])
        a = _np.ascontiguousarray(a.T if name in _TRANSPOSED else a)
        arrays[f"in_{name}_dram"] = a
        args.append(nc.dram_tensor(f"in_{name}_dram", a.shape, _mybir.dt.from_np(a.dtype), kind="ExternalInput").ap())
    n, d = inputs['x'].shape
    args.append(nc.dram_tensor("out_0_dram", (n, d), _mybir.dt.float32, kind="ExternalOutput").ap())
    gat_ffn(nc, *args)
    r = _run(nc, [arrays], core_ids=[0])
    return r.results[0]["out_0_dram"]
```
